# Optimizing a Trainium2 kernel written in Bass

```python
import numpy as np
import jax
import jax.numpy as jnp

def _softmax(x, axis=-1):
    return jax.nn.softmax(x, axis=axis)

def _gelu(x):
    return jax.nn.gelu(x, approximate=True)

def _silu(x):
    return jax.nn.silu(x)

def _sigmoid(x):
    return jax.nn.sigmoid(x)

def _layernorm(x, axis=-1, eps=1e-05):
    m = jnp.mean(x, axis=axis, keepdims=True)
    v = jnp.var(x, axis=axis, keepdims=True)
    return (x - m) / jnp.sqrt(v + eps)

def _scatter_add(tgt, idx, src, axis=0):
    return tgt.at[idx].add(src)

def _segment_sum(src, seg, n):
    return jax.ops.segment_sum(src, seg, n)
kernel_name = 'mk_sandwich_d2_jaxref_r8_f75e14'

def setup_inputs(seed: int=0):
    np.random.seed(seed)
    _w = jnp.asarray

    def _L0_attn_setup():
        import jax, jax.numpy as jnp
        import numpy as np
        B, S, D = (2, 512, 256)
        H, DK, DV = (16, 128, 128)
        SEG = 64
        UPDATE = 'delta'
        CAUSAL = True
        key = jax.random.key(seed)
        ks = jax.random.split(key, 6)
        s = 0.02
        return {'x': jax.random.normal(ks[0], (B, S, D), jnp.float32), 'Wq': jax.random.normal(ks[1], (D, H * DK), jnp.float32) * s, 'Wk': jax.random.normal(ks[2], (D, H * DK), jnp.float32) * s, 'Wv': jax.random.normal(ks[3], (D, H * DV), jnp.float32) * s, 'Wo': jax.random.normal(ks[4], (H * DV, D), jnp.float32) * s, 'betas': jax.random.normal(ks[5], (1, H, 1, DV), jnp.float32)}
    _L0_attn_in = _L0_attn_setup()

    def _L0_ffn_setup():
        import jax, jax.numpy as jnp
        import numpy as np
        DIM_IN = 256
        DIM_HIDDEN = 1024
        key = jax.random.key(seed)
        k_x, k_g, k_u, k_d = jax.random.split(key, 4)
        s_in = 1.0 / np.sqrt(DIM_IN)
        s_hid = 1.0 / np.sqrt(DIM_HIDDEN)
        x = jax.random.normal(k_x, (4, 256, DIM_IN), dtype=jnp.float32)
        w_gate = jax.random.uniform(k_g, (DIM_HIDDEN, DIM_IN), jnp.float32, -s_in, s_in)
        w_up = jax.random.uniform(k_u, (DIM_HIDDEN, DIM_IN), jnp.float32, -s_in, s_in)
        w_down = jax.random.uniform(k_d, (DIM_IN, DIM_HIDDEN), jnp.float32, -s_hid, s_hid)
        return {'x': x, 'w_gate': w_gate, 'w_up': w_up, 'w_down': w_down}
    _L0_ffn_in = _L0_ffn_setup()

    def _L1_attn_setup():
        import jax, jax.numpy as jnp
        import numpy as np
        import math
        D_MODEL = 256
        NUM_HEADS = 16
        HEAD_DIM = D_MODEL // NUM_HEADS
        key = jax.random.key(seed)
        k_x, k_wqkv, k_bqkv, k_wo, k_bo = jax.random.split(key, 5)
        B, S = (2, 256)
        scale = 1.0 / math.sqrt(D_MODEL)
        return {'x': jax.random.normal(k_x, (B, S, D_MODEL), dtype=jnp.float32), 'w_qkv': jax.random.normal(k_wqkv, (3 * D_MODEL, D_MODEL), dtype=jnp.float32) * scale, 'b_qkv': jax.random.normal(k_bqkv, (3 * D_MODEL,), dtype=jnp.float32) * 0.01, 'w_out': jax.random.normal(k_wo, (D_MODEL, D_MODEL), dtype=jnp.float32) * scale, 'b_out': jax.random.normal(k_bo, (D_MODEL,), dtype=jnp.float32) * 0.01}
    _L1_attn_in = _L1_attn_setup()

    def _L1_ffn_setup():
        import jax, jax.numpy as jnp
        import numpy as np
        ZERO_POINT = 128.0

        def _dequant(wq, scale):
            return (wq.astype(jnp.float32) - ZERO_POINT) * scale[:, None]
        key = jax.random.key(seed)
        ks = jax.random.split(key, 7)
        H, I = (256, 1024)
        B, S = (2, 256)
        hidden_state = jax.random.normal(ks[0], (B, S, H), dtype=jnp.float32)
        gate_w = jax.random.randint(ks[1], (I, H), 0, 32, dtype=jnp.int32)
        up_w = jax.random.randint(ks[2], (I, H), 0, 32, dtype=jnp.int32)
        down_w = jax.random.randint(ks[3], (H, I), 0, 32, dtype=jnp.int32)
        gate_scale = jax.random.uniform(ks[4], (I,), dtype=jnp.float32) * 0.02
        up_scale = jax.random.uniform(ks[5], (I,), dtype=jnp.float32) * 0.02
        down_scale = jax.random.uniform(ks[6], (H,), dtype=jnp.float32) * 0.02
        return {'hidden_state': hidden_state, 'gate_w': gate_w, 'gate_scale': gate_scale, 'up_w': up_w, 'up_scale': up_scale, 'down_w': down_w, 'down_scale': down_scale}
    _L1_ffn_in = _L1_ffn_setup()
    _d = {'L0_attn_x': _L0_attn_in['x'], 'L0_attn_Wq': _L0_attn_in['Wq'], 'L0_attn_Wk': _L0_attn_in['Wk'], 'L0_attn_Wv': _L0_attn_in['Wv'], 'L0_attn_Wo': _L0_attn_in['Wo'], 'L0_attn_betas': _L0_attn_in['betas'], 'L0_ffn_w_gate': _L0_ffn_in['w_gate'], 'L0_ffn_w_up': _L0_ffn_in['w_up'], 'L0_ffn_w_down': _L0_ffn_in['w_down'], 'L1_attn_w_qkv': _L1_attn_in['w_qkv'], 'L1_attn_b_qkv': _L1_attn_in['b_qkv'], 'L1_attn_w_out': _L1_attn_in['w_out'], 'L1_attn_b_out': _L1_attn_in['b_out'], 'L1_ffn_gate_w': _L1_ffn_in['gate_w'], 'L1_ffn_gate_scale': _L1_ffn_in['gate_scale'], 'L1_ffn_up_w': _L1_ffn_in['up_w'], 'L1_ffn_up_scale': _L1_ffn_in['up_scale'], 'L1_ffn_down_w': _L1_ffn_in['down_w'], 'L1_ffn_down_scale': _L1_ffn_in['down_scale']}
    _x0 = _d['L0_attn_x']
    _d['L0_attn_x'] = jax.random.normal(jax.random.fold_in(jax.random.key(seed), 1), (1, 2048, 256), dtype=_x0.dtype)
    del _x0
    return _d

def reference(L0_attn_x, L0_attn_Wq, L0_attn_Wk, L0_attn_Wv, L0_attn_Wo, L0_attn_betas, L0_ffn_w_gate, L0_ffn_w_up, L0_ffn_w_down, L1_attn_w_qkv, L1_attn_b_qkv, L1_attn_w_out, L1_attn_b_out, L1_ffn_gate_w, L1_ffn_gate_scale, L1_ffn_up_w, L1_ffn_up_scale, L1_ffn_down_w, L1_ffn_down_scale):

    def _L0_attn_ref(x, Wq, Wk, Wv, Wo, betas):
        import jax, jax.numpy as jnp
        import numpy as np
        B, S, D = (2, 512, 256)
        H, DK, DV = (16, 128, 128)
        SEG = 64
        UPDATE = 'delta'
        CAUSAL = True
        Bsz, seq, _ = x.shape
        nseg = seq // SEG
        q = (x @ Wq).reshape(Bsz, seq, H, DK).transpose(0, 2, 1, 3)
        k = (x @ Wk).reshape(Bsz, seq, H, DK).transpose(0, 2, 1, 3)
        v = (x @ Wv).reshape(Bsz, seq, H, DV).transpose(0, 2, 1, 3)
        qs = q.reshape(Bsz, H, nseg, SEG, DK).transpose(2, 0, 1, 3, 4)
        ks_ = k.reshape(Bsz, H, nseg, SEG, DK).transpose(2, 0, 1, 3, 4)
        vs = v.reshape(Bsz, H, nseg, SEG, DV).transpose(2, 0, 1, 3, 4)
        causal_mask = jnp.tril(jnp.ones((SEG, SEG), bool))
        scale = DK ** 0.5
        beta = jax.nn.sigmoid(betas)

        def step(carry, seg):
            mem, z = carry
            qq, kk, vv = seg
            sigma_q = jax.nn.elu(qq) + 1.0
            scores = jnp.einsum('bhsk,bhtk->bhst', qq, kk) / scale
            if CAUSAL:
                scores = jnp.where(causal_mask, scores, -jnp.inf)
            att_dot = jax.nn.softmax(scores, axis=-1) @ vv
            att_mem = sigma_q @ mem / (sigma_q @ z)
            sigma_k = jax.nn.elu(kk) + 1.0
            if UPDATE == 'linear':
                mem_new = mem + jnp.einsum('bhsk,bhsv->bhkv', sigma_k, vv)
            else:
                delta = vv - sigma_k @ mem / (sigma_k @ z)
                mem_new = mem + jnp.einsum('bhsk,bhsv->bhkv', sigma_k, delta)
            z_new = z + sigma_k.sum(axis=-2, keepdims=True).transpose(0, 1, 3, 2)
            att = beta * att_mem + (1.0 - beta) * att_dot
            out = att.reshape(Bsz, SEG, H * DV) @ Wo
            return ((mem_new, z_new), out)
        mem0 = jnp.zeros((Bsz, H, DK, DV), x.dtype)
        z0 = jnp.ones((Bsz, H, DK, 1), x.dtype) / DK
        _, outs = jax.lax.scan(step, (mem0, z0), (qs, ks_, vs))
        return outs.transpose(1, 0, 2, 3).reshape(Bsz, seq, D)

    def _L0_ffn_ref(x, w_gate, w_up, w_down):
        import jax, jax.numpy as jnp
        import numpy as np
        DIM_IN = 256
        DIM_HIDDEN = 1024
        gate = jnp.einsum('bsd,hd->bsh', x, w_gate)
        up = jnp.einsum('bsd,hd->bsh', x, w_up)
        gated = jax.nn.silu(gate) * up
        return jnp.einsum('bsh,dh->bsd', gated, w_down)

    def _L1_attn_ref(x, w_qkv, b_qkv, w_out, b_out):
        import jax, jax.numpy as jnp
        import numpy as np
        import math
        D_MODEL = 256
        NUM_HEADS = 16
        HEAD_DIM = D_MODEL // NUM_HEADS
        B, S, D = x.shape
        H, Hd = (NUM_HEADS, HEAD_DIM)
        qkv = jnp.einsum('bsd,ed->bse', x, w_qkv) + b_qkv
        qkv = qkv.reshape(B, S, 3, H, Hd)
        q = jnp.transpose(qkv[:, :, 0], (0, 2, 1, 3))
        k = jnp.transpose(qkv[:, :, 1], (0, 2, 1, 3))
        v = jnp.transpose(qkv[:, :, 2], (0, 2, 1, 3))
        scores = jnp.einsum('bhqd,bhkd->bhqk', q, k) / math.sqrt(Hd)
        causal = jnp.triu(jnp.full((S, S), -jnp.inf, dtype=scores.dtype), k=1)
        scores = scores + causal[None, None]
        attn = jax.nn.softmax(scores, axis=-1)
        out = jnp.einsum('bhqk,bhkd->bhqd', attn, v)
        out = jnp.transpose(out, (0, 2, 1, 3)).reshape(B, S, D)
        return jnp.einsum('bsd,ed->bse', out, w_out) + b_out

    def _L1_ffn_ref(hidden_state, gate_w, gate_scale, up_w, up_scale, down_w, down_scale):
        import jax, jax.numpy as jnp
        import numpy as np
        ZERO_POINT = 128.0

        def _dequant(wq, scale):
            return (wq.astype(jnp.float32) - ZERO_POINT) * scale[:, None]
        Wg = _dequant(gate_w, gate_scale)
        Wu = _dequant(up_w, up_scale)
        Wd = _dequant(down_w, down_scale)
        g = jnp.einsum('bsh,ih->bsi', hidden_state, Wg)
        u = jnp.einsum('bsh,ih->bsi', hidden_state, Wu)
        h = jax.nn.silu(g) * u
        return jnp.einsum('bsi,hi->bsh', h, Wd)
    x = L0_attn_x
    x = x + _layernorm(_L0_attn_ref(_layernorm(x, axis=-1), L0_attn_Wq, L0_attn_Wk, L0_attn_Wv, L0_attn_Wo, L0_attn_betas), axis=-1)
    x = x + _layernorm(_L0_ffn_ref(_layernorm(x, axis=-1), L0_ffn_w_gate, L0_ffn_w_up, L0_ffn_w_down), axis=-1)
    x = x + _layernorm(_L1_attn_ref(_layernorm(x, axis=-1), L1_attn_w_qkv, L1_attn_b_qkv, L1_attn_w_out, L1_attn_b_out), axis=-1)
    x = x + _layernorm(_L1_ffn_ref(_layernorm(x, axis=-1), L1_ffn_gate_w, L1_ffn_gate_scale, L1_ffn_up_w, L1_ffn_up_scale, L1_ffn_down_w, L1_ffn_down_scale), axis=-1)
    return x

_drawn_inputs = setup_inputs


def setup_inputs(seed=0):
    import zlib

    import numpy as np

    out = dict(_drawn_inputs(seed))
    spreads = {}
    factors = {}
    for name, (base, spread) in spreads.items():
        noise = np.random.default_rng([zlib.crc32(name.encode()), seed]).standard_normal(out[name].shape)
        drawn = base * np.exp(spread * noise) if base else spread * noise
        out[name] = jnp.asarray(drawn.astype(out[name].dtype))
    for name, factor in factors.items():
        out[name] = (out[name] * factor).astype(out[name].dtype)
    return out
```

```python
from contextlib import ExitStack

import concourse.bass as bass
from concourse import mybir

F32 = mybir.dt.float32
F32R = mybir.dt.float32r
BF16 = mybir.dt.bfloat16
I32 = mybir.dt.int32
ALU = mybir.AluOpType
ACT = mybir.ActivationFunctionType
AX_X = mybir.AxisListType.X

P = 128
D = 256
KD = D // P
T = 2048
TILES = T // P
CHUNK = 512
R = CHUNK // P
CHUNKS = T // CHUNK
F = 1024
FB = F // P
EPS = 1e-5


def reach(eng, sem, value):
    if isinstance(value, int) and value <= 0:
        return
    eng.wait_ge(sem, value)


def stand_alone(eng, passed):
    eng.sem_inc(passed, 1)


def first_then_loop(eng, count, body):
    body(0)
    with eng.Fori(1, count) as n:
        body(n)


def cols(n, width):
    return bass.ds(n * width, width)


class Mem:
    last_phase = None

    def __init__(self, nc, ctx, phase):
        self.nc, self.ctx, self.phase, self.sems = nc, ctx, phase, []

    def start(self):
        if Mem.last_phase is not None and Mem.last_phase.nc is self.nc:
            self.nc.clear_and_free_semaphores(Mem.last_phase.sems)
        Mem.last_phase = self
        return self.ctx.enter_context(self.nc.Block(no_gpsimd_drain=True))

    def sb(self, name, shape, dt=F32):
        return self.ctx.enter_context(self.nc.sbuf_tensor(f"{self.phase}_{name}", shape, dt))

    def ps(self, name, shape, dt=F32):
        return self.ctx.enter_context(self.nc.psum_tensor(f"{self.phase}_{name}", shape, dt))

    def sem(self, name):
        self.sems.append(self.nc.alloc_semaphore(f"{self.phase}_{name}"))
        return self.sems[-1]


class Stats:

    def __init__(self, m, name):
        self.sums = m.sb(name + "_sums", [P, R, 6])
        self.mean_var = m.sb(name + "_mean_var", [P, R, 2])
        self.var_eps = m.sb(name + "_var_eps", [P, R])
        self.std = m.sb(name + "_std", [P, R])
        self.rstd = m.sb(name + "_rstd", [P, R])
        self.sums_ready = m.sem(name + "_sums_ready")
        self.sums_passed = m.sem(name + "_sums_passed")
        self.mean_ready = m.sem(name + "_mean_ready")
        self.var_ready = m.sem(name + "_var_ready")
        self.std_ready = m.sem(name + "_std_ready")
        self.rstd_ready = m.sem(name + "_rstd_ready")

    def dve_variance(self, dve, tile_of, n):
        for r in range(R):
            last = dve.bn_stats(self.sums[:, r, :], tile_of(r))
        last.then_inc(self.sums_ready, 1)
        dve.wait_ge(self.sums_ready, n + 1)
        stand_alone(dve, self.sums_passed)
        for r in range(R):
            last = dve.bn_aggr(self.mean_var[:, r, :], self.sums[:, r, :])
        last.then_inc(self.mean_ready, 1)
        dve.wait_ge(self.mean_ready, n + 1)
        reach(dve, self.std_ready, n)
        dve.tensor_scalar(self.var_eps[:], self.mean_var[:, :, 1], EPS, None, ALU.add).then_inc(self.var_ready, 1)

    def act_std(self, act, n):
        act.wait_ge(self.var_ready, n + 1)
        reach(act, self.rstd_ready, n)
        act.activation(self.std[:], self.var_eps[:], ACT.Sqrt).then_inc(self.std_ready, 1)

    def dve_rstd(self, dve, n):
        dve.wait_ge(self.std_ready, n + 1)
        dve.reciprocal(self.rstd[:], self.std[:]).then_inc(self.rstd_ready, 1)
        dve.wait_ge(self.rstd_ready, n + 1)

    def dve_normalise(self, dve, out_of, tile_of):
        for r in range(R):
            last = dve.tensor_scalar(out_of(r), tile_of(r), self.mean_var[:, r, 0:1], self.rstd[:, r:r + 1],
                                     ALU.subtract, ALU.mult)
        return last


class Turn:

    def __init__(self, m, core, name="turn"):
        self.core = core
        self.xn = m.sb(name + "_xn", [P, R, D])
        self.turned = m.ps(name + "_turned", [P, KD, CHUNK])
        self.xn_ready = m.sem(name + "_xn_ready")
        self.turned_ready = m.sem(name + "_turned_ready")
        self.hi_ready = m.sem(name + "_hi_ready")
        self.lo_ready = m.sem(name + "_lo_ready")

    def pe_turn(self, pe, n):
        pe.wait_ge(self.xn_ready, n + 1)
        reach(pe, self.lo_ready, KD * n)
        for k in range(KD):
            for r in range(R):
                last = pe.transpose(self.turned[:, k, r * P:(r + 1) * P], self.xn[:, r, k * P:(k + 1) * P],
                                    self.core.ident[:])
            last.then_inc(self.turned_ready, 1)

    def act_hi(self, act, n, c):
        for k in range(KD):
            act.wait_ge(self.turned_ready, KD * n + k + 1)
            act.activation(self.core.xt_hi[:, k, cols(c, CHUNK)], self.turned[:, k, :],
                           ACT.Copy).then_inc(self.hi_ready, 1)

    def dve_lo(self, dve, n, c):
        for k in range(KD):
            dve.wait_ge(self.hi_ready, KD * n + k + 1)
            dve.tensor_tensor(self.core.xt_lo[:, k, cols(c, CHUNK)], self.turned[:, k, :],
                              self.core.xt_hi[:, k, cols(c, CHUNK)].bitcast(F32),
                              ALU.subtract).then_inc(self.lo_ready, 1)


class Core:

    def __init__(self, nc, ctx):
        m = Mem(nc, ctx, "core")
        self.xt_hi = m.sb("xt_hi", [P, KD, T], F32R)
        self.xt_lo = m.sb("xt_lo", [P, KD, T], F32R)
        self.ident = m.sb("ident", [P, P])

    def hold_x(self, nc, ctx):
        self.x = Mem(nc, ctx, "core").sb("x", [P, TILES, D])

    def x_tile(self, c):
        return lambda r: self.x[:, bass.ds(c * R + r, 1), :].rearrange("p a d -> p (a d)")

    def x_chunk(self, c):
        return self.x[:, cols(c, R), :].rearrange("p a d -> p (a d)")


def phase_input(nc, core, x_in):
    with ExitStack() as ctx:
        m = Mem(nc, ctx, "in")
        norm, turn = Stats(m, "norm"), Turn(m, core)
        x = m.sb("x", [P, TILES, D])
        zeroed, ident_ready = m.sem("zeroed"), m.sem("ident_ready")
        x_loaded = [m.sem(f"x_loaded{c}") for c in range(CHUNKS)]
        block = m.start()

        @block.sync
        def _(sp):
            for c in range(CHUNKS):
                sp.dma_start(x[:, c * R:(c + 1) * R, :],
                             x_in[0, c * CHUNK:(c + 1) * CHUNK, :].rearrange("(a p) d -> p a d", p=P)).then_inc(x_loaded[c], 16)

        @block.gpsimd
        def _(pool):
            pool.memset(core.ident[:], 0.0).then_inc(zeroed, 1)
            pool.wait_ge(zeroed, 1)
            pool.affine_select(out=core.ident[:], in_=core.ident[:], compare_op=ALU.not_equal, fill=1.0, base=0,
                               pattern=[[-1, P]], channel_multiplier=1).then_inc(ident_ready, 1)

        @block.vector
        def _(dve):
            def normalise(c):
                x_tile = lambda r: x[:, c * R + r, :]
                dve.wait_ge(x_loaded[c], 16)
                norm.dve_variance(dve, x_tile, c)
                norm.dve_rstd(dve, c)
                reach(dve, turn.turned_ready, KD * c)
                norm.dve_normalise(dve, lambda r: turn.xn[:, r, :], x_tile).then_inc(turn.xn_ready, 1)

            for c in range(CHUNKS):
                normalise(c)
                turn.dve_lo(dve, c, c)

        @block.scalar
        def _(act):
            for c in range(CHUNKS):
                norm.act_std(act, c)
                turn.act_hi(act, c, c)

        @block.tensor
        def _(pe):
            pe.wait_ge(ident_ready, 1)
            for c in range(CHUNKS):
                turn.pe_turn(pe, c)


class TurnWeights:

    def __init__(self, m, core, bank_of):
        self.core, self.bank_of = core, bank_of
        self.turned_ready = m.sem("weights_turned_ready")
        self.hi_ready = m.sem("weights_hi_ready")
        self.lo_ready = m.sem("weights_lo_ready")

    def pe(self, pe, units, source_ready):
        for u, (sources, hi, lo, needs) in enumerate(units):
            source_ready(needs)
            reach(pe, self.lo_ready, u - 1)
            for s, source in enumerate(sources):
                last = pe.transpose(self.bank_of(u)[:, s * P:(s + 1) * P], source, self.core.ident[:])
            last.then_inc(self.turned_ready, 1)

    def act(self, act, units):
        for u, (sources, hi, lo, needs) in enumerate(units):
            act.wait_ge(self.turned_ready, u + 1)
            act.activation(hi, self.bank_of(u)[:, 0:len(sources) * P], ACT.Copy).then_inc(self.hi_ready, 1)

    def dve(self, dve, units):
        for u, (sources, hi, lo, needs) in enumerate(units):
            dve.wait_ge(self.hi_ready, u + 1)
            dve.tensor_tensor(lo, self.bank_of(u)[:, 0:len(sources) * P], hi.bitcast(F32),
                              ALU.subtract).then_inc(self.lo_ready, 1)


def phase_ffn(nc, core, name, w_gate, w_up, w_down, scales=None, out=None):
    ZERO_POINT = 128.0
    with ExitStack() as ctx:
        m = Mem(nc, ctx, name)
        raw_dt = F32 if scales is None else I32
        raw_in = m.sb("raw_in", [P, FB, D], raw_dt)
        raw_in2 = m.sb("raw_in2", [P, FB, D], raw_dt)
        raw_down = m.sb("raw_down", [P, KD, F], raw_dt)
        gate_hi, gate_lo = m.sb("gate_hi", [P, KD, F], F32R), m.sb("gate_lo", [P, KD, F], F32R)
        up_hi, up_lo = m.sb("up_hi", [P, KD, F], F32R), m.sb("up_lo", [P, KD, F], F32R)
        down_hi, down_lo = m.sb("down_hi", [P, FB, D], F32R), m.sb("down_lo", [P, FB, D], F32R)
        silu = m.sb("silu", [P, 2, CHUNK])
        hidden = m.sb("hidden", [P, 2, CHUNK])
        hidden_hi, hidden_lo = m.sb("hidden_hi", [P, 2, CHUNK], F32R), m.sb("hidden_lo", [P, 2, CHUNK], F32R)
        y_normed = m.sb("y_normed", [P, R, D])
        post, pre, turn = Stats(m, "post"), Stats(m, "pre"), Turn(m, core)

        gate_ps = m.ps("gate_ps", [P, 2, CHUNK])
        up_ps = m.ps("up_ps", [P, 2, CHUNK])
        y_ps = m.ps("y_ps", [P, R // 2, 2 * D])

        raw_loaded = [m.sem(f"raw_loaded_{w}") for w in ("gate", "up", "down")]
        scaled = m.sem("weights_scaled")
        scales_loaded = m.sem("scales_loaded")
        gate_up_ready = m.sem("gate_up_ready")
        silu_ready = m.sem("silu_ready")
        hidden_ready = m.sem("hidden_ready")
        hidden_hi_ready = m.sem("hidden_hi_ready")
        hidden_lo_ready = m.sem("hidden_lo_ready")
        down_done = m.sem("down_done")
        y_ready = m.sem("y_ready")
        y_read = m.sem("y_read")
        x_updated = m.sem("x_updated")
        stored = m.sem("stored")
        last_layer = out is not None

        turning = TurnWeights(m, core, lambda u: gate_ps[:, u % 2, :])
        units = []
        if scales is None:
            gate_src, up_src, down_src = raw_in, raw_in2, raw_down
        else:
            gate_src, up_src, down_src = (t[:].bitcast(F32) for t in (raw_in, raw_in2, raw_down))
            scale_sb = m.sb("scale", [P, 2 * FB + KD])
        for w, (src, hi, lo) in enumerate(((gate_src, gate_hi, gate_lo), (up_src, up_hi, up_lo))):
            for k in range(KD):
                for j0 in range(0, FB, 4):
                    units.append(([src[:, j, k * P:(k + 1) * P] for j in range(j0, j0 + 4)],
                                  hi[:, k, j0 * P:(j0 + 4) * P], lo[:, k, j0 * P:(j0 + 4) * P], w))
        for j0 in range(0, FB, 2):
            units.append(([down_src[:, k, j * P:(j + 1) * P] for j in (j0, j0 + 1) for k in range(KD)],
                          down_hi[:, j0:j0 + 2, :].rearrange("p j d -> p (j d)"),
                          down_lo[:, j0:j0 + 2, :].rearrange("p j d -> p (j d)"), 2))
        N_UNITS = len(units)

        block = m.start()

        @block.sync
        def _(sp):
            for src, dst, loaded, rows in ((w_gate, raw_in, 0, FB), (w_up, raw_in2, 1, FB), (w_down, raw_down, 2, KD)):
                sp.dma_start(dst[:], src.rearrange("(j p) n -> p j n", p=P)).then_inc(raw_loaded[loaded], 16)
            if scales is not None:
                with nc.allow_non_contiguous_dma(reason="one scale per partition"):
                    for s, (at, n) in zip(scales, ((0, FB), (FB, FB), (2 * FB, KD))):
                        sp.dma_start(scale_sb[:, at:at + n], s.rearrange("(j p) -> p j", p=P)).then_inc(scales_loaded, 16)
            if last_layer:
                def store(n):
                    sp.wait_ge(x_updated, n + 1)
                    sp.dma_start(out[0, cols(n, CHUNK), :].rearrange("(a p) d -> p a d", p=P),
                                 core.x[:, cols(n, R), :]).then_inc(stored, 16)
                with sp.Fori(0, CHUNKS) as n:
                    store(n)
                sp.wait_ge(stored, 16 * CHUNKS)

        @block.tensor
        def _(pe):
            if scales is None:
                source_ready = lambda w: pe.wait_ge(raw_loaded[w], 16)
            else:
                source_ready = lambda w: pe.wait_ge(scaled, w + 1)
            turning.pe(pe, units, source_ready)
            pe.wait_ge(turning.lo_ready, N_UNITS)

            def gate_up(n, j):
                reach(pe, hidden_ready, FB * n + j - 1)
                for w_hi, w_lo, ps in ((gate_hi, gate_lo, gate_ps), (up_hi, up_lo, up_ps)):
                    for k in range(KD):
                        for i, (w, x) in enumerate(((w_hi, core.xt_hi), (w_hi, core.xt_lo), (w_lo, core.xt_hi))):
                            last = pe.matmul(ps[:, j % 2, :], w[:, k, j * P:(j + 1) * P], x[:, k, cols(n, CHUNK)],
                                             start=(k == 0 and i == 0), stop=(k == KD - 1 and i == 2))
                last.then_inc(gate_up_ready, 1)

            def down(n, j):
                if j == 0:
                    reach(pe, y_read, n)
                pe.wait_ge(hidden_lo_ready, FB * n + j + 1)
                for r in range(R):
                    at = slice(r * P, (r + 1) * P)
                    for i, (h, w) in enumerate(((hidden_hi, down_hi), (hidden_hi, down_lo), (hidden_lo, down_hi))):
                        last = pe.matmul(y_ps[:, r // 2, (r % 2) * D:(r % 2 + 1) * D], h[:, j % 2, at], w[:, j, :],
                                         start=(j == 0 and r % 2 == 0 and i == 0), stop=(j == FB - 1 and i == 2),
                                         skip_group_check=True)
                last.then_inc(down_done, 1)
                if j == FB - 1:
                    pass

            def chunk(n):
                gate_up(n, 0)
                for j in range(1, FB):
                    gate_up(n, j)
                    if j == 4 and not last_layer and not (isinstance(n, int) and n == 0):
                        turn.pe_turn(pe, n - 1)
                    down(n, j - 1)
                down(n, FB - 1)

            first_then_loop(pe, CHUNKS, chunk)
            if not last_layer:
                turn.pe_turn(pe, CHUNKS - 1)

        @block.scalar
        def _(act):
            turning.act(act, units)

            def chunk(n):
                first = isinstance(n, int) and n == 0
                for j in range(FB):
                    if j == 0 and not first:
                        post.act_std(act, n - 1)
                    if j == 1 and not first and not last_layer:
                        pre.act_std(act, n - 1)
                    act.wait_ge(gate_up_ready, FB * n + j + 1)
                    reach(act, hidden_ready, FB * n + j - 1)
                    act.activation(silu[:, j % 2, :], gate_ps[:, j % 2, :], ACT.Silu).then_inc(silu_ready, 1)
                    if j == 4 and not first and not last_layer:
                        turn.act_hi(act, n - 1, n - 1)
                    act.wait_ge(hidden_ready, FB * n + j + 1)
                    reach(act, down_done, FB * n + j - 1)
                    act.activation(hidden_hi[:, j % 2, :], hidden[:, j % 2, :], ACT.Copy).then_inc(hidden_hi_ready, 1)

            first_then_loop(act, CHUNKS, chunk)
            post.act_std(act, CHUNKS - 1)
            if not last_layer:
                pre.act_std(act, CHUNKS - 1)
                turn.act_hi(act, CHUNKS - 1, CHUNKS - 1)

        @block.gpsimd
        def _(pool):
            def chunk(n):
                for j in range(FB):
                    pool.wait_ge(hidden_hi_ready, FB * n + j + 1)
                    pool.tensor_tensor(hidden_lo[:, j % 2, :], hidden[:, j % 2, :], hidden_hi[:, j % 2, :].bitcast(F32),
                                       ALU.subtract).then_inc(hidden_lo_ready, 1)

            with pool.Fori(0, CHUNKS) as n:
                chunk(n)

        @block.vector
        def _(dve):
            if scales is not None:
                dve.wait_ge(scales_loaded, 16 * 3)
                for w, (raw, at, n) in enumerate(((raw_in, 0, FB), (raw_in2, FB, FB), (raw_down, 2 * FB, KD))):
                    dve.wait_ge(raw_loaded[w], 16)
                    for j in range(n):
                        last = dve.tensor_scalar(raw[:, j, :].bitcast(F32), raw[:, j, :], ZERO_POINT,
                                                 scale_sb[:, at + j:at + j + 1], ALU.subtract, ALU.mult)
                    last.then_inc(scaled, 1)
            turning.dve(dve, units)

            y_tile = lambda r: y_ps[:, r // 2, (r % 2) * D:(r % 2 + 1) * D]

            def tail_y_stats(c):
                dve.wait_ge(down_done, FB * (c + 1))
                post.dve_variance(dve, y_tile, c)

            def tail_add(c):
                post.dve_rstd(dve, c)
                post.dve_normalise(dve, lambda r: y_normed[:, r, :], y_tile).then_inc(y_read, 1)
                dve.wait_ge(y_read, c + 1)
                dve.tensor_tensor(core.x_chunk(c), core.x_chunk(c), y_normed[:].rearrange("p a d -> p (a d)"),
                                  ALU.add).then_inc(x_updated, 1)
                dve.wait_ge(x_updated, c + 1)
                if not last_layer:
                    pre.dve_variance(dve, core.x_tile(c), c)

            def tail_xn(c):
                pre.dve_rstd(dve, c)
                pre.dve_normalise(dve, lambda r: turn.xn[:, r, :], core.x_tile(c)).then_inc(turn.xn_ready, 1)

            def chunk(n):
                first = isinstance(n, int) and n == 0
                for j in range(FB):
                    if j == 0 and not first:
                        tail_y_stats(n - 1)
                    dve.wait_ge(silu_ready, FB * n + j + 1)
                    reach(dve, hidden_lo_ready, FB * n + j - 1)
                    dve.tensor_tensor(hidden[:, j % 2, :], silu[:, j % 2, :], up_ps[:, j % 2, :],
                                      ALU.mult).then_inc(hidden_ready, 1)
                    if j == 0 and not first:
                        tail_add(n - 1)
                    if j == 1 and not first and not last_layer:
                        tail_xn(n - 1)
                    if j == 4 and not first and not last_layer:
                        turn.dve_lo(dve, n - 1, n - 1)

            first_then_loop(dve, CHUNKS, chunk)
            tail_y_stats(CHUNKS - 1)
            tail_add(CHUNKS - 1)
            if not last_layer:
                tail_xn(CHUNKS - 1)
                turn.dve_lo(dve, CHUNKS - 1, CHUNKS - 1)

HEADS = 16
DH = 128
SEG = 64
G = 4
GROUPS = HEADS // G
HALF = 2 * P
HALVES = T // HALF
UNITS = 6
PAIRS = T // P
QUADS = PAIRS // 4
STRIPS = SEG // HEADS
CREDIT = 8
NEG = -1e30


class Beat:

    def __init__(self, m, name, per=1):
        self.sem, self.per = m.sem(name), per

    def credit(self, eng):
        eng.sem_inc(self.sem, CREDIT)

    def at(self, n, m=None):
        return n * self.per + (CREDIT + (self.per if m is None else m))

    def wait(self, eng, n, m=None):
        eng.wait_ge(self.sem, self.at(n, m))

    def wait_alone(self, eng, passed, n, m=None):
        self.wait(eng, n, m)
        stand_alone(eng, passed)

    def wait_before(self, eng, n, back=1):
        eng.wait_ge(self.sem, n * self.per + (CREDIT + 1 - back))


def phase_memory_attention(nc, core, y_out, w_q, w_k, w_v, w_o, betas):
    with ExitStack() as ctx:
        m = Mem(nc, ctx, "mem")
        W = G * DH
        raw = [m.sb(f"raw_{n}", [P, KD, W]) for n in "kqv"]
        hi = [m.sb(f"{n}_hi", [P, KD, W], F32R) for n in "kqv"]
        lo = [m.sb(f"{n}_lo", [P, KD, W], F32R) for n in "kqv"]
        o_hi, o_lo = m.sb("o_hi", [P, HEADS, D], F32R), m.sb("o_lo", [P, HEADS, D], F32R)
        beta_all = m.sb("beta_all", [P, HEADS * DH])
        beta, beta_rest = m.sb("beta", [P, G, DH]), m.sb("beta_rest", [P, G, DH])
        mask = m.sb("mask", [P, P])
        keyed_hi = [m.sb(f"keyed_hi{b}", [P, KD, HALF], F32R) for b in range(2)]
        keyed_lo = [m.sb(f"keyed_lo{b}", [P, KD, HALF], F32R) for b in range(2)]
        q_t = [m.sb(f"q_t{b}", [P, G, 2, P]) for b in range(2)]
        k_t = [m.sb(f"k_t{b}", [P, G, 2, P]) for b in range(2)]
        sigma = [m.sb(f"sigma{b}", [P, G, 2, 4 * SEG]) for b in range(2)]
        sigma_kt = [m.sb(f"sigma_kt{b}", [P, G, 2, P]) for b in range(2)]
        v = [m.sb(f"v{b}", [P, 2, G, DH]) for b in range(2)]
        z_step = [m.sb(f"z_step{b}", [P, G, 2, 2]) for b in range(2)]
        exp_min = m.sb("exp_min", [P, 2, W])
        memory = m.sb("memory", [P, G, DH + 1])
        probs = m.sb("probs", [P, G, P])
        row_max, neg_max = m.sb("row_max", [P, G]), m.sb("neg_max", [P, G])
        row_sum, inv_sum = m.sb("row_sum", [P, G]), m.sb("inv_sum", [P, G])
        probs_t = m.sb("probs_t", [P, G, P])
        sigma_k = m.sb("sigma_k", [P, G, DH])
        inv_den = m.sb("inv_den", [P, 2, 2])
        neg_delta = m.sb("neg_delta", [P, G, DH])
        from_memory, local, att = (m.sb(n, [P, G, DH]) for n in ("from_memory", "local", "att"))
        att_hi, att_lo = m.sb("att_hi", [P, HEADS, P], F32R), m.sb("att_lo", [P, HEADS, P], F32R)
        y_stage = m.sb("y_stage", [P, D])

        proj_ps = m.ps("proj_ps", [P, 2, W])
        scores_ps = m.ps("scores_ps", [P, G, P])
        out_ps = m.ps("out_ps", [P, W])
        turn_ps = m.ps("turn_ps", [P, G, P])
        read_ps = m.ps("read_ps", [P, 2, 512])
        update_ps = m.ps("update_ps", [P, G, DH])

        w_loaded, betas_loaded = Beat(m, "w_loaded", 48), m.sem("betas_loaded")
        o_loaded, o_hi_ready, o_lo_ready = m.sem("o_loaded"), m.sem("o_hi_ready"), m.sem("o_lo_ready")
        w_hi, w_lo = Beat(m, "w_hi", 3), Beat(m, "w_lo", 3)
        beta_steps, beta_exp = m.sem("beta_steps"), m.sem("beta_exp")
        beta_copied = Beat(m, "beta_copied", 2)
        mask_steps = m.sem("mask_steps")
        z_cleared = m.sem("z_cleared")
        pool_passed, dve_passed = m.sem("pool_passed"), m.sem("dve_passed")
        memory_reset = Beat(m, "memory_reset")
        keyed = Beat(m, "keyed")
        projected = Beat(m, "projected", UNITS)
        raw_copied = Beat(m, "raw_copied", 4)
        relued, exped = Beat(m, "relued", 4), Beat(m, "exped", 4)
        sigma_ready, z_ready = Beat(m, "sigma_ready", 4), Beat(m, "z_ready", 2)
        v_ready = Beat(m, "v_ready", 2)
        keys_gathered = Beat(m, "keys_gathered", 2)
        scored = Beat(m, "scored")
        max_ready, neg_ready = Beat(m, "max_ready"), Beat(m, "neg_ready")
        probs_ready, probs_turned, probs_t_ready = Beat(m, "probs_ready"), Beat(m, "probs_turned"), Beat(m, "probs_t_ready")
        sigma_turned, sigma_k_ready = Beat(m, "sigma_turned"), Beat(m, "sigma_k_ready")
        retrieved, den_ready = Beat(m, "retrieved", 2), Beat(m, "den_ready", 2)
        delta_ready, from_memory_ready = Beat(m, "delta_ready", 2), Beat(m, "from_memory_ready", 2)
        updated, memory_ready = Beat(m, "updated", 2), Beat(m, "memory_ready", 2)
        attended, inv_sum_ready, local_ready = Beat(m, "attended"), Beat(m, "inv_sum_ready"), Beat(m, "local_ready")
        mixed, att_turned, att_hi_ready, att_lo_ready = (Beat(m, n) for n in ("mixed", "att_turned", "att_hi_ready", "att_lo_ready"))
        y_ready, y_copied, y_stored = Beat(m, "y_ready"), Beat(m, "y_copied"), Beat(m, "y_stored", 16)

        raw_o = [sigma[b][:].rearrange("p h t c -> p (h t c)").rearrange("p (j n) -> p j n", n=D) for b in range(2)]

        KINDS = ("k", "q", "v", "k", "q", "v")
        EVEN, ODD = 0, 1
        Q_ROWS = {EVEN: slice(0, SEG), ODD: slice(SEG, P)}
        K_ROWS = {EVEN: slice(SEG, P), ODD: slice(0, SEG)}
        SIGMA_OF = {EVEN: slice(P, 2 * P), ODD: slice(0, P)}

        def groups(eng, group):
            with eng.Fori(0, GROUPS) as g:
                group(g)

        ROWS = 2 * G * STRIPS

        def before_pair(q, b, p):
            slot = 2 * b + p
            return (q, slot - 1) if slot else (q - 1, 3)

        def turned_rows():
            return turn_ps[:].rearrange("p a b -> p (a b)").rearrange("p (r j) -> p j r", j=HEADS)

        def quads(eng, g, before, pair, after):
            def body(i, first, last):
                for b in range(2):
                    for p in range(2):
                        pair(g * QUADS + i, i, b, p, first and b == 0 and p == 0, last and b == 1)
            before(g * QUADS)
            body(0, True, False)
            with eng.Fori(1, QUADS - 1) as i:
                body(i, False, False)
            body(QUADS - 1, False, True)
            after(g * QUADS + (QUADS - 1))

        block = m.start()

        @block.sync
        def _(sp):
            w_loaded.credit(sp), y_stored.credit(sp)

            def load_weights(g):
                for src, dst in zip((w_k, w_q, w_v), raw):
                    sp.dma_start(dst[:], src[:, cols(g, W)].rearrange("(k p) n -> p k n", p=P)).then_inc(w_loaded.sem, 16)

            load_weights(0)
            sp.dma_start(beta_all[:], betas.rearrange("a h b d -> a (h b d)").to_broadcast([P, HEADS * DH])).then_inc(betas_loaded, 16)
            for i in range(2):
                sp.dma_start(raw_o[i], w_o[i * (HEADS // 2) * P:(i + 1) * (HEADS // 2) * P, :].rearrange("(j p) n -> p j n", p=P)
                             ).then_inc(o_loaded, 16)

            def group(g, last):
                if not last:
                    w_lo.wait(sp, g)
                    load_weights(g + 1)
                with sp.Fori(0, QUADS) as i:
                    y_copied.wait(sp, g * QUADS + i)
                    sp.dma_start(y_out.rearrange("(t r) d -> t r d", r=SEG)[:, bass.ds(g * (G * STRIPS), G * STRIPS), :][cols(i, 8), :, :],
                                 y_stage[:]).then_inc(y_stored.sem, 16)

            with sp.Fori(0, GROUPS - 1) as g:
                group(g, False)
            group(GROUPS - 1, True)
            y_stored.wait(sp, GROUPS * QUADS - 1)

        @block.gpsimd
        def _(pool):
            for s in (keyed, mixed, beta_copied, keys_gathered):
                s.credit(pool)
            pool.memset(mask[:], 0.0).then_inc(mask_steps, 1)
            pool.wait_ge(mask_steps, 1)
            pool.affine_select(out=mask[:, 0:SEG], in_=mask[:, 0:SEG], compare_op=ALU.is_ge, fill=NEG, base=-SEG,
                               pattern=[[-1, SEG]], channel_multiplier=1).then_inc(mask_steps, 1)
            pool.affine_select(out=mask[:, SEG:P], in_=mask[:, SEG:P], compare_op=ALU.is_ge, fill=NEG, base=0,
                               pattern=[[-1, SEG]], channel_multiplier=1).then_inc(mask_steps, 1)
            pool.wait_ge(mask_steps, 3)
            pool.affine_select(out=mask[:, SEG:P], in_=mask[:, SEG:P], compare_op=ALU.is_ge, fill=NEG, base=SEG - 1,
                               pattern=[[0, SEG]], channel_multiplier=-1).then_inc(mask_steps, 1)
            pool.wait_ge(beta_steps, 2)

            def key_order(h, c, b):
                projected.wait_alone(pool, pool_passed, h - 2)
                for src, dst in ((core.xt_hi, keyed_hi[b]), (core.xt_lo, keyed_lo[b])):
                    s = src[:, :, cols(c, HALF)].rearrange("p k (t s c) -> p k t s c", t=2, s=2)
                    d = dst[:].rearrange("p k (t s c) -> p k t s c", t=2, s=2)
                    for k in range(KD):
                        for seg in range(2):
                            last = pool.tensor_copy(d[:, k, :, 1 - seg, :], s[:, k, :, seg, :].bitcast(F32))
                last.then_inc(keyed.sem, 1)

            def gather_keys(h, b, half):
                sigma_ready.wait_alone(pool, pool_passed, h, 2 * half + 1)
                src = sigma[b][:, 2 * half:2 * half + 2, :, :].rearrange("p h t (s c) -> p (h t) s c", c=SEG)[:, :, 0:4:3, :]
                dst = sigma_kt[b][:, 2 * half:2 * half + 2, :, :].rearrange("p h t (s c) -> p (h t) s c", c=SEG)
                pool.tensor_copy(dst, src).then_inc(keys_gathered.sem, 1)

            def group(g):
                local_ready.wait_before(pool, g * PAIRS)
                stand_alone(pool, pool_passed)
                pool.tensor_copy(beta[:], beta_all[:, cols(g, W)].rearrange("p (h d) -> p h d", h=G)).then_inc(beta_copied.sem, 1)
                beta_copied.wait_alone(pool, pool_passed, g, 1)
                pool.tensor_scalar(beta_rest[:], beta[:], -1.0, 1.0, ALU.mult, ALU.add).then_inc(beta_copied.sem, 1)

                def pair(q, i, b, p, first, last):
                    h, c = q * 2 + b, i * 2 + b
                    if p == 0 and not last:
                        key_order(h + 1, c + 1, 1 - b)
                    if not last:
                        gather_keys(h + 1, 1 - b, p)
                    n = h * 2 + p
                    from_memory_ready.wait(pool, n)
                    local_ready.wait(pool, n)
                    att_turned.wait_before(pool, n)
                    pool.tensor_tensor(att[:], from_memory[:], local[:], ALU.add).then_inc(mixed.sem, 1)

                def before(q):
                    h = q * 2
                    key_order(h, 0, 0)
                    gather_keys(h, 0, 0)
                    gather_keys(h, 0, 1)

                quads(pool, g, before, pair, lambda q: None)

            groups(pool, group)

        @block.tensor
        def _(pe):
            for s in (projected, scored, retrieved, updated, sigma_turned, probs_turned, att_turned, attended, y_ready):
                s.credit(pe)

            def unit(h, c, b, u):
                bank = proj_ps[:, u % 2, :]
                if u == 0:
                    keyed.wait(pe, h)
                before = (u - 2) % UNITS
                turn = h if u >= 2 else h - 1
                if KINDS[before] == "v":
                    v_ready.wait(pe, turn, before // 3 + 1)
                else:
                    sigma_ready.wait(pe, turn, 2 * (before // 3) + before % 3 + 1)
                kind, half = KINDS[u], u // 3
                w_h, w_l = hi["kqv".index(kind)], lo["kqv".index(kind)]
                if kind == "v":
                    at = slice(half * P, (half + 1) * P)
                    for k in range(KD):
                        for i, (x, w) in enumerate(((keyed_hi, w_h), (keyed_hi, w_l), (keyed_lo, w_h))):
                            last = pe.matmul(bank, x[b][:, k, at], w[:, k, :], start=(k == 0 and i == 0),
                                             stop=(k == KD - 1 and i == 2))
                else:
                    if kind == "k":
                        x_h, x_l = (lambda k: keyed_hi[b][:, k, :]), (lambda k: keyed_lo[b][:, k, :])
                    else:
                        x_h = lambda k: core.xt_hi[:, k, cols(c, HALF)]
                        x_l = lambda k: core.xt_lo[:, k, cols(c, HALF)]
                    for a in range(2):
                        head = slice((2 * half + a) * DH, (2 * half + a + 1) * DH)
                        for k in range(KD):
                            for i, (w, x) in enumerate(((w_h, x_h), (w_h, x_l), (w_l, x_h))):
                                last = pe.matmul(bank[:, a * HALF:(a + 1) * HALF], w[:, k, head], x(k),
                                                 start=(k == 0 and i == 0), stop=(k == KD - 1 and i == 2))
                last.then_inc(projected.sem, 1)

            def retrieve(n, b, p, seg):
                if seg == EVEN:
                    memory_ready.wait_before(pe, n)
                    from_memory_ready.wait_before(pe, n)
                else:
                    memory_ready.wait(pe, n, 1)
                    from_memory_ready.wait(pe, n, 1)
                for h in range(G):
                    last = pe.matmul(read_ps[:, h // 2, (h % 2) * (DH + 1):(h % 2 + 1) * (DH + 1)],
                                     sigma[b][:, h, p, SIGMA_OF[seg]], memory[:, h, :], start=True, stop=True)
                last.then_inc(retrieved.sem, 1)

            def update(n, seg):
                if seg == EVEN:
                    sigma_k_ready.wait(pe, n)
                delta_ready.wait(pe, n, seg + 1)
                rows = K_ROWS[seg]
                for h in range(G):
                    last = pe.matmul(update_ps[:, h, :], sigma_k[rows, h, :], neg_delta[rows, h, :], start=True, stop=True)
                last.then_inc(updated.sem, 1)

            def turn_att(n):
                probs_t_ready.wait(pe, n)
                mixed.wait(pe, n)
                for h in range(G):
                    out = turn_ps[:].rearrange("p a b -> p (a b)").rearrange("p (s h c) -> p h s c", s=2, h=G)[:, h, :, :]
                    last = pe.transpose(out, att[:, h, :], core.ident[:])
                last.then_inc(att_turned.sem, 1)

            def project_out(q, js):
                if js.start == 0:
                    att_lo_ready.wait(pe, q * 4 + 3)
                    local_ready.wait(pe, q * 4 + 3)
                for j in js:
                    for i, (a, w) in enumerate(((att_hi, o_hi), (att_hi, o_lo), (att_lo, o_hi))):
                        last = pe.matmul(out_ps[:, 0:D], a[:, j, :], w[:, j, :], start=(j == 0 and i == 0),
                                         stop=(j == HEADS - 1 and i == 2))
                if js.stop == HEADS:
                    last.then_inc(y_ready.sem, 1)

            def group(g):
                def before(q):
                    w_lo.wait(pe, g)
                    for u in range(UNITS):
                        unit(q * 2, 0, 0, u)

                def pair(q, i, b, p, first, last):
                    h, c, n = q * 2 + b, i * 2 + b, q * 4 + (b * 2 + p)
                    project_last = (b, p) == (0, 0) and not first
                    next_unit = (lambda u: None) if last else (lambda u: unit(h + 1, c + 1, 1 - b, 3 * p + u))
                    if p == 0:
                        sigma_ready.wait(pe, h)
                        v_ready.wait(pe, h)
                    max_ready.wait_before(pe, n)
                    for hh in range(G):
                        mm = pe.matmul(scores_ps[:, hh, :], q_t[b][:, hh, p, :], k_t[b][:, hh, p, :], start=True, stop=True)
                    mm.then_inc(scored.sem, 1)
                    if first:
                        memory_reset.wait(pe, g)
                    retrieve(n, b, p, EVEN)
                    if not first:
                        turn_att(n - 1)
                    next_unit(0)
                    if p == 0:
                        keys_gathered.wait(pe, h)
                    if first:
                        probs_t_ready.wait_before(pe, n)
                    else:
                        att_lo_ready.wait(pe, n - 1)
                    for hh in range(G):
                        mm = pe.transpose(turn_ps[:, hh, :], sigma_kt[b][:, hh, p, :], core.ident[:])
                    mm.then_inc(sigma_turned.sem, 1)
                    if project_last:
                        project_out(q - 1, range(0, HEADS // 2))
                    next_unit(1)
                    probs_ready.wait(pe, n)
                    sigma_k_ready.wait(pe, n)
                    for hh in range(G):
                        mm = pe.transpose(turn_ps[:, hh, :], probs[:, hh, :], core.ident[:])
                    mm.then_inc(probs_turned.sem, 1)
                    update(n, EVEN)
                    if project_last:
                        project_out(q - 1, range(HEADS // 2, HEADS))
                    probs_t_ready.wait(pe, n)
                    if (b, p) == (0, 0):
                        y_copied.wait_before(pe, q)
                    for hh in range(G):
                        mm = pe.matmul(out_ps[:, hh * DH:(hh + 1) * DH], probs_t[:, hh, :], v[b][:, p, hh, :], start=True, stop=True)
                    mm.then_inc(attended.sem, 1)
                    retrieve(n, b, p, ODD)
                    next_unit(2)
                    update(n, ODD)

                def after(q):
                    turn_att(q * 4 + 3)
                    project_out(q, range(0, HEADS))

                quads(pe, g, before, pair, after)

            groups(pe, group)

        @block.scalar
        def _(act):
            for s in (y_copied, w_hi, raw_copied, relued, exped, v_ready, probs_ready, probs_t_ready, sigma_k_ready, att_hi_ready):
                s.credit(act)
            act.wait_ge(betas_loaded, 16)
            act.activation(beta_all[:], beta_all[:], ACT.Exp, scale=-1.0).then_inc(beta_exp, 1)
            act.wait_ge(o_loaded, 32)
            for i in range(2):
                act.activation(o_hi[:, i * (HEADS // 2):(i + 1) * (HEADS // 2), :], raw_o[i], ACT.Copy).then_inc(o_hi_ready, 1)

            def unit(h, b, u):
                projected.wait(act, h, u + 1)
                bank = proj_ps[:, u % 2, :]
                kind, half = KINDS[u], u // 3
                if kind == "v":
                    act.activation(v[b][:, half, :, :].rearrange("p h d -> p (h d)"), bank, ACT.Copy).then_inc(v_ready.sem, 1)
                    return
                s = 2 * half + u % 3
                dst = (k_t if kind == "k" else q_t)[b]
                act.activation(dst[:, 2 * half:2 * half + 2, :, :].rearrange("p h t c -> p (h t c)"), bank,
                               ACT.Copy).then_inc(raw_copied.sem, 1)
                sigma_ready.wait(act, h if s >= 2 else h - 1, (s - 2) % 4 + 1)
                act.activation(exp_min[:, s % 2, :], bank, ACT.Relu, scale=-1.0).then_inc(relued.sem, 1)
                relued.wait(act, h, s + 1)
                act.activation(exp_min[:, s % 2, :], exp_min[:, s % 2, :], ACT.Exp, scale=-1.0).then_inc(exped.sem, 1)

            def att_parts(q, slot):
                if slot == 0:
                    y_ready.wait_before(act, q)
                att_turned.wait(act, q * 4 + slot)
                act.activation(att_hi[:, :, slot * ROWS:(slot + 1) * ROWS], turned_rows(),
                               ACT.Copy).then_inc(att_hi_ready.sem, 1)

            def copy_y(q):
                y_ready.wait(act, q)
                y_stored.wait_before(act, q)
                act.activation(y_stage[:], out_ps[:, 0:D], ACT.Copy).then_inc(y_copied.sem, 1)

            def group(g):
                def before(q):
                    w_loaded.wait(act, g)
                    for src, dst in zip(raw, hi):
                        act.activation(dst[:], src[:], ACT.Copy).then_inc(w_hi.sem, 1)
                    for u in range(UNITS):
                        unit(q * 2, 0, u)

                def pair(q, i, b, p, first, last):
                    h, n = q * 2 + b, q * 4 + (b * 2 + p)
                    next_unit = (lambda u: None) if last else (lambda u: unit(h + 1, 1 - b, 3 * p + u))
                    neg_ready.wait(act, n)
                    for hh in range(G):
                        e = act.activation(probs[:, hh, :], probs[:, hh, :], ACT.Exp, bias=neg_max[:, hh:hh + 1],
                                           accum_out=row_sum[:, hh:hh + 1])
                    e.then_inc(probs_ready.sem, 1)
                    if not first:
                        att_parts(*before_pair(q, b, p))
                    next_unit(0)
                    sigma_turned.wait(act, n)
                    act.activation(sigma_k[:], turn_ps[:], ACT.Copy).then_inc(sigma_k_ready.sem, 1)
                    probs_turned.wait(act, n)
                    act.activation(probs_t[:], turn_ps[:], ACT.Copy).then_inc(probs_t_ready.sem, 1)
                    if (b, p) == (0, 0) and not first:
                        copy_y(q - 1)
                    next_unit(1)
                    next_unit(2)

                def after(q):
                    att_parts(q, 3)
                    copy_y(q)

                quads(act, g, before, pair, after)

            groups(act, group)

        @block.vector
        def _(dve):
            for s in (w_lo, sigma_ready, z_ready, max_ready, neg_ready, den_ready, delta_ready, from_memory_ready,
                      memory_ready, memory_reset, inv_sum_ready, local_ready, att_lo_ready):
                s.credit(dve)
            dve.wait_ge(beta_exp, 1)
            dve.tensor_scalar(beta_all[:], beta_all[:], 1.0, None, ALU.add).then_inc(beta_steps, 1)
            dve.wait_ge(beta_steps, 1)
            dve.reciprocal(beta_all[:], beta_all[:]).then_inc(beta_steps, 1)
            for i in range(2):
                dve.wait_ge(o_hi_ready, i + 1)
                part = slice(i * (HEADS // 2), (i + 1) * (HEADS // 2))
                dve.tensor_tensor(o_lo[:, part, :], raw_o[i], o_hi[:, part, :].bitcast(F32), ALU.subtract).then_inc(o_lo_ready, 1)
            dve.wait_ge(o_lo_ready, 2)
            dve.wait_ge(mask_steps, 4)

            def unit(h, b, u):
                kind, half = KINDS[u], u // 3
                if kind == "v":
                    return
                s = 2 * half + u % 3
                exped.wait(dve, h, s + 1)
                heads = slice(2 * half, 2 * half + 2)
                x = proj_ps[:, u % 2, :].rearrange("p (ht s c) -> p ht s c", s=2, c=SEG)
                e = exp_min[:, s % 2, :].rearrange("p (ht s c) -> p ht s c", s=2, c=SEG)
                out = sigma[b][:, heads, :, :].rearrange("p h t (s c) -> p (h t) s c", c=SEG)
                for seg in (EVEN, ODD):
                    to = 3 * seg if kind == "k" else 2 - seg
                    last = dve.scalar_tensor_tensor(out=out[:, :, to, :], in0=x[:, :, seg, :], scalar=0.0,
                                                    in1=e[:, :, seg, :], op0=ALU.max, op1=ALU.add)
                last.then_inc(sigma_ready.sem, 1)
                if kind == "k":
                    sigma_ready.wait(dve, h, s + 1)
                    dve.reduce_sum(z_step[b][:, heads, :, :].rearrange("p h t s -> p (h t) s"), out[:, :, 0:4:3, :],
                                   AX_X).then_inc(z_ready.sem, 1)

            def retrieval(n, b, p, seg):
                retrieved.wait(dve, n, seg + 1)
                dve.reciprocal(inv_den[:], read_ps[:, :, DH:2 * (DH + 1):DH + 1]).then_inc(den_ready.sem, 1)
                den_ready.wait(dve, n, seg + 1)
                got = lambda h, rows: read_ps[rows, h // 2, (h % 2) * (DH + 1):(h % 2) * (DH + 1) + DH]
                den = lambda h, rows: inv_den[rows, h // 2, h % 2:h % 2 + 1]
                rows = K_ROWS[seg]
                for h in range(G):
                    last = dve.scalar_tensor_tensor(out=neg_delta[rows, h, :], in0=got(h, rows), scalar=den(h, rows),
                                                    in1=v[b][rows, p, h, :], op0=ALU.mult, op1=ALU.subtract)
                last.then_inc(delta_ready.sem, 1)
                if seg == EVEN:
                    mixed.wait_before(dve, n)
                rows = Q_ROWS[seg]
                for h in range(G):
                    last = dve.scalar_tensor_tensor(out=from_memory[rows, h, :], in0=got(h, rows), scalar=den(h, rows),
                                                    in1=beta[rows, h, :], op0=ALU.mult, op1=ALU.mult)
                last.then_inc(from_memory_ready.sem, 1)

            def update(n, b, p, seg):
                updated.wait(dve, n, seg + 1)
                dve.tensor_tensor(memory[:, :, 0:DH], memory[:, :, 0:DH], update_ps[:], ALU.subtract)
                z = memory[:, :, DH]
                dve.tensor_tensor(z, z, z_step[b][:, :, p, 1 - seg], ALU.add).then_inc(memory_ready.sem, 1)
                memory_ready.wait_alone(dve, dve_passed, n, seg + 1)

            def att_parts(q, slot):
                att_hi_ready.wait(dve, q * 4 + slot)
                columns = slice(slot * ROWS, (slot + 1) * ROWS)
                dve.tensor_tensor(att_lo[:, :, columns], turned_rows(), att_hi[:, :, columns].bitcast(F32),
                                  ALU.subtract).then_inc(att_lo_ready.sem, 1)

            def group(g):
                def before(q):
                    for i, (src, part, dst) in enumerate(zip(raw, hi, lo)):
                        w_hi.wait(dve, g, i + 1)
                        dve.tensor_tensor(dst[:], src[:], part[:].bitcast(F32), ALU.subtract).then_inc(w_lo.sem, 1)
                    dve.memset(memory[:], 0.0)
                    beta_copied.wait(dve, g)
                    dve.memset(z_step[1][:], 0.0).then_inc(z_cleared, 1)
                    dve.wait_ge(z_cleared, g + 1)
                    dve.memset(memory[:, :, DH], 1.0 / DH).then_inc(memory_reset.sem, 1)
                    memory_reset.wait(dve, g)
                    for u in range(UNITS):
                        unit(q * 2, 0, u)

                def pair(q, i, b, p, first, last):
                    h, n = q * 2 + b, q * 4 + (b * 2 + p)
                    next_unit = (lambda u: None) if last else (lambda u: unit(h + 1, 1 - b, 3 * p + u))
                    scored.wait_alone(dve, dve_passed, n)
                    for hh in range(G):
                        t = dve.tensor_tensor_reduce(probs[:, hh, :], scores_ps[:, hh, :], mask[:], DH ** -0.5, NEG,
                                                     ALU.add, ALU.max, row_max[:, hh:hh + 1])
                    t.then_inc(max_ready.sem, 1)
                    max_ready.wait(dve, n)
                    dve.tensor_scalar(neg_max[:], row_max[:], -1.0, None, ALU.mult).then_inc(neg_ready.sem, 1)
                    retrieval(n, b, p, EVEN)
                    if not first:
                        att_parts(*before_pair(q, b, p))
                    next_unit(0)
                    update(n, b, p, EVEN)
                    next_unit(1)
                    attended.wait(dve, n)
                    dve.reciprocal(inv_sum[:], row_sum[:]).then_inc(inv_sum_ready.sem, 1)
                    inv_sum_ready.wait(dve, n)
                    for hh in range(G):
                        t = dve.scalar_tensor_tensor(out=local[:, hh, :], in0=out_ps[:, hh * DH:(hh + 1) * DH],
                                                     scalar=inv_sum[:, hh:hh + 1], in1=beta_rest[:, hh, :],
                                                     op0=ALU.mult, op1=ALU.mult)
                    t.then_inc(local_ready.sem, 1)
                    retrieval(n, b, p, ODD)
                    next_unit(2)
                    update(n, b, p, ODD)

                quads(dve, g, before, pair, lambda q: att_parts(q, 3))

            groups(dve, group)

def phase_residual(nc, core, x_in, y_in, name):
    with ExitStack() as ctx:
        m = Mem(nc, ctx, name)
        post, pre, turn = Stats(m, "post"), Stats(m, "pre"), Turn(m, core)
        y, y_normed = m.sb("y", [P, TILES, D]), m.sb("y_normed", [P, R, D])
        loaded = [m.sem(f"loaded{c}") for c in range(CHUNKS)]
        y_read, x_updated = m.sem("y_read"), m.sem("x_updated")
        block = m.start()

        @block.sync
        def _(sp):
            for c in range(CHUNKS):
                for src, dst in ((y_in, y), (x_in[0], core.x)):
                    sp.dma_start(dst[:, c * R:(c + 1) * R, :],
                                 src[c * CHUNK:(c + 1) * CHUNK, :].rearrange("(a p) d -> p a d", p=P)).then_inc(loaded[c], 16)

        @block.vector
        def _(dve):
            def chunk(c):
                y_tile = lambda r: y[:, c * R + r, :]
                dve.wait_ge(loaded[c], 32)
                post.dve_variance(dve, y_tile, c)
                post.dve_rstd(dve, c)
                post.dve_normalise(dve, lambda r: y_normed[:, r, :], y_tile).then_inc(y_read, 1)
                dve.wait_ge(y_read, c + 1)
                dve.tensor_tensor(core.x_chunk(c), core.x_chunk(c), y_normed[:].rearrange("p a d -> p (a d)"),
                                  ALU.add).then_inc(x_updated, 1)
                dve.wait_ge(x_updated, c + 1)
                pre.dve_variance(dve, core.x_tile(c), c)
                pre.dve_rstd(dve, c)
                reach(dve, turn.turned_ready, KD * c)
                pre.dve_normalise(dve, lambda r: turn.xn[:, r, :], core.x_tile(c)).then_inc(turn.xn_ready, 1)
                turn.dve_lo(dve, c, c)

            for c in range(CHUNKS):
                chunk(c)

        @block.scalar
        def _(act):
            for c in range(CHUNKS):
                post.act_std(act, c)
                pre.act_std(act, c)
                turn.act_hi(act, c, c)

        @block.tensor
        def _(pe):
            for c in range(CHUNKS):
                turn.pe_turn(pe, c)



H1 = 16
HD = 16
QB = (T // P)
TERMS = ((0, 0), (0, 1), (1, 0), (0, 2), (2, 0), (1, 1))
MAX_ROW = HD * len(TERMS)
STACK = MAX_ROW + 3
PARTS = 3


def phase_qkv(nc, core, values, w_qkv, b_qkv, q_parts, k_parts):
    NB = 3 * D // P
    QK = 4
    with ExitStack() as ctx:
        m = Mem(nc, ctx, "qkv")
        raw = m.sb("raw", [P, NB, D])
        w_hi, w_lo = m.sb("w_hi", [P, KD, NB * P], F32R), m.sb("w_lo", [P, KD, NB * P], F32R)
        bias = m.sb("bias", [P, NB])
        biased = m.sb("biased", [P, NB, CHUNK])
        rest = m.sb("rest", [P, QK, CHUNK])
        parts = m.sb("parts", [P, QK, PARTS, CHUNK], BF16)
        qkv_ps = m.ps("qkv_ps", [P, NB, CHUNK])
        v_ps = m.ps("v_ps", [P, 2, CHUNK])

        raw_loaded, bias_loaded = m.sem("raw_loaded"), m.sem("bias_loaded")
        projected, biased_ready = m.sem("projected"), m.sem("biased_ready")
        part0_ready, rest_ready, part1_ready, part2_ready = (m.sem(s) for s in ("part0_ready", "rest_ready", "part1_ready", "part2_ready"))
        stored = [m.sem(f"stored{j}") for j in range(QK)]
        v_turned, v_copied = m.sem("v_turned"), m.sem("v_copied")
        turning = TurnWeights(m, core, lambda u: v_ps[:, u % 2, :])
        units = [([raw[:, j, k * P:(k + 1) * P] for j in range(j0, j0 + 3)], w_hi[:, k, j0 * P:(j0 + 3) * P],
                  w_lo[:, k, j0 * P:(j0 + 3) * P], 0) for k in range(KD) for j0 in (0, 3)]
        block = m.start()

        @block.sync
        def _(sp):
            sp.dma_start(raw[:], w_qkv.rearrange("(j p) n -> p j n", p=P)).then_inc(raw_loaded, 16)
            with nc.allow_non_contiguous_dma(reason="one bias per partition"):
                sp.dma_start(bias[:], b_qkv.rearrange("(j p) -> p j", p=P)).then_inc(bias_loaded, 16)
            with sp.Fori(0, CHUNKS) as n:
                for j in range(QK):
                    sp.wait_ge(part2_ready, QK * n + j + 1)
                    dst = (q_parts, q_parts, k_parts, k_parts)[j]
                    rows = slice((j % 2) * P, (j % 2 + 1) * P)
                    sp.dma_start(dst[:, rows, cols(n, CHUNK)].rearrange("a p n -> p a n"), parts[:, j, :, :]).then_inc(stored[j], 16)
            for j in range(QK):
                sp.wait_ge(stored[j], 16 * CHUNKS)

        @block.tensor
        def _(pe):
            turning.pe(pe, units, lambda w: pe.wait_ge(raw_loaded, 16))
            pe.wait_ge(turning.lo_ready, len(units))

            def turn_values(n, j):
                pe.wait_ge(biased_ready, NB * n + j + 1)
                reach(pe, v_copied, 2 * n + (j - QK) - 1)
                for r in range(R):
                    last = pe.transpose(v_ps[:, j - QK, r * P:(r + 1) * P], biased[:, j, r * P:(r + 1) * P], core.ident[:])
                last.then_inc(v_turned, 1)

            def chunk(n):
                for j in range(NB):
                    reach(pe, biased_ready, NB * n + j + 1 - NB)
                    for k in range(KD):
                        for i, (w, x) in enumerate(((w_hi, core.xt_hi), (w_hi, core.xt_lo), (w_lo, core.xt_hi))):
                            last = pe.matmul(qkv_ps[:, j, :], w[:, k, j * P:(j + 1) * P], x[:, k, cols(n, CHUNK)],
                                             start=(k == 0 and i == 0), stop=(k == KD - 1 and i == 2))
                    last.then_inc(projected, 1)
                for j in range(QK, NB):
                    turn_values(n, j)

            first_then_loop(pe, CHUNKS, chunk)

        @block.vector
        def _(dve):
            turning.dve(dve, units)
            dve.wait_ge(bias_loaded, 16)

            def chunk(n):
                for s in range(NB + 2):
                    if s < NB:
                        dve.wait_ge(projected, NB * n + s + 1)
                        if s < QK:
                            reach(dve, rest_ready, QK * n + s + 1 - QK)
                        else:
                            reach(dve, v_turned, 2 * n + (s - QK) + 1 - 2)
                        dve.tensor_scalar(biased[:, s, :], qkv_ps[:, s, :], bias[:, s:s + 1],
                                          HD ** -0.5 if s < 2 else 1.0, ALU.add, ALU.mult).then_inc(biased_ready, 1)
                    if 0 <= s - 1 < QK:
                        j = s - 1
                        dve.wait_ge(part0_ready, QK * n + j + 1)
                        dve.tensor_tensor(rest[:, j, :], biased[:, j, :], parts[:, j, 0, :], ALU.subtract).then_inc(rest_ready, 1)
                    if 0 <= s - 2 < QK:
                        j = s - 2
                        dve.wait_ge(part1_ready, QK * n + j + 1)
                        dve.tensor_tensor(parts[:, j, 2, :], rest[:, j, :], parts[:, j, 1, :], ALU.subtract).then_inc(part2_ready, 1)

            first_then_loop(dve, CHUNKS, chunk)

        @block.scalar
        def _(act):
            turning.act(act, units)

            def chunk(n):
                for s in range(QK + 1):
                    if s < QK:
                        act.wait_ge(biased_ready, NB * n + s + 1)
                        reach(act, stored[s], 16 * n)
                        act.activation(parts[:, s, 0, :], biased[:, s, :], ACT.Copy).then_inc(part0_ready, 1)
                    if s > 0:
                        j = s - 1
                        act.wait_ge(rest_ready, QK * n + j + 1)
                        act.activation(parts[:, j, 1, :], rest[:, j, :], ACT.Copy).then_inc(part1_ready, 1)
                for j in range(2):
                    act.wait_ge(v_turned, 2 * n + j + 1)
                    act.activation(values[:, cols(n, R), j * P:(j + 1) * P], v_ps[:, j, :].rearrange("p (a d) -> p a d", a=R),
                                   ACT.Copy).then_inc(v_copied, 1)

            first_then_loop(act, CHUNKS, chunk)


def phase_attention(nc, core, att, values, q_parts, k_parts, max_parts):
    GROUPS1 = H1 // G
    with ExitStack() as ctx:
        m = Mem(nc, ctx, "att")
        q_stack = m.sb("q_stack", [P, 2, G, T], BF16)
        k_stack = m.sb("k_stack", [P, 2, G, T], BF16)
        v_ones = m.sb("v_ones", [P, QB, G, 2 * HD])
        probs = m.sb("probs", [P, 2, 2, 2, CHUNK])
        causal = m.sb("causal", [P, P])
        masked = m.sb("masked", [P, 2, P])
        maxima = m.sb("maxima", [P, G, QB, 5])
        neg_max, row_max = m.sb("neg_max", [P, G * QB]), m.sb("row_max", [P, G * QB])
        max_rest = m.sb("max_rest", [G * QB, 2, P])
        max_split = m.sb("max_split", [G * QB, PARTS, P], BF16)
        out_t = m.sb("out_t", [P, CHUNK])
        inv_sum = m.sb("inv_sum", [P, R, G])

        keyed_ps = m.ps("keyed_ps", [P, 2, 2, CHUNK])
        rows_ps = m.ps("rows_ps", [P, 2, CHUNK])
        out_ps = m.ps("out_ps", [P, CHUNK])
        misc_ps = m.ps("misc_ps", [P, CHUNK])

        E_STEPS = [(c, kb) for c in range(CHUNKS) for kb in range(R * (c + 1))]
        M_STEPS = [(c, r, kc) for c in range(CHUNKS) for r in range(R) for kc in range(c + 1)]
        NS = len(E_STEPS)
        N_DIAGONAL = CHUNKS * R
        assert len(M_STEPS) == NS

        stacks_loaded = Beat(m, "stacks_loaded", 16 * 2 * len(TERMS))
        max_loaded = Beat(m, "max_loaded", 16)
        max_stored = Beat(m, "max_stored", 16)
        v_ones_ready = Beat(m, "v_ones_ready")
        rows_scored, rows_reduced = Beat(m, "rows_scored", NS * G), Beat(m, "rows_reduced", NS * G)
        max_ready, neg_max_ready, max_turned = Beat(m, "max_ready"), Beat(m, "neg_max_ready"), Beat(m, "max_turned")
        split_steps, max_split_ready = Beat(m, "split_steps", 4), Beat(m, "max_split_ready")
        keyed_scored, exped = Beat(m, "keyed_scored", NS * 2), Beat(m, "exped", NS * 2)
        triangled = Beat(m, "triangled", N_DIAGONAL * 2)
        weighted = Beat(m, "weighted", NS)
        out_copied, out_turned, inv_ready, out_ready = (Beat(m, s, CHUNKS) for s in ("out_copied", "out_turned", "inv_ready", "out_ready"))
        prepared, ones_rows = m.sem("prepared"), m.sem("ones_rows")
        pool_passed, dve_passed, pe_passed = m.sem("pool_passed"), m.sem("dve_passed"), m.sem("pe_passed")
        slot = lambda g: g % 2
        block = m.start()

        def passes(eng, prologue, group):
            prologue(0)
            with eng.Fori(0, GROUPS1 - 1) as g:
                group(g, False)
            group(GROUPS1 - 1, True)

        @block.sync
        def _(sp):
            stacks_loaded.credit(sp), max_loaded.credit(sp), max_stored.credit(sp)

            def load_stacks(g):
                if not (isinstance(g, int) and g == 0):
                    weighted.wait_before(sp, g - 1)
                for stack, src, which in ((q_stack, q_parts, 0), (k_stack, k_parts, 1)):
                    for t, term in enumerate(TERMS):
                        rows = src[term[which], cols(g, G * HD), :].rearrange("(h d) n -> d h n", d=HD)
                        sp.dma_start(stack[t * HD:(t + 1) * HD, bass.ds(slot(g), 1), :, :].rearrange("d a h n -> d (a h) n"),
                                     rows).then_inc(stacks_loaded.sem, 16)

            def move_max(g):
                max_split_ready.wait(sp, g)
                sp.dma_start(max_parts.rearrange("a r n -> r a n"), max_split[:]).then_inc(max_stored.sem, 16)
                max_stored.wait(sp, g)
                sp.dma_start(q_stack[MAX_ROW:STACK, bass.ds(slot(g), 1), :, :].rearrange("d a h n -> d (a h n)"),
                             max_parts.rearrange("a r n -> a (r n)")).then_inc(max_loaded.sem, 16)

            def prologue(g):
                load_stacks(0)
                move_max(0)

            def group(g, last):
                if not last:
                    load_stacks(g + 1)
                    move_max(g + 1)

            passes(sp, prologue, group)

        @block.gpsimd
        def _(pool):
            v_ones_ready.credit(pool), triangled.credit(pool)
            pool.memset(k_stack[MAX_ROW:P, :, :, :], 1.0).then_inc(ones_rows, 1)
            pool.wait_ge(ones_rows, 1)
            pool.memset(causal[:], 0.0).then_inc(prepared, 1)
            pool.memset(v_ones[:], 0.0).then_inc(prepared, 1)
            pool.memset(maxima[:], NEG).then_inc(prepared, 1)
            pool.wait_ge(prepared, 3)
            pool.affine_select(out=causal[:], in_=causal[:], compare_op=ALU.is_ge, fill=NEG, base=0,
                               pattern=[[-1, P]], channel_multiplier=1).then_inc(prepared, 1)
            pool.memset(v_ones[:, :, :, HD:HD + 1], 1.0).then_inc(prepared, 1)
            pool.wait_ge(prepared, 5)

            def group(g):
                weighted.wait_before(pool, g)
                stand_alone(pool, pool_passed)
                pool.tensor_copy(v_ones[:, :, :, 0:HD], values[:, :, cols(g, G * HD)].rearrange("p b (h d) -> p b h d", d=HD)
                                 ).then_inc(v_ones_ready.sem, 1)
                d = 0
                for s, (c, kb) in enumerate(E_STEPS):
                    r = kb - R * c
                    if r < 0:
                        continue
                    for hp in range(2):
                        exped.wait_alone(pool, pool_passed, g, 2 * s + hp + 1)
                        block_ = probs[:, s % 2, hp, :, r * P:(r + 1) * P]
                        pool.affine_select(out=block_, in_=block_, compare_op=ALU.is_ge, fill=0.0, base=0,
                                           pattern=[[0, 2], [1, P]], channel_multiplier=-1).then_inc(triangled.sem, 1)

            with pool.Fori(0, GROUPS1) as g:
                group(g)

        @block.tensor
        def _(pe):
            for s in (rows_scored, max_turned, keyed_scored, weighted, out_turned):
                s.credit(pe)
            pe.wait_ge(ones_rows, 1)

            def stack_at(stack, rows, g, h, at, size):
                return stack[0:rows, bass.ds(slot(g), 1), h, at:at + size].rearrange("k a n -> k (a n)")

            def row_scores(g, s):
                c, r, kc = M_STEPS[s]
                width = CHUNK if kc < c else (r + 1) * P
                for h in range(G):
                    rows_reduced.wait_before(pe, g, 0 - (G * s + h) + 2)
                    pe.matmul(rows_ps[:, h % 2, 0:width], stack_at(q_stack, MAX_ROW, g, h, (R * c + r) * P, P),
                              stack_at(k_stack, MAX_ROW, g, h, kc * CHUNK, width), start=True, stop=True).then_inc(rows_scored.sem, 1)

            def turn_max(g):
                neg_max_ready.wait(pe, g)
                out_turned_free(g)
                stand_alone(pe, pe_passed)
                pe.transpose(misc_ps[0:G * QB, 0:P], neg_max[:], core.ident[:]).then_inc(max_turned.sem, 1)

            def out_turned_free(g):
                out_ready.wait_before(pe, g)

            def key_scores(g, s):
                c, kb = E_STEPS[s]
                off = max(0, kb - R * c) * P
                for hp in range(2):
                    exped.wait_before(pe, g, 2 - (2 * s + hp))
                    for a in range(2):
                        last = pe.matmul(keyed_ps[:, hp, a, off:CHUNK], stack_at(k_stack, STACK, g, 2 * hp + a, kb * P, P),
                                         stack_at(q_stack, STACK, g, 2 * hp + a, c * CHUNK + off, CHUNK - off),
                                         start=True, stop=True)
                    last.then_inc(keyed_scored.sem, 1)

            def weigh(g, s, d):
                c, kb = E_STEPS[s]
                off = max(0, kb - R * c) * P
                exped.wait(pe, g, 2 * s + 2)
                if kb >= R * c:
                    triangled.wait(pe, g, 2 * (R * c + kb - R * c) + 2)
                if kb == 0:
                    out_copied.wait_before(pe, g, 1 - c)
                for h in range(G):
                    last = pe.matmul(out_ps[2 * HD * h:2 * HD * (h + 1), off:CHUNK], v_ones[:, kb, h, :],
                                     probs[:, s % 2, h // 2, h % 2, off:CHUNK], start=(kb == 0), stop=(kb == R * (c + 1) - 1),
                                     tile_position=(0, 2 * HD * h))
                last.then_inc(weighted.sem, 1)

            def turn_out(g, c):
                out_copied.wait(pe, g, c + 1)
                out_ready.wait_before(pe, g, 1 - c)
                if c == 0:
                    split_steps.wait(pe, g)
                for r in range(R):
                    last = pe.transpose(misc_ps[:, r * P:(r + 1) * P], out_t[:, r * P:(r + 1) * P], core.ident[:])
                last.then_inc(out_turned.sem, 1)

            def prologue(g):
                stacks_loaded.wait(pe, 0)
                for s in range(NS):
                    row_scores(0, s)
                turn_max(0)

            def group(g, last):
                v_ones_ready.wait(pe, g)
                max_loaded.wait(pe, g)
                if not last:
                    stacks_loaded.wait(pe, g + 1)
                pending = None
                for s, (c, kb) in enumerate(E_STEPS):
                    key_scores(g, s)
                    if not last:
                        row_scores(g + 1, s)
                    if s > 0:
                        weigh(g, s - 1, None)
                    if pending is not None and kb == 1:
                        turn_out(g, pending)
                        pending = None
                    if kb == R * (c + 1) - 1:
                        pending = c
                weigh(g, NS - 1, None)
                turn_out(g, CHUNKS - 1)
                if not last:
                    turn_max(g + 1)

            passes(pe, prologue, group)

        @block.scalar
        def _(act):
            exped.credit(act), out_copied.credit(act)

            def copy_out(g, c):
                weighted.wait(act, g, sum(R * (x + 1) for x in range(c + 1)))
                out_turned.wait_before(act, g, 1 - c)
                act.activation(out_t[:], out_ps[:], ACT.Copy).then_inc(out_copied.sem, 1)

            def group(g):
                pending = None
                for s, (c, kb) in enumerate(E_STEPS):
                    off = max(0, kb - R * c) * P
                    for hp in range(2):
                        keyed_scored.wait(act, g, 2 * s + hp + 1)
                        if hp == 0:
                            weighted.wait_before(act, g, 2 - s)
                        act.activation(probs[:, s % 2, hp, :, off:CHUNK], keyed_ps[:, hp, :, off:CHUNK],
                                       ACT.Exp).then_inc(exped.sem, 1)
                    if pending is not None:
                        copy_out(g, pending)
                        pending = None
                    if kb == R * (c + 1) - 1:
                        pending = c
                copy_out(g, CHUNKS - 1)

            with act.Fori(0, GROUPS1) as g:
                group(g)

        @block.vector
        def _(dve):
            for s in (rows_reduced, max_ready, neg_max_ready, split_steps, max_split_ready, inv_ready, out_ready):
                s.credit(dve)
            dve.wait_ge(prepared, 5)

            def reduce_rows(g, s):
                c, r, kc = M_STEPS[s]
                for h in range(G):
                    rows_scored.wait(dve, g, G * s + h + 1)
                    if kc == c and r == 0:
                        stand_alone(dve, dve_passed)
                    ps, to = rows_ps[:, h % 2, :], maxima[:, h, R * c + r, :]
                    if kc < c:
                        last = dve.reduce_max(to[:, kc:kc + 1], ps, AX_X)
                    else:
                        if r > 0:
                            dve.reduce_max(to[:, kc:kc + 1], ps[:, 0:r * P], AX_X)
                        last = dve.tensor_tensor_reduce(masked[:, h % 2, :], ps[:, r * P:(r + 1) * P], causal[:], 1.0, NEG,
                                                        ALU.add, ALU.max, to[:, 4:5])
                    last.then_inc(rows_reduced.sem, 1)

            def finish_max(g):
                rows_reduced.wait(dve, g)
                dve.reduce_max(row_max[:], maxima[:].rearrange("p h b s -> p (h b) s"), AX_X).then_inc(max_ready.sem, 1)
                max_ready.wait(dve, g)
                dve.tensor_scalar(neg_max[:], row_max[:], -1.0, None, ALU.mult).then_inc(neg_max_ready.sem, 1)

            def split_max(g):
                max_turned.wait(dve, g)
                max_stored.wait_before(dve, g, 16 - 15)
                turned = misc_ps[0:G * QB, 0:P]
                dve.tensor_copy(max_split[:, 0, :], turned).then_inc(split_steps.sem, 1)
                split_steps.wait(dve, g, 1)
                dve.tensor_tensor(max_rest[:, 0, :], turned, max_split[:, 0, :], ALU.subtract).then_inc(split_steps.sem, 1)
                split_steps.wait(dve, g, 2)
                dve.tensor_copy(max_split[:, 1, :], max_rest[:, 0, :]).then_inc(split_steps.sem, 1)
                split_steps.wait(dve, g, 3)
                dve.tensor_tensor(max_rest[:, 1, :], max_rest[:, 0, :], max_split[:, 1, :], ALU.subtract).then_inc(split_steps.sem, 1)
                split_steps.wait(dve, g, 4)
                dve.tensor_copy(max_split[:, 2, :], max_rest[:, 1, :]).then_inc(max_split_ready.sem, 1)

            def divide(g, c):
                out_turned.wait(dve, g, c + 1)
                turned = misc_ps[:].rearrange("p (r h d) -> p r h d", r=R, h=G)
                dve.reciprocal(inv_sum[:], turned[:, :, :, HD]).then_inc(inv_ready.sem, 1)
                inv_ready.wait(dve, g, c + 1)
                for r in range(R):
                    out = att[:, R * c + r, cols(g, G * HD)].rearrange("p (h d) -> p h d", h=G)
                    last = dve.tensor_tensor(out, turned[:, r, :, 0:HD],
                                             inv_sum[:, r, :].unsqueeze(2).to_broadcast([P, G, HD]), ALU.mult)
                last.then_inc(out_ready.sem, 1)

            def prologue(g):
                for s in range(NS):
                    reduce_rows(0, s)
                finish_max(0)
                split_max(0)

            def group(g, last):
                pending = None
                for s, (c, kb) in enumerate(E_STEPS):
                    if not last:
                        reduce_rows(g + 1, s)
                    if pending is not None and kb == 3:
                        divide(g, pending)
                        pending = None
                    if kb == R * (c + 1) - 1:
                        pending = c
                if not last:
                    finish_max(g + 1)
                divide(g, CHUNKS - 1)
                if not last:
                    split_max(g + 1)

            passes(dve, prologue, group)


def phase_attention_out(nc, core, att, w_out, b_out):
    with ExitStack() as ctx:
        m = Mem(nc, ctx, "out")
        raw = m.sb("raw", [P, KD, D])
        w_hi, w_lo = m.sb("w_hi", [P, KD, D], F32R), m.sb("w_lo", [P, KD, D], F32R)
        bias = m.sb("bias", [P, D])
        att_hi, att_lo = m.sb("att_hi", [P, KD, CHUNK], F32R), m.sb("att_lo", [P, KD, CHUNK], F32R)
        y, y_normed = m.sb("y", [P, R, D]), m.sb("y_normed", [P, R, D])
        post, pre, turn = Stats(m, "post"), Stats(m, "pre"), Turn(m, core)
        att_ps, y_ps = m.ps("att_ps", [P, KD, CHUNK]), m.ps("y_ps", [P, R // 2, 2 * D])
        w_loaded, b_loaded = m.sem("w_loaded"), m.sem("b_loaded")
        att_chunk = m.sb("att_chunk", [P, R, D])
        att_staged, pool_passed = m.sem("att_staged"), m.sem("pool_passed")
        att_turned, att_hi_ready, att_lo_ready = m.sem("att_turned"), m.sem("att_hi_ready"), m.sem("att_lo_ready")
        projected, y_ready, y_read, x_updated = (m.sem(s) for s in ("projected", "y_ready", "y_read", "x_updated"))
        turning = TurnWeights(m, core, lambda u: att_ps[:, u % 2, :])
        units = [([raw[:, j, k * P:(k + 1) * P] for j in range(KD)], w_hi[:, k, :], w_lo[:, k, :], 0) for k in range(KD)]
        block = m.start()

        @block.sync
        def _(sp):
            sp.dma_start(raw[:], w_out.rearrange("(j p) n -> p j n", p=P)).then_inc(w_loaded, 16)
            sp.dma_start(bias[:], b_out.rearrange("(a n) -> a n", a=1).to_broadcast([P, D])).then_inc(b_loaded, 16)

        @block.tensor
        def _(pe):
            turning.pe(pe, units, lambda w: pe.wait_ge(w_loaded, 16))
            pe.wait_ge(turning.lo_ready, len(units))

            def chunk(c):
                reach(pe, att_lo_ready, KD * c)
                for k in range(KD):
                    for r in range(R):
                        last = pe.transpose(att_ps[:, k, r * P:(r + 1) * P], att_chunk[:, r, k * P:(k + 1) * P], core.ident[:])
                    last.then_inc(att_turned, 1)
                pe.wait_ge(att_lo_ready, KD * (c + 1))
                reach(pe, y_ready, c)
                for r in range(R):
                    at = slice(r * P, (r + 1) * P)
                    for k in range(KD):
                        for i, (a, w) in enumerate(((att_hi, w_hi), (att_hi, w_lo), (att_lo, w_hi))):
                            last = pe.matmul(y_ps[:, r // 2, (r % 2) * D:(r % 2 + 1) * D], a[:, k, at], w[:, k, :],
                                             start=(k == 0 and i == 0), stop=(k == KD - 1 and i == 2))
                last.then_inc(projected, 1)
                turn.pe_turn(pe, c)

            def staged(c):
                pe.wait_ge(att_staged, c + 1)
                chunk(c)

            first_then_loop(pe, CHUNKS, staged)

        @block.gpsimd
        def _(pool):
            def chunk(c):
                reach(pool, att_turned, KD * c)
                stand_alone(pool, pool_passed)
                pool.tensor_copy(att_chunk[:], att[:, cols(c, R), :]).then_inc(att_staged, 1)
            first_then_loop(pool, CHUNKS, chunk)

        @block.scalar
        def _(act):
            turning.act(act, units)

            def chunk(c):
                reach(act, projected, c)
                for k in range(KD):
                    act.wait_ge(att_turned, KD * c + k + 1)
                    act.activation(att_hi[:, k, :], att_ps[:, k, :], ACT.Copy).then_inc(att_hi_ready, 1)
                post.act_std(act, c)
                pre.act_std(act, c)
                turn.act_hi(act, c, c)
            first_then_loop(act, CHUNKS, chunk)

        @block.vector
        def _(dve):
            turning.dve(dve, units)
            dve.wait_ge(b_loaded, 16)

            def chunk(c):
                for k in range(KD):
                    dve.wait_ge(att_hi_ready, KD * c + k + 1)
                    dve.tensor_tensor(att_lo[:, k, :], att_ps[:, k, :], att_hi[:, k, :].bitcast(F32),
                                      ALU.subtract).then_inc(att_lo_ready, 1)
                dve.wait_ge(projected, c + 1)
                for r in range(R):
                    last = dve.tensor_tensor(y[:, r, :], y_ps[:, r // 2, (r % 2) * D:(r % 2 + 1) * D], bias[:], ALU.add)
                last.then_inc(y_ready, 1)
                dve.wait_ge(y_ready, c + 1)
                post.dve_variance(dve, lambda r: y[:, r, :], c)
                post.dve_rstd(dve, c)
                post.dve_normalise(dve, lambda r: y_normed[:, r, :], lambda r: y[:, r, :]).then_inc(y_read, 1)
                dve.wait_ge(y_read, c + 1)
                dve.tensor_tensor(core.x_chunk(c), core.x_chunk(c), y_normed[:].rearrange("p a d -> p (a d)"),
                                  ALU.add).then_inc(x_updated, 1)
                dve.wait_ge(x_updated, c + 1)
                pre.dve_variance(dve, core.x_tile(c), c)
                pre.dve_rstd(dve, c)
                pre.dve_normalise(dve, lambda r: turn.xn[:, r, :], core.x_tile(c)).then_inc(turn.xn_ready, 1)
                turn.dve_lo(dve, c, c)

            first_then_loop(dve, CHUNKS, chunk)



def build(nc, x, w_q, w_k, w_v, w_o, betas, w_gate0, w_up0, w_down0, w_qkv, b_qkv, w_out, b_out,
          w_gate1, gate_scale, w_up1, up_scale, w_down1, down_scale, out):
    q_parts = nc.dram_tensor("q_parts", [PARTS, D, T], BF16, kind="Internal").ap()
    k_parts = nc.dram_tensor("k_parts", [PARTS, D, T], BF16, kind="Internal").ap()
    max_parts = nc.dram_tensor("max_parts", [PARTS, G * QB, P], BF16, kind="Internal").ap()
    memory_att = nc.dram_tensor("memory_att", [T, D], F32, kind="Internal").ap()
    with ExitStack() as ctx:
        core = Core(nc, ctx)
        phase_input(nc, core, x)
        phase_memory_attention(nc, core, memory_att, w_q, w_k, w_v, w_o, betas)
        core.hold_x(nc, ctx)
        phase_residual(nc, core, x, memory_att, "res0")
        phase_ffn(nc, core, "ffn0", w_gate0, w_up0, w_down0)
        mixed = ctx.enter_context(nc.sbuf_tensor("mixed", [P, TILES, D], F32))
        with nc.sbuf_tensor("values", [P, TILES, D], F32) as values:
            phase_qkv(nc, core, values, w_qkv, b_qkv, q_parts, k_parts)
            phase_attention(nc, core, mixed, values, q_parts, k_parts, max_parts)
        phase_attention_out(nc, core, mixed, w_out, b_out)
        phase_ffn(nc, core, "ffn1", w_gate1, w_up1, w_down1, scales=(gate_scale, up_scale, down_scale), out=out)


_INS = ["L0_attn_x", "L0_attn_Wq", "L0_attn_Wk", "L0_attn_Wv", "L0_attn_Wo", "L0_attn_betas",
        "L0_ffn_w_gate", "L0_ffn_w_up", "L0_ffn_w_down",
        "L1_attn_w_qkv", "L1_attn_b_qkv", "L1_attn_w_out", "L1_attn_b_out",
        "L1_ffn_gate_w", "L1_ffn_gate_scale", "L1_ffn_up_w", "L1_ffn_up_scale", "L1_ffn_down_w", "L1_ffn_down_scale"]


def kernel(**inputs):
    import numpy as np
    import concourse.bacc as bacc
    from concourse.bass_utils import run_bass_kernel_spmd

    nc = bacc.Bacc("TRN2", target_bir_lowering=False, num_devices=1)
    nc.disable_value_cache = True
    arrays, args = {}, []
    for name in _INS:
        a = np.ascontiguousarray(inputs[name])
        arrays[name] = a
        args.append(nc.dram_tensor(name, a.shape, mybir.dt.from_np(a.dtype), kind="ExternalInput").ap())
    out = nc.dram_tensor("out", (1, T, D), F32, kind="ExternalOutput").ap()
    build(nc, *args, out)
    r = run_bass_kernel_spmd(nc, [arrays], core_ids=[0])
    return r.results[0]["out"]
```

```python
from contextlib import ExitStack

import concourse.bass as bass
from concourse import mybir

F32 = mybir.dt.float32
F32R = mybir.dt.float32r
BF16 = mybir.dt.bfloat16
I32 = mybir.dt.int32
ALU = mybir.AluOpType
ACT = mybir.ActivationFunctionType
AX_X = mybir.AxisListType.X

P = 128
D = 256
KD = D // P
T = 2048
TILES = T // P
CHUNK = 512
R = CHUNK // P
CHUNKS = T // CHUNK
F = 1024
FB = F // P
EPS = 1e-5


def reach(eng, sem, value):
    if isinstance(value, int) and value <= 0:
        return
    eng.wait_ge(sem, value)


def stand_alone(eng, passed):
    eng.sem_inc(passed, 1)


def first_then_loop(eng, count, body):
    body(0)
    with eng.Fori(1, count) as n:
        body(n)


def cols(n, width):
    return bass.ds(n * width, width)


class Mem:
    last_phase = None

    def __init__(self, nc, ctx, phase):
        self.nc, self.ctx, self.phase, self.sems = nc, ctx, phase, []

    def start(self):
        if Mem.last_phase is not None and Mem.last_phase.nc is self.nc:
            self.nc.clear_and_free_semaphores(Mem.last_phase.sems)
        Mem.last_phase = self
        return self.ctx.enter_context(self.nc.Block(no_gpsimd_drain=True))

    def sb(self, name, shape, dt=F32):
        return self.ctx.enter_context(self.nc.sbuf_tensor(f"{self.phase}_{name}", shape, dt))

    def ps(self, name, shape, dt=F32):
        return self.ctx.enter_context(self.nc.psum_tensor(f"{self.phase}_{name}", shape, dt))

    def sem(self, name):
        self.sems.append(self.nc.alloc_semaphore(f"{self.phase}_{name}"))
        return self.sems[-1]


class Stats:

    def __init__(self, m, name):
        self.sums = m.sb(name + "_sums", [P, R, 6])
        self.mean_var = m.sb(name + "_mean_var", [P, R, 2])
        self.var_eps = m.sb(name + "_var_eps", [P, R])
        self.std = m.sb(name + "_std", [P, R])
        self.rstd = m.sb(name + "_rstd", [P, R])
        self.sums_ready = m.sem(name + "_sums_ready")
        self.sums_passed = m.sem(name + "_sums_passed")
        self.mean_ready = m.sem(name + "_mean_ready")
        self.var_ready = m.sem(name + "_var_ready")
        self.std_ready = m.sem(name + "_std_ready")
        self.rstd_ready = m.sem(name + "_rstd_ready")

    def dve_variance(self, dve, tile_of, n):
        for r in range(R):
            last = dve.bn_stats(self.sums[:, r, :], tile_of(r))
        last.then_inc(self.sums_ready, 1)
        dve.wait_ge(self.sums_ready, n + 1)
        stand_alone(dve, self.sums_passed)
        for r in range(R):
            last = dve.bn_aggr(self.mean_var[:, r, :], self.sums[:, r, :])
        last.then_inc(self.mean_ready, 1)
        dve.wait_ge(self.mean_ready, n + 1)
        reach(dve, self.std_ready, n)
        dve.tensor_scalar(self.var_eps[:], self.mean_var[:, :, 1], EPS, None, ALU.add).then_inc(self.var_ready, 1)

    def act_std(self, act, n):
        act.wait_ge(self.var_ready, n + 1)
        reach(act, self.rstd_ready, n)
        act.activation(self.std[:], self.var_eps[:], ACT.Sqrt).then_inc(self.std_ready, 1)

    def dve_rstd(self, dve, n):
        dve.wait_ge(self.std_ready, n + 1)
        dve.reciprocal(self.rstd[:], self.std[:]).then_inc(self.rstd_ready, 1)
        dve.wait_ge(self.rstd_ready, n + 1)

    def dve_normalise(self, dve, out_of, tile_of):
        for r in range(R):
            last = dve.tensor_scalar(out_of(r), tile_of(r), self.mean_var[:, r, 0:1], self.rstd[:, r:r + 1],
                                     ALU.subtract, ALU.mult)
        return last


class Turn:

    def __init__(self, m, core, name="turn"):
        self.core = core
        self.xn = m.sb(name + "_xn", [P, R, D])
        self.turned = m.ps(name + "_turned", [P, KD, CHUNK])
        self.xn_ready = m.sem(name + "_xn_ready")
        self.turned_ready = m.sem(name + "_turned_ready")
        self.hi_ready = m.sem(name + "_hi_ready")
        self.lo_ready = m.sem(name + "_lo_ready")

    def pe_turn(self, pe, n):
        pe.wait_ge(self.xn_ready, n + 1)
        reach(pe, self.lo_ready, KD * n)
        for k in range(KD):
            for r in range(R):
                last = pe.transpose(self.turned[:, k, r * P:(r + 1) * P], self.xn[:, r, k * P:(k + 1) * P],
                                    self.core.ident[:])
            last.then_inc(self.turned_ready, 1)

    def act_hi(self, act, n, c):
        for k in range(KD):
            act.wait_ge(self.turned_ready, KD * n + k + 1)
            act.activation(self.core.xt_hi[:, k, cols(c, CHUNK)], self.turned[:, k, :],
                           ACT.Copy).then_inc(self.hi_ready, 1)

    def dve_lo(self, dve, n, c):
        for k in range(KD):
            dve.wait_ge(self.hi_ready, KD * n + k + 1)
            dve.tensor_tensor(self.core.xt_lo[:, k, cols(c, CHUNK)], self.turned[:, k, :],
                              self.core.xt_hi[:, k, cols(c, CHUNK)].bitcast(F32),
                              ALU.subtract).then_inc(self.lo_ready, 1)


class Core:

    def __init__(self, nc, ctx):
        m = Mem(nc, ctx, "core")
        self.xt_hi = m.sb("xt_hi", [P, KD, T], F32R)
        self.xt_lo = m.sb("xt_lo", [P, KD, T], F32R)
        self.ident = m.sb("ident", [P, P])

    def hold_x(self, nc, ctx):
        self.x = Mem(nc, ctx, "core").sb("x", [P, TILES, D])

    def x_tile(self, c):
        return lambda r: self.x[:, bass.ds(c * R + r, 1), :].rearrange("p a d -> p (a d)")

    def x_chunk(self, c):
        return self.x[:, cols(c, R), :].rearrange("p a d -> p (a d)")


def phase_input(nc, core, x_in):
    with ExitStack() as ctx:
        m = Mem(nc, ctx, "in")
        norm, turn = Stats(m, "norm"), Turn(m, core)
        x = m.sb("x", [P, TILES, D])
        zeroed, ident_ready = m.sem("zeroed"), m.sem("ident_ready")
        x_loaded = [m.sem(f"x_loaded{c}") for c in range(CHUNKS)]
        block = m.start()

        @block.sync
        def _(sp):
            for c in range(CHUNKS):
                sp.dma_start(x[:, c * R:(c + 1) * R, :],
                             x_in[0, c * CHUNK:(c + 1) * CHUNK, :].rearrange("(a p) d -> p a d", p=P)).then_inc(x_loaded[c], 16)

        @block.gpsimd
        def _(pool):
            pool.memset(core.ident[:], 0.0).then_inc(zeroed, 1)
            pool.wait_ge(zeroed, 1)
            pool.affine_select(out=core.ident[:], in_=core.ident[:], compare_op=ALU.not_equal, fill=1.0, base=0,
                               pattern=[[-1, P]], channel_multiplier=1).then_inc(ident_ready, 1)

        @block.vector
        def _(dve):
            def normalise(c):
                x_tile = lambda r: x[:, c * R + r, :]
                dve.wait_ge(x_loaded[c], 16)
                norm.dve_variance(dve, x_tile, c)
                norm.dve_rstd(dve, c)
                reach(dve, turn.turned_ready, KD * c)
                norm.dve_normalise(dve, lambda r: turn.xn[:, r, :], x_tile).then_inc(turn.xn_ready, 1)

            for c in range(CHUNKS):
                normalise(c)
                turn.dve_lo(dve, c, c)

        @block.scalar
        def _(act):
            for c in range(CHUNKS):
                norm.act_std(act, c)
                turn.act_hi(act, c, c)

        @block.tensor
        def _(pe):
            pe.wait_ge(ident_ready, 1)
            for c in range(CHUNKS):
                turn.pe_turn(pe, c)


class TurnWeights:

    def __init__(self, m, core, bank_of):
        self.core, self.bank_of = core, bank_of
        self.turned_ready = m.sem("weights_turned_ready")
        self.hi_ready = m.sem("weights_hi_ready")
        self.lo_ready = m.sem("weights_lo_ready")

    def pe(self, pe, units, source_ready):
        for u, (sources, hi, lo, needs) in enumerate(units):
            source_ready(needs)
            reach(pe, self.lo_ready, u - 1)
            for s, source in enumerate(sources):
                last = pe.transpose(self.bank_of(u)[:, s * P:(s + 1) * P], source, self.core.ident[:])
            last.then_inc(self.turned_ready, 1)

    def act(self, act, units):
        for u, (sources, hi, lo, needs) in enumerate(units):
            act.wait_ge(self.turned_ready, u + 1)
            act.activation(hi, self.bank_of(u)[:, 0:len(sources) * P], ACT.Copy).then_inc(self.hi_ready, 1)

    def dve(self, dve, units):
        for u, (sources, hi, lo, needs) in enumerate(units):
            dve.wait_ge(self.hi_ready, u + 1)
            dve.tensor_tensor(lo, self.bank_of(u)[:, 0:len(sources) * P], hi.bitcast(F32),
                              ALU.subtract).then_inc(self.lo_ready, 1)


def phase_ffn(nc, core, name, w_gate, w_up, w_down, scales=None, out=None):
    ZERO_POINT = 128.0
    with ExitStack() as ctx:
        m = Mem(nc, ctx, name)
        raw_dt = F32 if scales is None else I32
        raw_in = m.sb("raw_in", [P, FB, D], raw_dt)
        raw_in2 = m.sb("raw_in2", [P, FB, D], raw_dt)
        raw_down = m.sb("raw_down", [P, KD, F], raw_dt)
        gate_hi, gate_lo = m.sb("gate_hi", [P, KD, F], F32R), m.sb("gate_lo", [P, KD, F], F32R)
        up_hi, up_lo = m.sb("up_hi", [P, KD, F], F32R), m.sb("up_lo", [P, KD, F], F32R)
        down_hi, down_lo = m.sb("down_hi", [P, FB, D], F32R), m.sb("down_lo", [P, FB, D], F32R)
        silu = m.sb("silu", [P, 2, CHUNK])
        hidden = m.sb("hidden", [P, 2, CHUNK])
        hidden_hi, hidden_lo = m.sb("hidden_hi", [P, 2, CHUNK], F32R), m.sb("hidden_lo", [P, 2, CHUNK], F32R)
        y_normed = m.sb("y_normed", [P, R, D])
        post, pre, turn = Stats(m, "post"), Stats(m, "pre"), Turn(m, core)

        gate_ps = m.ps("gate_ps", [P, 2, CHUNK])
        up_ps = m.ps("up_ps", [P, 2, CHUNK])
        y_ps = m.ps("y_ps", [P, R // 2, 2 * D])

        raw_loaded = [m.sem(f"raw_loaded_{w}") for w in ("gate", "up", "down")]
        scaled = m.sem("weights_scaled")
        scales_loaded = m.sem("scales_loaded")
        gate_up_ready = m.sem("gate_up_ready")
        silu_ready = m.sem("silu_ready")
        hidden_ready = m.sem("hidden_ready")
        hidden_hi_ready = m.sem("hidden_hi_ready")
        hidden_lo_ready = m.sem("hidden_lo_ready")
        down_done = m.sem("down_done")
        y_ready = m.sem("y_ready")
        y_read = m.sem("y_read")
        x_updated = m.sem("x_updated")
        stored = m.sem("stored")
        last_layer = out is not None

        turning = TurnWeights(m, core, lambda u: gate_ps[:, u % 2, :])
        units = []
        if scales is None:
            gate_src, up_src, down_src = raw_in, raw_in2, raw_down
        else:
            gate_src, up_src, down_src = (t[:].bitcast(F32) for t in (raw_in, raw_in2, raw_down))
            scale_sb = m.sb("scale", [P, 2 * FB + KD])
        for w, (src, hi, lo) in enumerate(((gate_src, gate_hi, gate_lo), (up_src, up_hi, up_lo))):
            for k in range(KD):
                for j0 in range(0, FB, 4):
                    units.append(([src[:, j, k * P:(k + 1) * P] for j in range(j0, j0 + 4)],
                                  hi[:, k, j0 * P:(j0 + 4) * P], lo[:, k, j0 * P:(j0 + 4) * P], w))
        for j0 in range(0, FB, 2):
            units.append(([down_src[:, k, j * P:(j + 1) * P] for j in (j0, j0 + 1) for k in range(KD)],
                          down_hi[:, j0:j0 + 2, :].rearrange("p j d -> p (j d)"),
                          down_lo[:, j0:j0 + 2, :].rearrange("p j d -> p (j d)"), 2))
        N_UNITS = len(units)

        block = m.start()

        @block.sync
        def _(sp):
            for src, dst, loaded, rows in ((w_gate, raw_in, 0, FB), (w_up, raw_in2, 1, FB), (w_down, raw_down, 2, KD)):
                sp.dma_start(dst[:], src.rearrange("(j p) n -> p j n", p=P)).then_inc(raw_loaded[loaded], 16)
            if scales is not None:
                with nc.allow_non_contiguous_dma(reason="one scale per partition"):
                    for s, (at, n) in zip(scales, ((0, FB), (FB, FB), (2 * FB, KD))):
                        sp.dma_start(scale_sb[:, at:at + n], s.rearrange("(j p) -> p j", p=P)).then_inc(scales_loaded, 16)
            if last_layer:
                def store(n):
                    sp.wait_ge(x_updated, n + 1)
                    sp.dma_start(out[0, cols(n, CHUNK), :].rearrange("(a p) d -> p a d", p=P),
                                 core.x[:, cols(n, R), :]).then_inc(stored, 16)
                with sp.Fori(0, CHUNKS) as n:
                    store(n)
                sp.wait_ge(stored, 16 * CHUNKS)

        @block.tensor
        def _(pe):
            if scales is None:
                source_ready = lambda w: pe.wait_ge(raw_loaded[w], 16)
            else:
                source_ready = lambda w: pe.wait_ge(scaled, w + 1)
            turning.pe(pe, units, source_ready)
            pe.wait_ge(turning.lo_ready, N_UNITS)

            def gate_up(n, j):
                reach(pe, hidden_ready, FB * n + j - 1)
                for w_hi, w_lo, ps in ((gate_hi, gate_lo, gate_ps), (up_hi, up_lo, up_ps)):
                    for k in range(KD):
                        for i, (w, x) in enumerate(((w_hi, core.xt_hi), (w_hi, core.xt_lo), (w_lo, core.xt_hi))):
                            last = pe.matmul(ps[:, j % 2, :], w[:, k, j * P:(j + 1) * P], x[:, k, cols(n, CHUNK)],
                                             start=(k == 0 and i == 0), stop=(k == KD - 1 and i == 2))
                last.then_inc(gate_up_ready, 1)

            def down(n, j):
                if j == 0:
                    reach(pe, y_read, n)
                pe.wait_ge(hidden_lo_ready, FB * n + j + 1)
                for r in range(R):
                    at = slice(r * P, (r + 1) * P)
                    for i, (h, w) in enumerate(((hidden_hi, down_hi), (hidden_hi, down_lo), (hidden_lo, down_hi))):
                        last = pe.matmul(y_ps[:, r // 2, (r % 2) * D:(r % 2 + 1) * D], h[:, j % 2, at], w[:, j, :],
                                         start=(j == 0 and r % 2 == 0 and i == 0), stop=(j == FB - 1 and i == 2),
                                         skip_group_check=True)
                last.then_inc(down_done, 1)
                if j == FB - 1:
                    pass

            def chunk(n):
                gate_up(n, 0)
                for j in range(1, FB):
                    gate_up(n, j)
                    if j == 4 and not last_layer and not (isinstance(n, int) and n == 0):
                        turn.pe_turn(pe, n - 1)
                    down(n, j - 1)
                down(n, FB - 1)

            first_then_loop(pe, CHUNKS, chunk)
            if not last_layer:
                turn.pe_turn(pe, CHUNKS - 1)

        @block.scalar
        def _(act):
            turning.act(act, units)

            def chunk(n):
                first = isinstance(n, int) and n == 0
                for j in range(FB):
                    if j == 0 and not first:
                        post.act_std(act, n - 1)
                    if j == 1 and not first and not last_layer:
                        pre.act_std(act, n - 1)
                    act.wait_ge(gate_up_ready, FB * n + j + 1)
                    reach(act, hidden_ready, FB * n + j - 1)
                    act.activation(silu[:, j % 2, :], gate_ps[:, j % 2, :], ACT.Silu).then_inc(silu_ready, 1)
                    if j == 4 and not first and not last_layer:
                        turn.act_hi(act, n - 1, n - 1)
                    act.wait_ge(hidden_ready, FB * n + j + 1)
                    reach(act, down_done, FB * n + j - 1)
                    act.activation(hidden_hi[:, j % 2, :], hidden[:, j % 2, :], ACT.Copy).then_inc(hidden_hi_ready, 1)

            first_then_loop(act, CHUNKS, chunk)
            post.act_std(act, CHUNKS - 1)
            if not last_layer:
                pre.act_std(act, CHUNKS - 1)
                turn.act_hi(act, CHUNKS - 1, CHUNKS - 1)

        @block.gpsimd
        def _(pool):
            def chunk(n):
                for j in range(FB):
                    pool.wait_ge(hidden_hi_ready, FB * n + j + 1)
                    pool.tensor_tensor(hidden_lo[:, j % 2, :], hidden[:, j % 2, :], hidden_hi[:, j % 2, :].bitcast(F32),
                                       ALU.subtract).then_inc(hidden_lo_ready, 1)

            with pool.Fori(0, CHUNKS) as n:
                chunk(n)

        @block.vector
        def _(dve):
            if scales is not None:
                dve.wait_ge(scales_loaded, 16 * 3)
                for w, (raw, at, n) in enumerate(((raw_in, 0, FB), (raw_in2, FB, FB), (raw_down, 2 * FB, KD))):
                    dve.wait_ge(raw_loaded[w], 16)
                    for j in range(n):
                        last = dve.tensor_scalar(raw[:, j, :].bitcast(F32), raw[:, j, :], ZERO_POINT,
                                                 scale_sb[:, at + j:at + j + 1], ALU.subtract, ALU.mult)
                    last.then_inc(scaled, 1)
            turning.dve(dve, units)

            y_tile = lambda r: y_ps[:, r // 2, (r % 2) * D:(r % 2 + 1) * D]

            def tail_y_stats(c):
                dve.wait_ge(down_done, FB * (c + 1))
                post.dve_variance(dve, y_tile, c)

            def tail_add(c):
                post.dve_rstd(dve, c)
                post.dve_normalise(dve, lambda r: y_normed[:, r, :], y_tile).then_inc(y_read, 1)
                dve.wait_ge(y_read, c + 1)
                dve.tensor_tensor(core.x_chunk(c), core.x_chunk(c), y_normed[:].rearrange("p a d -> p (a d)"),
                                  ALU.add).then_inc(x_updated, 1)
                dve.wait_ge(x_updated, c + 1)
                if not last_layer:
                    pre.dve_variance(dve, core.x_tile(c), c)

            def tail_xn(c):
                pre.dve_rstd(dve, c)
                pre.dve_normalise(dve, lambda r: turn.xn[:, r, :], core.x_tile(c)).then_inc(turn.xn_ready, 1)

            def chunk(n):
                first = isinstance(n, int) and n == 0
                for j in range(FB):
                    if j == 0 and not first:
                        tail_y_stats(n - 1)
                    dve.wait_ge(silu_ready, FB * n + j + 1)
                    reach(dve, hidden_lo_ready, FB * n + j - 1)
                    dve.tensor_tensor(hidden[:, j % 2, :], silu[:, j % 2, :], up_ps[:, j % 2, :],
                                      ALU.mult).then_inc(hidden_ready, 1)
                    if j == 0 and not first:
                        tail_add(n - 1)
                    if j == 1 and not first and not last_layer:
                        tail_xn(n - 1)
                    if j == 4 and not first and not last_layer:
                        turn.dve_lo(dve, n - 1, n - 1)

            first_then_loop(dve, CHUNKS, chunk)
            tail_y_stats(CHUNKS - 1)
            tail_add(CHUNKS - 1)
            if not last_layer:
                tail_xn(CHUNKS - 1)
                turn.dve_lo(dve, CHUNKS - 1, CHUNKS - 1)

HEADS = 16
DH = 128
SEG = 64
G = 4
GROUPS = HEADS // G
HALF = 2 * P
HALVES = T // HALF
UNITS = 6
PAIRS = T // P
QUADS = PAIRS // 4
STRIPS = SEG // HEADS
CREDIT = 8
NEG = -1e30


class Beat:

    def __init__(self, m, name, per=1):
        self.sem, self.per = m.sem(name), per

    def credit(self, eng):
        eng.sem_inc(self.sem, CREDIT)

    def at(self, n, m=None):
        return n * self.per + (CREDIT + (self.per if m is None else m))

    def wait(self, eng, n, m=None):
        eng.wait_ge(self.sem, self.at(n, m))

    def wait_alone(self, eng, passed, n, m=None):
        self.wait(eng, n, m)
        stand_alone(eng, passed)

    def wait_before(self, eng, n, back=1):
        eng.wait_ge(self.sem, n * self.per + (CREDIT + 1 - back))


def phase_memory_attention(nc, core, y_out, sigmoids, w_q, w_k, w_v, w_o, betas):
    with ExitStack() as ctx:
        m = Mem(nc, ctx, "mem")
        W = G * DH
        raw = [m.sb(f"raw_{n}", [P, KD, W]) for n in "kqv"]
        hi = [m.sb(f"{n}_hi", [P, KD, W], F32R) for n in "kqv"]
        lo = [m.sb(f"{n}_lo", [P, KD, W], F32R) for n in "kqv"]
        o_hi, o_lo = m.sb("o_hi", [P, HEADS, D], F32R), m.sb("o_lo", [P, HEADS, D], F32R)
        beta_heads = m.sb("beta_heads", [HEADS, 2, DH])
        beta, beta_rest = m.sb("beta", [P, W]), m.sb("beta_rest", [P, W])
        mask = m.sb("mask", [P, P])
        keyed_hi = [m.sb(f"keyed_hi{b}", [P, KD, HALF], F32R) for b in range(2)]
        keyed_lo = [m.sb(f"keyed_lo{b}", [P, KD, HALF], F32R) for b in range(2)]
        q_t = [m.sb(f"q_t{b}", [P, G, 2, P]) for b in range(2)]
        k_t = [m.sb(f"k_t{b}", [P, G, 2, P]) for b in range(2)]
        sigma = [m.sb(f"sigma{b}", [P, G, 2, 4 * SEG]) for b in range(2)]
        sigma_kt = [m.sb(f"sigma_kt{b}", [P, G, 2, P]) for b in range(2)]
        v = [m.sb(f"v{b}", [P, 2, W]) for b in range(2)]
        v_rest = [m.sb(f"v_rest{b}", [P, 2, W]) for b in range(2)]
        z_step = [m.sb(f"z_step{b}", [P, G, 2, 2]) for b in range(2)]
        exp_min = m.sb("exp_min", [P, 2, W])
        memory = m.sb("memory", [P, G, DH + 1])
        probs = m.sb("probs", [P, G, P])
        row_max, neg_max = m.sb("row_max", [P, G]), m.sb("neg_max", [P, G])
        row_sum, inv_sum = m.sb("row_sum", [P, G]), m.sb("inv_sum", [P, G])
        probs_t = m.sb("probs_t", [P, G, P])
        sigma_k = m.sb("sigma_k", [P, G, DH])
        inv_den = m.sb("inv_den", [P, 2, 2])
        neg_delta = m.sb("neg_delta", [P, G, DH])
        from_memory, weighted_memory, att = (m.sb(n, [P, W]) for n in ("from_memory", "weighted_memory", "att"))
        att_hi, att_lo = m.sb("att_hi", [P, HEADS, P], F32R), m.sb("att_lo", [P, HEADS, P], F32R)
        y_stage = m.sb("y_stage", [P, D])

        proj_ps = m.ps("proj_ps", [P, 2, W])
        scores_ps = m.ps("scores_ps", [P, G, P])
        out_ps = m.ps("out_ps", [P, W])
        turn_ps = m.ps("turn_ps", [P, G, P])
        read_ps = m.ps("read_ps", [P, 2, 512])
        update_ps = m.ps("update_ps", [P, G, DH])

        w_loaded, betas_loaded = Beat(m, "w_loaded", 48), m.sem("betas_loaded")
        o_loaded, o_hi_ready, o_lo_ready = m.sem("o_loaded"), m.sem("o_hi_ready"), m.sem("o_lo_ready")
        w_hi, w_lo = Beat(m, "w_hi", 3), Beat(m, "w_lo", 3)
        beta_steps, betas_stored = m.sem("beta_steps"), m.sem("betas_stored")
        beta_loaded, beta_rest_loaded = Beat(m, "beta_loaded", 16), Beat(m, "beta_rest_loaded", 16)
        mask_steps = m.sem("mask_steps")
        pool_passed, dve_passed = m.sem("pool_passed"), m.sem("dve_passed")
        memory_reset = m.sem("memory_reset")
        keyed = Beat(m, "keyed")
        projected = Beat(m, "projected", UNITS)
        raw_copied = Beat(m, "raw_copied", 4)
        relued, exped = Beat(m, "relued", 4), Beat(m, "exped", 4)
        sigma_ready, z_ready = Beat(m, "sigma_ready", 4), Beat(m, "z_ready", 2)
        keys_copied = Beat(m, "keys_copied", 2)
        v_ready, v_rest_ready = Beat(m, "v_ready", 2), Beat(m, "v_rest_ready", 2)
        scored = Beat(m, "scored")
        max_ready, neg_ready = Beat(m, "max_ready"), Beat(m, "neg_ready")
        probs_ready, probs_turned, probs_t_ready = Beat(m, "probs_ready"), Beat(m, "probs_turned"), Beat(m, "probs_t_ready")
        sigma_turned, sigma_k_ready = Beat(m, "sigma_turned"), Beat(m, "sigma_k_ready")
        retrieved, den_ready = Beat(m, "retrieved", 2), Beat(m, "den_ready", 2)
        delta_ready, from_memory_ready = Beat(m, "delta_ready", 2), Beat(m, "from_memory_ready", 2)
        memory_weighted = Beat(m, "memory_weighted")
        updated, memory_ready = Beat(m, "updated", 2), Beat(m, "memory_ready", 2)
        attended, inv_sum_ready, att_ready = Beat(m, "attended"), Beat(m, "inv_sum_ready"), Beat(m, "att_ready")
        att_turned, att_hi_ready, att_lo_ready = (Beat(m, n) for n in ("att_turned", "att_hi_ready", "att_lo_ready"))
        y_ready, y_copied, y_stored = Beat(m, "y_ready"), Beat(m, "y_copied"), Beat(m, "y_stored", 16)

        raw_o = [sigma[b][:].rearrange("p h t c -> p (h t c)").rearrange("p (j n) -> p j n", n=D) for b in range(2)]

        KINDS = ("k", "q", "v", "k", "q", "v")
        EVEN, ODD = 0, 1
        Q_ROWS = {EVEN: slice(0, SEG), ODD: slice(SEG, P)}
        K_ROWS = {EVEN: slice(SEG, P), ODD: slice(0, SEG)}
        SIGMA_OF = {EVEN: slice(P, 2 * P), ODD: slice(0, P)}
        ROWS = 2 * G * STRIPS
        LAST_Q, LAST_N = GROUPS * QUADS - 1, GROUPS * PAIRS - 1

        class Pair:

            def __init__(self, g, i, b, p, kind):
                self.g, self.b, self.p, self.slot = g, b, p, 2 * b + p
                self.q = g * QUADS + i
                self.h, self.n = self.q * 2 + b, self.q * 4 + self.slot
                ends = kind in ("switch", "last")
                self.c = i * 2 + b
                self.c1 = 0 if ends and b == 1 else self.c + 1
                self.c2 = b if ends else self.c + 2
                self.first = kind == "first" and self.slot == 0
                self.switch = kind == "switch" and b == 1
                self.has_next_half = not (kind == "last" and b == 1)
                self.has_second_next = kind != "last"
                self.has_next_pair = not (kind == "last" and self.slot == 3)
                self.group_ends = ends and self.slot == 3
                self.next_h, self.next_b = (self.h, b) if p == 0 else (self.h + 1, 1 - b)
                self.quad_before = self.q - 1 if self.slot == 0 else self.q

        def pairs(eng, pair):
            def body(g, i, kind):
                for b in range(2):
                    for p in range(2):
                        pair(Pair(g, i, b, p, kind))
            def middle(g):
                with eng.Fori(1, QUADS - 1) as i:
                    body(g, i, "middle")
            body(0, 0, "first")
            with eng.Fori(0, GROUPS - 1) as g:
                middle(g)
                body(g, QUADS - 1, "switch")
                body(g + 1, 0, "middle")
            middle(GROUPS - 1)
            body(GROUPS - 1, QUADS - 1, "last")

        def turned_rows():
            return turn_ps[:].rearrange("p a b -> p (a b)").rearrange("p (r j) -> p j r", j=HEADS)

        block = m.start()

        @block.sync
        def _(sp):
            for s in (w_loaded, y_stored, beta_loaded, beta_rest_loaded):
                s.credit(sp)

            def load_weights(g):
                for src, dst in zip((w_k, w_q, w_v), raw):
                    sp.dma_start(dst[:], src[:, cols(g, W)].rearrange("(k p) n -> p k n", p=P)).then_inc(w_loaded.sem, 16)

            def load_beta(g, which, dst, loaded):
                sp.dma_start(dst[:], sigmoids[cols(g, G), which, :].rearrange("h (a d) -> a h d", a=1).to_broadcast([P, G, DH])
                             ).then_inc(loaded.sem, 16)

            def store_y(g, i):
                y_copied.wait(sp, g * QUADS + i)
                sp.dma_start(y_out.rearrange("(t r) d -> t r d", r=SEG)[:, bass.ds(g * (G * STRIPS), G * STRIPS), :][cols(i, 8), :, :],
                             y_stage[:]).then_inc(y_stored.sem, 16)

            load_weights(0)
            sp.dma_start(beta_heads[:, 0, :], betas.rearrange("a h b d -> (a h) (b d)")).then_inc(betas_loaded, 16)
            for i in range(2):
                sp.dma_start(raw_o[i], w_o[i * (HEADS // 2) * P:(i + 1) * (HEADS // 2) * P, :].rearrange("(j p) n -> p j n", p=P)
                             ).then_inc(o_loaded, 16)
            sp.wait_ge(beta_steps, 4)
            sp.dma_start(sigmoids, beta_heads[:]).then_inc(betas_stored, 16)
            sp.wait_ge(betas_stored, 16)
            load_beta(0, 1, beta_rest, beta_rest_loaded)
            load_beta(0, 0, beta, beta_loaded)

            with sp.Fori(0, GROUPS - 1) as g:
                w_lo.wait(sp, g)
                load_weights(g + 1)
                with sp.Fori(0, QUADS - 1) as i:
                    store_y(g, i)
                v_rest_ready.wait(sp, g * HALVES + (HALVES - 1))
                load_beta(g + 1, 1, beta_rest, beta_rest_loaded)
                memory_weighted.wait(sp, g * PAIRS + (PAIRS - 1))
                load_beta(g + 1, 0, beta, beta_loaded)
                store_y(g, QUADS - 1)
            with sp.Fori(0, QUADS) as i:
                store_y(GROUPS - 1, i)
            y_stored.wait(sp, LAST_Q)

        @block.gpsimd
        def _(pool):
            for s in (keyed, v_rest_ready, memory_weighted):
                s.credit(pool)

            def key_order(h, c, b, part):
                src, dst = ((core.xt_hi, keyed_hi[b]), (core.xt_lo, keyed_lo[b]))[part]
                s = src[:, :, cols(c, HALF)].rearrange("p k (t s c) -> p k t s c", t=2, s=2)
                d = dst[:].rearrange("p k (t s c) -> p k t s c", t=2, s=2)
                for k in range(KD):
                    for seg in range(2):
                        last = pool.tensor_copy(d[:, k, :, 1 - seg, :], s[:, k, :, seg, :].bitcast(F32))
                if part == 1:
                    last.then_inc(keyed.sem, 1)

            def weigh_values(h, b, p):
                v_ready.wait(pool, h, p + 1)
                pool.tensor_tensor(v_rest[b][:, p, :], v[b][:, p, :], beta_rest[:], ALU.mult).then_inc(v_rest_ready.sem, 1)

            for h in range(2):
                for part in range(2):
                    key_order(h, h, h, part)
            pool.memset(mask[:], 0.0).then_inc(mask_steps, 1)
            pool.wait_ge(mask_steps, 1)
            pool.affine_select(out=mask[:, 0:SEG], in_=mask[:, 0:SEG], compare_op=ALU.is_ge, fill=NEG, base=-SEG,
                               pattern=[[-1, SEG]], channel_multiplier=1).then_inc(mask_steps, 1)
            pool.affine_select(out=mask[:, SEG:P], in_=mask[:, SEG:P], compare_op=ALU.is_ge, fill=NEG, base=0,
                               pattern=[[-1, SEG]], channel_multiplier=1).then_inc(mask_steps, 1)
            pool.wait_ge(mask_steps, 3)
            pool.affine_select(out=mask[:, SEG:P], in_=mask[:, SEG:P], compare_op=ALU.is_ge, fill=NEG, base=SEG - 1,
                               pattern=[[0, SEG]], channel_multiplier=-1).then_inc(mask_steps, 1)
            beta_rest_loaded.wait(pool, 0)
            for p in range(2):
                weigh_values(0, 0, p)

            def pair(x):
                if x.has_second_next:
                    if x.p == 0:
                        projected.wait_alone(pool, pool_passed, x.h)
                    key_order(x.h + 2, x.c2, x.b, x.p)
                from_memory_ready.wait(pool, x.n)
                att_ready.wait_before(pool, x.n)
                if (x.c == 0 if isinstance(x.c, int) else False) and x.slot == 0:
                    beta_loaded.wait(pool, x.g)
                pool.tensor_tensor(weighted_memory[:], from_memory[:], beta[:], ALU.mult).then_inc(memory_weighted.sem, 1)
                if x.has_next_half:
                    if x.switch and x.p == 0:
                        beta_rest_loaded.wait(pool, x.g + 1)
                    weigh_values(x.h + 1, 1 - x.b, x.p)

            pairs(pool, pair)

        @block.tensor
        def _(pe):
            for s in (projected, scored, retrieved, updated, sigma_turned, probs_turned, att_turned, attended, y_ready):
                s.credit(pe)

            def unit(h, c, b, u):
                bank = proj_ps[:, u % 2, :]
                if u == 0:
                    keyed.wait(pe, h)
                before = (u - 2) % UNITS
                turn = h if u >= 2 else h - 1
                if KINDS[before] == "v":
                    v_ready.wait(pe, turn, before // 3 + 1)
                else:
                    sigma_ready.wait(pe, turn, 2 * (before // 3) + before % 3 + 1)
                kind, half = KINDS[u], u // 3
                w_h, w_l = hi["kqv".index(kind)], lo["kqv".index(kind)]
                if kind == "v":
                    at = slice(half * P, (half + 1) * P)
                    for k in range(KD):
                        for i, (x, w) in enumerate(((keyed_hi, w_h), (keyed_hi, w_l), (keyed_lo, w_h))):
                            last = pe.matmul(bank, x[b][:, k, at], w[:, k, :], start=(k == 0 and i == 0),
                                             stop=(k == KD - 1 and i == 2))
                else:
                    if kind == "k":
                        x_h, x_l = (lambda k: keyed_hi[b][:, k, :]), (lambda k: keyed_lo[b][:, k, :])
                    else:
                        x_h = lambda k: core.xt_hi[:, k, cols(c, HALF)]
                        x_l = lambda k: core.xt_lo[:, k, cols(c, HALF)]
                    for a in range(2):
                        head = slice((2 * half + a) * DH, (2 * half + a + 1) * DH)
                        for k in range(KD):
                            for i, (w, x) in enumerate(((w_h, x_h), (w_h, x_l), (w_l, x_h))):
                                last = pe.matmul(bank[:, a * HALF:(a + 1) * HALF], w[:, k, head], x(k),
                                                 start=(k == 0 and i == 0), stop=(k == KD - 1 and i == 2))
                last.then_inc(projected.sem, 1)

            def score(n, h, b, p):
                if p == 0:
                    raw_copied.wait(pe, h)
                max_ready.wait_before(pe, n)
                for hh in range(G):
                    mm = pe.matmul(scores_ps[:, hh, :], q_t[b][:, hh, p, :], k_t[b][:, hh, p, :], start=True, stop=True)
                mm.then_inc(scored.sem, 1)

            def turn_sigma(n, h, b, p):
                if p == 0:
                    keys_copied.wait(pe, h)
                probs_t_ready.wait_before(pe, n)
                for hh in range(G):
                    mm = pe.transpose(turn_ps[:, hh, :], sigma_kt[b][:, hh, p, :], core.ident[:])
                mm.then_inc(sigma_turned.sem, 1)

            def retrieve(x, seg):
                if seg == EVEN:
                    memory_ready.wait_before(pe, x.n)
                    from_memory_ready.wait_before(pe, x.n)
                else:
                    memory_ready.wait(pe, x.n, 1)
                    from_memory_ready.wait(pe, x.n, 1)
                for h in range(G):
                    last = pe.matmul(read_ps[:, h // 2, (h % 2) * (DH + 1):(h % 2 + 1) * (DH + 1)],
                                     sigma[x.b][:, h, x.p, SIGMA_OF[seg]], memory[:, h, :], start=True, stop=True)
                last.then_inc(retrieved.sem, 1)

            def update(n, seg):
                if seg == EVEN:
                    sigma_k_ready.wait(pe, n)
                delta_ready.wait(pe, n, seg + 1)
                rows = K_ROWS[seg]
                for h in range(G):
                    last = pe.matmul(update_ps[:, h, :], sigma_k[rows, h, :], neg_delta[rows, h, :], start=True, stop=True)
                last.then_inc(updated.sem, 1)

            def turn_att(n):
                att_ready.wait(pe, n)
                for h in range(G):
                    out = turn_ps[:].rearrange("p a b -> p (a b)").rearrange("p (s h c) -> p h s c", s=2, h=G)[:, h, :, :]
                    last = pe.transpose(out, att[:, h * DH:(h + 1) * DH], core.ident[:])
                last.then_inc(att_turned.sem, 1)

            def project_out(q, js):
                if js.start == 0:
                    att_lo_ready.wait(pe, q * 4 + 3)
                for j in js:
                    for i, (a, w) in enumerate(((att_hi, o_hi), (att_hi, o_lo), (att_lo, o_hi))):
                        last = pe.matmul(out_ps[:, 0:D], a[:, j, :], w[:, j, :], start=(j == 0 and i == 0),
                                         stop=(j == HEADS - 1 and i == 2))
                if js.stop == HEADS:
                    last.then_inc(y_ready.sem, 1)

            w_lo.wait(pe, 0)
            for u in range(UNITS):
                unit(0, 0, 0, u)
            score(0, 0, 0, 0)
            turn_sigma(0, 0, 0, 0)
            pe.wait_ge(memory_reset, 1)

            def pair(x):
                def next_unit(u):
                    if x.has_next_half:
                        if x.switch and x.p == 0:
                            w_lo.wait(pe, x.g + 1, u + 1)
                        unit(x.h + 1, x.c1, 1 - x.b, 3 * x.p + u)

                project = x.slot == 0 and not x.first
                if x.p == 0:
                    sigma_ready.wait(pe, x.h)
                retrieve(x, EVEN)
                next_unit(0)
                if not x.first:
                    sigma_k_ready.wait(pe, x.n)
                    turn_att(x.n - 1)
                update(x.n, EVEN)
                next_unit(1)
                retrieve(x, ODD)
                if project:
                    project_out(x.q - 1, range(0, HEADS // 2))
                probs_ready.wait(pe, x.n)
                att_lo_ready.wait_before(pe, x.n)
                sigma_k_ready.wait(pe, x.n)
                for hh in range(G):
                    mm = pe.transpose(turn_ps[:, hh, :], probs[:, hh, :], core.ident[:])
                mm.then_inc(probs_turned.sem, 1)
                if project:
                    project_out(x.q - 1, range(HEADS // 2, HEADS))
                next_unit(2)
                if x.has_next_pair:
                    score(x.n + 1, x.next_h, x.next_b, 1 - x.p)
                update(x.n, ODD)
                if x.has_next_pair:
                    turn_sigma(x.n + 1, x.next_h, x.next_b, 1 - x.p)
                probs_t_ready.wait(pe, x.n)
                if x.p == 0:
                    v_rest_ready.wait(pe, x.h)
                if x.slot == 0:
                    y_copied.wait_before(pe, x.q)
                for hh in range(G):
                    head = slice(hh * DH, (hh + 1) * DH)
                    mm = pe.matmul(out_ps[:, head], probs_t[:, hh, :], v_rest[x.b][:, x.p, head], start=True, stop=True)
                mm.then_inc(attended.sem, 1)

            pairs(pe, pair)
            turn_att(LAST_N)
            project_out(LAST_Q, range(0, HEADS))

        @block.scalar
        def _(act):
            for s in (y_copied, w_hi, raw_copied, relued, exped, v_ready, probs_ready, probs_t_ready, sigma_k_ready,
                      att_hi_ready, from_memory_ready):
                s.credit(act)

            def split_weights(g, i):
                if i == 0:
                    w_loaded.wait(act, g)
                act.activation(hi[i][:], raw[i][:], ACT.Copy).then_inc(w_hi.sem, 1)

            def unit(h, b, u):
                projected.wait(act, h, u + 1)
                bank = proj_ps[:, u % 2, :]
                kind, half = KINDS[u], u // 3
                if kind == "v":
                    act.activation(v[b][:, half, :], bank, ACT.Copy).then_inc(v_ready.sem, 1)
                    return
                s = 2 * half + u % 3
                dst = (k_t if kind == "k" else q_t)[b]
                act.activation(dst[:, 2 * half:2 * half + 2, :, :].rearrange("p h t c -> p (h t c)"), bank,
                               ACT.Copy).then_inc(raw_copied.sem, 1)
                sigma_ready.wait(act, h if s >= 2 else h - 1, (s - 2) % 4 + 1)
                act.activation(exp_min[:, s % 2, :], bank, ACT.Relu, scale=-1.0).then_inc(relued.sem, 1)
                relued.wait(act, h, s + 1)
                act.activation(exp_min[:, s % 2, :], exp_min[:, s % 2, :], ACT.Exp, scale=-1.0).then_inc(exped.sem, 1)

            def retrieval(n, seg):
                den_ready.wait(act, n, seg + 1)
                if seg == EVEN:
                    memory_weighted.wait_before(act, n)
                rows = Q_ROWS[seg]
                for h in range(G):
                    at = (h % 2) * (DH + 1)
                    last = act.activation(from_memory[rows, h * DH:(h + 1) * DH], read_ps[rows, h // 2, at:at + DH], ACT.Copy,
                                          scale=inv_den[rows, h // 2, h % 2:h % 2 + 1])
                last.then_inc(from_memory_ready.sem, 1)

            def att_part(n, q, slot):
                if slot == 0:
                    y_ready.wait_before(act, q)
                att_turned.wait(act, n)
                act.activation(att_hi[:, :, slot * ROWS:(slot + 1) * ROWS], turned_rows(),
                               ACT.Copy).then_inc(att_hi_ready.sem, 1)

            def copy_y(q):
                y_ready.wait(act, q)
                y_stored.wait_before(act, q)
                act.activation(y_stage[:], out_ps[:, 0:D], ACT.Copy).then_inc(y_copied.sem, 1)

            for i in range(3):
                split_weights(0, i)
            act.wait_ge(betas_loaded, 16)
            act.activation(beta_heads[:, 0, :], beta_heads[:, 0, :], ACT.Exp, scale=-1.0).then_inc(beta_steps, 1)
            act.wait_ge(o_loaded, 32)
            for i in range(2):
                act.activation(o_hi[:, i * (HEADS // 2):(i + 1) * (HEADS // 2), :], raw_o[i], ACT.Copy).then_inc(o_hi_ready, 1)
            for u in range(UNITS):
                unit(0, 0, u)

            def pair(x):
                def next_unit(u):
                    if x.has_next_half:
                        unit(x.h + 1, 1 - x.b, 3 * x.p + u)

                if x.switch and x.p == 0:
                    projected.wait(act, x.h)
                    split_weights(x.g + 1, 0)
                sigma_turned.wait(act, x.n)
                act.activation(sigma_k[:], turn_ps[:], ACT.Copy).then_inc(sigma_k_ready.sem, 1)
                neg_ready.wait(act, x.n)
                for hh in range(G):
                    e = act.activation(probs[:, hh, :], probs[:, hh, :], ACT.Exp, bias=neg_max[:, hh:hh + 1],
                                       accum_out=row_sum[:, hh:hh + 1])
                e.then_inc(probs_ready.sem, 1)
                retrieval(x.n, EVEN)
                if x.switch and x.p == 0:
                    split_weights(x.g + 1, 1)
                next_unit(0)
                if not x.first:
                    att_part(x.n - 1, x.quad_before, (x.slot - 1) % 4)
                if x.switch and x.p == 0:
                    split_weights(x.g + 1, 2)
                next_unit(1)
                retrieval(x.n, ODD)
                probs_turned.wait(act, x.n)
                act.activation(probs_t[:], turn_ps[:], ACT.Copy).then_inc(probs_t_ready.sem, 1)
                if x.slot == 0 and not x.first:
                    copy_y(x.q - 1)
                next_unit(2)

            pairs(act, pair)
            att_part(LAST_N, LAST_Q, 3)
            copy_y(LAST_Q)

        @block.vector
        def _(dve):
            for s in (w_lo, sigma_ready, z_ready, keys_copied, max_ready, neg_ready, den_ready, delta_ready,
                      memory_ready, inv_sum_ready, att_ready, att_lo_ready):
                s.credit(dve)

            def split_weights(g, i):
                w_hi.wait(dve, g, i + 1)
                dve.tensor_tensor(lo[i][:], raw[i][:], hi[i][:].bitcast(F32), ALU.subtract).then_inc(w_lo.sem, 1)

            def unit(h, b, u):
                kind, half = KINDS[u], u // 3
                if kind == "v":
                    return
                s = 2 * half + u % 3
                exped.wait(dve, h, s + 1)
                heads = slice(2 * half, 2 * half + 2)
                x = proj_ps[:, u % 2, :].rearrange("p (ht s c) -> p ht s c", s=2, c=SEG)
                e = exp_min[:, s % 2, :].rearrange("p (ht s c) -> p ht s c", s=2, c=SEG)
                out = sigma[b][:, heads, :, :].rearrange("p h t (s c) -> p (h t) s c", c=SEG)
                for seg in (EVEN, ODD):
                    to = 3 * seg if kind == "k" else 2 - seg
                    last = dve.scalar_tensor_tensor(out=out[:, :, to, :], in0=x[:, :, seg, :], scalar=0.0,
                                                    in1=e[:, :, seg, :], op0=ALU.max, op1=ALU.add)
                last.then_inc(sigma_ready.sem, 1)
                if kind == "k":
                    keys = out[:, :, 0:4:3, :]
                    sigma_ready.wait(dve, h, s + 1)
                    dve.tensor_copy(sigma_kt[b][:, heads, :, :].rearrange("p h t (s c) -> p (h t) s c", c=SEG),
                                    keys).then_inc(keys_copied.sem, 1)
                    dve.reduce_sum(z_step[b][:, heads, :, :].rearrange("p h t s -> p (h t) s"), keys,
                                   AX_X).then_inc(z_ready.sem, 1)

            def retrieval(x, seg):
                retrieved.wait(dve, x.n, seg + 1)
                dve.reciprocal(inv_den[:], read_ps[:, :, DH:2 * (DH + 1):DH + 1]).then_inc(den_ready.sem, 1)
                den_ready.wait(dve, x.n, seg + 1)
                rows = K_ROWS[seg]
                for h in range(G):
                    at = (h % 2) * (DH + 1)
                    last = dve.scalar_tensor_tensor(out=neg_delta[rows, h, :], in0=read_ps[rows, h // 2, at:at + DH],
                                                    scalar=inv_den[rows, h // 2, h % 2:h % 2 + 1],
                                                    in1=v[x.b][rows, x.p, h * DH:(h + 1) * DH], op0=ALU.mult, op1=ALU.subtract)
                last.then_inc(delta_ready.sem, 1)

            def reset_memory():
                dve.memset(memory[:, :, 0:DH], 0.0)
                return dve.memset(memory[:, :, DH], 1.0 / DH)

            def update(x, seg):
                updated.wait(dve, x.n, seg + 1)
                if seg == ODD and x.group_ends:
                    reset_memory().then_inc(memory_ready.sem, 1)
                else:
                    dve.tensor_tensor(memory[:, :, 0:DH], memory[:, :, 0:DH], update_ps[:], ALU.subtract)
                    z = memory[:, :, DH]
                    dve.tensor_tensor(z, z, z_step[x.b][:, :, x.p, 1 - seg], ALU.add).then_inc(memory_ready.sem, 1)

            def score_max(n):
                scored.wait_alone(dve, dve_passed, n)
                for hh in range(G):
                    t = dve.tensor_tensor_reduce(probs[:, hh, :], scores_ps[:, hh, :], mask[:], DH ** -0.5, NEG,
                                                 ALU.add, ALU.max, row_max[:, hh:hh + 1])
                t.then_inc(max_ready.sem, 1)
                max_ready.wait(dve, n)
                dve.tensor_scalar(neg_max[:], row_max[:], -1.0, None, ALU.mult).then_inc(neg_ready.sem, 1)

            def mix(n):
                inv_sum_ready.wait(dve, n)
                attended.wait(dve, n)
                memory_weighted.wait(dve, n)
                for hh in range(G):
                    head = slice(hh * DH, (hh + 1) * DH)
                    t = dve.scalar_tensor_tensor(out=att[:, head], in0=out_ps[:, head], scalar=inv_sum[:, hh:hh + 1],
                                                 in1=weighted_memory[:, head], op0=ALU.mult, op1=ALU.add)
                t.then_inc(att_ready.sem, 1)

            def att_part(n, slot):
                att_hi_ready.wait(dve, n)
                columns = slice(slot * ROWS, (slot + 1) * ROWS)
                dve.tensor_tensor(att_lo[:, :, columns], turned_rows(), att_hi[:, :, columns].bitcast(F32),
                                  ALU.subtract).then_inc(att_lo_ready.sem, 1)

            reset_memory().then_inc(memory_reset, 1)
            for i in range(3):
                split_weights(0, i)
            dve.wait_ge(beta_steps, 1)
            dve.tensor_scalar(beta_heads[:, 0, :], beta_heads[:, 0, :], 1.0, None, ALU.add).then_inc(beta_steps, 1)
            dve.wait_ge(beta_steps, 2)
            dve.reciprocal(beta_heads[:, 0, :], beta_heads[:, 0, :]).then_inc(beta_steps, 1)
            dve.wait_ge(beta_steps, 3)
            dve.tensor_scalar(beta_heads[:, 1, :], beta_heads[:, 0, :], -1.0, 1.0, ALU.mult, ALU.add).then_inc(beta_steps, 1)
            for i in range(2):
                dve.wait_ge(o_hi_ready, i + 1)
                part = slice(i * (HEADS // 2), (i + 1) * (HEADS // 2))
                dve.tensor_tensor(o_lo[:, part, :], raw_o[i], o_hi[:, part, :].bitcast(F32), ALU.subtract).then_inc(o_lo_ready, 1)
            dve.wait_ge(o_lo_ready, 2)
            dve.wait_ge(mask_steps, 4)
            for u in range(UNITS):
                unit(0, 0, u)
            score_max(0)

            def pair(x):
                def next_unit(u):
                    if x.has_next_half:
                        unit(x.h + 1, 1 - x.b, 3 * x.p + u)

                def next_weights(i):
                    if x.switch and x.p == 0:
                        split_weights(x.g + 1, i)

                if not x.first:
                    mix(x.n - 1)
                next_weights(0)
                retrieval(x, EVEN)
                next_weights(1)
                update(x, EVEN)
                if not x.first:
                    att_part(x.n - 1, (x.slot - 1) % 4)
                next_unit(0)
                next_weights(2)
                retrieval(x, ODD)
                next_unit(1)
                probs_ready.wait(dve, x.n)
                dve.reciprocal(inv_sum[:], row_sum[:]).then_inc(inv_sum_ready.sem, 1)
                if x.has_next_pair:
                    score_max(x.n + 1)
                update(x, ODD)

            pairs(dve, pair)
            mix(LAST_N)
            att_part(LAST_N, 3)

def phase_residual(nc, core, x_in, y_in, name):
    with ExitStack() as ctx:
        m = Mem(nc, ctx, name)
        post, pre, turn = Stats(m, "post"), Stats(m, "pre"), Turn(m, core)
        y, y_normed = m.sb("y", [P, TILES, D]), m.sb("y_normed", [P, R, D])
        loaded = [m.sem(f"loaded{c}") for c in range(CHUNKS)]
        y_read, x_updated = m.sem("y_read"), m.sem("x_updated")
        block = m.start()

        @block.sync
        def _(sp):
            for c in range(CHUNKS):
                for src, dst in ((y_in, y), (x_in[0], core.x)):
                    sp.dma_start(dst[:, c * R:(c + 1) * R, :],
                                 src[c * CHUNK:(c + 1) * CHUNK, :].rearrange("(a p) d -> p a d", p=P)).then_inc(loaded[c], 16)

        @block.vector
        def _(dve):
            def chunk(c):
                y_tile = lambda r: y[:, c * R + r, :]
                dve.wait_ge(loaded[c], 32)
                post.dve_variance(dve, y_tile, c)
                post.dve_rstd(dve, c)
                post.dve_normalise(dve, lambda r: y_normed[:, r, :], y_tile).then_inc(y_read, 1)
                dve.wait_ge(y_read, c + 1)
                dve.tensor_tensor(core.x_chunk(c), core.x_chunk(c), y_normed[:].rearrange("p a d -> p (a d)"),
                                  ALU.add).then_inc(x_updated, 1)
                dve.wait_ge(x_updated, c + 1)
                pre.dve_variance(dve, core.x_tile(c), c)
                pre.dve_rstd(dve, c)
                reach(dve, turn.turned_ready, KD * c)
                pre.dve_normalise(dve, lambda r: turn.xn[:, r, :], core.x_tile(c)).then_inc(turn.xn_ready, 1)
                turn.dve_lo(dve, c, c)

            for c in range(CHUNKS):
                chunk(c)

        @block.scalar
        def _(act):
            for c in range(CHUNKS):
                post.act_std(act, c)
                pre.act_std(act, c)
                turn.act_hi(act, c, c)

        @block.tensor
        def _(pe):
            for c in range(CHUNKS):
                turn.pe_turn(pe, c)



H1 = 16
HD = 16
QB = (T // P)
TERMS = ((0, 0), (0, 1), (1, 0), (0, 2), (2, 0), (1, 1))
MAX_ROW = HD * len(TERMS)
STACK = MAX_ROW + 3
PARTS = 3


def phase_qkv(nc, core, values, w_qkv, b_qkv, q_parts, k_parts):
    NB = 3 * D // P
    QK = 4
    with ExitStack() as ctx:
        m = Mem(nc, ctx, "qkv")
        raw = m.sb("raw", [P, NB, D])
        w_hi, w_lo = m.sb("w_hi", [P, KD, NB * P], F32R), m.sb("w_lo", [P, KD, NB * P], F32R)
        bias = m.sb("bias", [P, NB])
        biased = m.sb("biased", [P, NB, CHUNK])
        rest = m.sb("rest", [P, QK, CHUNK])
        parts = m.sb("parts", [P, QK, PARTS, CHUNK], BF16)
        qkv_ps = m.ps("qkv_ps", [P, NB, CHUNK])
        v_ps = m.ps("v_ps", [P, 2, CHUNK])

        raw_loaded, bias_loaded = m.sem("raw_loaded"), m.sem("bias_loaded")
        projected, biased_ready = m.sem("projected"), m.sem("biased_ready")
        part0_ready, rest_ready, part1_ready, part2_ready = (m.sem(s) for s in ("part0_ready", "rest_ready", "part1_ready", "part2_ready"))
        stored = [m.sem(f"stored{j}") for j in range(QK)]
        v_turned, v_copied = m.sem("v_turned"), m.sem("v_copied")
        turning = TurnWeights(m, core, lambda u: v_ps[:, u % 2, :])
        units = [([raw[:, j, k * P:(k + 1) * P] for j in range(j0, j0 + 3)], w_hi[:, k, j0 * P:(j0 + 3) * P],
                  w_lo[:, k, j0 * P:(j0 + 3) * P], 0) for k in range(KD) for j0 in (0, 3)]
        block = m.start()

        @block.sync
        def _(sp):
            sp.dma_start(raw[:], w_qkv.rearrange("(j p) n -> p j n", p=P)).then_inc(raw_loaded, 16)
            with nc.allow_non_contiguous_dma(reason="one bias per partition"):
                sp.dma_start(bias[:], b_qkv.rearrange("(j p) -> p j", p=P)).then_inc(bias_loaded, 16)
            with sp.Fori(0, CHUNKS) as n:
                for j in range(QK):
                    sp.wait_ge(part2_ready, QK * n + j + 1)
                    dst = (q_parts, q_parts, k_parts, k_parts)[j]
                    rows = slice((j % 2) * P, (j % 2 + 1) * P)
                    sp.dma_start(dst[:, rows, cols(n, CHUNK)].rearrange("a p n -> p a n"), parts[:, j, :, :]).then_inc(stored[j], 16)
            for j in range(QK):
                sp.wait_ge(stored[j], 16 * CHUNKS)

        @block.tensor
        def _(pe):
            turning.pe(pe, units, lambda w: pe.wait_ge(raw_loaded, 16))
            pe.wait_ge(turning.lo_ready, len(units))

            def turn_values(n, j):
                pe.wait_ge(biased_ready, NB * n + j + 1)
                reach(pe, v_copied, 2 * n + (j - QK) - 1)
                for r in range(R):
                    last = pe.transpose(v_ps[:, j - QK, r * P:(r + 1) * P], biased[:, j, r * P:(r + 1) * P], core.ident[:])
                last.then_inc(v_turned, 1)

            def chunk(n):
                for j in range(NB):
                    reach(pe, biased_ready, NB * n + j + 1 - NB)
                    for k in range(KD):
                        for i, (w, x) in enumerate(((w_hi, core.xt_hi), (w_hi, core.xt_lo), (w_lo, core.xt_hi))):
                            last = pe.matmul(qkv_ps[:, j, :], w[:, k, j * P:(j + 1) * P], x[:, k, cols(n, CHUNK)],
                                             start=(k == 0 and i == 0), stop=(k == KD - 1 and i == 2))
                    last.then_inc(projected, 1)
                for j in range(QK, NB):
                    turn_values(n, j)

            first_then_loop(pe, CHUNKS, chunk)

        @block.vector
        def _(dve):
            turning.dve(dve, units)
            dve.wait_ge(bias_loaded, 16)

            def chunk(n):
                for s in range(NB + 2):
                    if s < NB:
                        dve.wait_ge(projected, NB * n + s + 1)
                        if s < QK:
                            reach(dve, rest_ready, QK * n + s + 1 - QK)
                        else:
                            reach(dve, v_turned, 2 * n + (s - QK) + 1 - 2)
                        dve.tensor_scalar(biased[:, s, :], qkv_ps[:, s, :], bias[:, s:s + 1],
                                          HD ** -0.5 if s < 2 else 1.0, ALU.add, ALU.mult).then_inc(biased_ready, 1)
                    if 0 <= s - 1 < QK:
                        j = s - 1
                        dve.wait_ge(part0_ready, QK * n + j + 1)
                        dve.tensor_tensor(rest[:, j, :], biased[:, j, :], parts[:, j, 0, :], ALU.subtract).then_inc(rest_ready, 1)
                    if 0 <= s - 2 < QK:
                        j = s - 2
                        dve.wait_ge(part1_ready, QK * n + j + 1)
                        dve.tensor_tensor(parts[:, j, 2, :], rest[:, j, :], parts[:, j, 1, :], ALU.subtract).then_inc(part2_ready, 1)

            first_then_loop(dve, CHUNKS, chunk)

        @block.scalar
        def _(act):
            turning.act(act, units)

            def chunk(n):
                for s in range(QK + 1):
                    if s < QK:
                        act.wait_ge(biased_ready, NB * n + s + 1)
                        reach(act, stored[s], 16 * n)
                        act.activation(parts[:, s, 0, :], biased[:, s, :], ACT.Copy).then_inc(part0_ready, 1)
                    if s > 0:
                        j = s - 1
                        act.wait_ge(rest_ready, QK * n + j + 1)
                        act.activation(parts[:, j, 1, :], rest[:, j, :], ACT.Copy).then_inc(part1_ready, 1)
                for j in range(2):
                    act.wait_ge(v_turned, 2 * n + j + 1)
                    act.activation(values[:, cols(n, R), j * P:(j + 1) * P], v_ps[:, j, :].rearrange("p (a d) -> p a d", a=R),
                                   ACT.Copy).then_inc(v_copied, 1)

            first_then_loop(act, CHUNKS, chunk)


def phase_attention(nc, core, att, values, q_parts, k_parts, max_parts):
    GROUPS1 = H1 // G
    with ExitStack() as ctx:
        m = Mem(nc, ctx, "att")
        q_stack = m.sb("q_stack", [P, 2, G, T], BF16)
        k_stack = m.sb("k_stack", [P, 2, G, T], BF16)
        v_ones = m.sb("v_ones", [P, QB, G, 2 * HD])
        probs = m.sb("probs", [P, 2, 2, 2, CHUNK])
        causal = m.sb("causal", [P, P])
        masked = m.sb("masked", [P, 2, P])
        maxima = m.sb("maxima", [P, G, QB, 5])
        neg_max, row_max = m.sb("neg_max", [P, G * QB]), m.sb("row_max", [P, G * QB])
        max_rest = m.sb("max_rest", [G * QB, 2, P])
        max_split = m.sb("max_split", [G * QB, PARTS, P], BF16)
        out_t = m.sb("out_t", [P, CHUNK])
        inv_sum = m.sb("inv_sum", [P, R, G])

        keyed_ps = m.ps("keyed_ps", [P, 2, 2, CHUNK])
        rows_ps = m.ps("rows_ps", [P, 2, CHUNK])
        out_ps = m.ps("out_ps", [P, CHUNK])
        misc_ps = m.ps("misc_ps", [P, CHUNK])

        E_STEPS = [(c, kb) for c in range(CHUNKS) for kb in range(R * (c + 1))]
        M_STEPS = [(c, r, kc) for c in range(CHUNKS) for r in range(R) for kc in range(c + 1)]
        NS = len(E_STEPS)
        N_DIAGONAL = CHUNKS * R
        assert len(M_STEPS) == NS

        stacks_loaded = Beat(m, "stacks_loaded", 16 * 2 * len(TERMS))
        max_loaded = Beat(m, "max_loaded", 16)
        max_stored = Beat(m, "max_stored", 16)
        v_ones_ready = Beat(m, "v_ones_ready")
        rows_scored, rows_reduced = Beat(m, "rows_scored", NS * G), Beat(m, "rows_reduced", NS * G)
        max_ready, neg_max_ready, max_turned = Beat(m, "max_ready"), Beat(m, "neg_max_ready"), Beat(m, "max_turned")
        split_steps, max_split_ready = Beat(m, "split_steps", 4), Beat(m, "max_split_ready")
        keyed_scored, exped = Beat(m, "keyed_scored", NS * 2), Beat(m, "exped", NS * 2)
        triangled = Beat(m, "triangled", N_DIAGONAL * 2)
        weighted = Beat(m, "weighted", NS)
        out_copied, out_turned, inv_ready, out_ready = (Beat(m, s, CHUNKS) for s in ("out_copied", "out_turned", "inv_ready", "out_ready"))
        prepared, ones_rows = m.sem("prepared"), m.sem("ones_rows")
        pool_passed, dve_passed, pe_passed = m.sem("pool_passed"), m.sem("dve_passed"), m.sem("pe_passed")
        slot = lambda g: g % 2
        block = m.start()

        def passes(eng, prologue, group):
            prologue(0)
            with eng.Fori(0, GROUPS1 - 1) as g:
                group(g, False)
            group(GROUPS1 - 1, True)

        @block.sync
        def _(sp):
            stacks_loaded.credit(sp), max_loaded.credit(sp), max_stored.credit(sp)

            def load_stacks(g):
                if not (isinstance(g, int) and g == 0):
                    weighted.wait_before(sp, g - 1)
                for stack, src, which in ((q_stack, q_parts, 0), (k_stack, k_parts, 1)):
                    for t, term in enumerate(TERMS):
                        rows = src[term[which], cols(g, G * HD), :].rearrange("(h d) n -> d h n", d=HD)
                        sp.dma_start(stack[t * HD:(t + 1) * HD, bass.ds(slot(g), 1), :, :].rearrange("d a h n -> d (a h) n"),
                                     rows).then_inc(stacks_loaded.sem, 16)

            def move_max(g):
                max_split_ready.wait(sp, g)
                sp.dma_start(max_parts.rearrange("a r n -> r a n"), max_split[:]).then_inc(max_stored.sem, 16)
                max_stored.wait(sp, g)
                sp.dma_start(q_stack[MAX_ROW:STACK, bass.ds(slot(g), 1), :, :].rearrange("d a h n -> d (a h n)"),
                             max_parts.rearrange("a r n -> a (r n)")).then_inc(max_loaded.sem, 16)

            def prologue(g):
                load_stacks(0)
                move_max(0)

            def group(g, last):
                if not last:
                    load_stacks(g + 1)
                    move_max(g + 1)

            passes(sp, prologue, group)

        @block.gpsimd
        def _(pool):
            v_ones_ready.credit(pool), triangled.credit(pool)
            pool.memset(k_stack[MAX_ROW:P, :, :, :], 1.0).then_inc(ones_rows, 1)
            pool.wait_ge(ones_rows, 1)
            pool.memset(causal[:], 0.0).then_inc(prepared, 1)
            pool.memset(v_ones[:], 0.0).then_inc(prepared, 1)
            pool.memset(maxima[:], NEG).then_inc(prepared, 1)
            pool.wait_ge(prepared, 3)
            pool.affine_select(out=causal[:], in_=causal[:], compare_op=ALU.is_ge, fill=NEG, base=0,
                               pattern=[[-1, P]], channel_multiplier=1).then_inc(prepared, 1)
            pool.memset(v_ones[:, :, :, HD:HD + 1], 1.0).then_inc(prepared, 1)
            pool.wait_ge(prepared, 5)

            def group(g):
                weighted.wait_before(pool, g)
                stand_alone(pool, pool_passed)
                pool.tensor_copy(v_ones[:, :, :, 0:HD], values[:, :, cols(g, G * HD)].rearrange("p b (h d) -> p b h d", d=HD)
                                 ).then_inc(v_ones_ready.sem, 1)
                d = 0
                for s, (c, kb) in enumerate(E_STEPS):
                    r = kb - R * c
                    if r < 0:
                        continue
                    for hp in range(2):
                        exped.wait_alone(pool, pool_passed, g, 2 * s + hp + 1)
                        block_ = probs[:, s % 2, hp, :, r * P:(r + 1) * P]
                        pool.affine_select(out=block_, in_=block_, compare_op=ALU.is_ge, fill=0.0, base=0,
                                           pattern=[[0, 2], [1, P]], channel_multiplier=-1).then_inc(triangled.sem, 1)

            with pool.Fori(0, GROUPS1) as g:
                group(g)

        @block.tensor
        def _(pe):
            for s in (rows_scored, max_turned, keyed_scored, weighted, out_turned):
                s.credit(pe)
            pe.wait_ge(ones_rows, 1)

            def stack_at(stack, rows, g, h, at, size):
                return stack[0:rows, bass.ds(slot(g), 1), h, at:at + size].rearrange("k a n -> k (a n)")

            def row_scores(g, s):
                c, r, kc = M_STEPS[s]
                width = CHUNK if kc < c else (r + 1) * P
                for h in range(G):
                    rows_reduced.wait_before(pe, g, 0 - (G * s + h) + 2)
                    pe.matmul(rows_ps[:, h % 2, 0:width], stack_at(q_stack, MAX_ROW, g, h, (R * c + r) * P, P),
                              stack_at(k_stack, MAX_ROW, g, h, kc * CHUNK, width), start=True, stop=True).then_inc(rows_scored.sem, 1)

            def turn_max(g):
                neg_max_ready.wait(pe, g)
                out_turned_free(g)
                stand_alone(pe, pe_passed)
                pe.transpose(misc_ps[0:G * QB, 0:P], neg_max[:], core.ident[:]).then_inc(max_turned.sem, 1)

            def out_turned_free(g):
                out_ready.wait_before(pe, g)

            def key_scores(g, s):
                c, kb = E_STEPS[s]
                off = max(0, kb - R * c) * P
                for hp in range(2):
                    exped.wait_before(pe, g, 2 - (2 * s + hp))
                    for a in range(2):
                        last = pe.matmul(keyed_ps[:, hp, a, off:CHUNK], stack_at(k_stack, STACK, g, 2 * hp + a, kb * P, P),
                                         stack_at(q_stack, STACK, g, 2 * hp + a, c * CHUNK + off, CHUNK - off),
                                         start=True, stop=True)
                    last.then_inc(keyed_scored.sem, 1)

            def weigh(g, s, d):
                c, kb = E_STEPS[s]
                off = max(0, kb - R * c) * P
                exped.wait(pe, g, 2 * s + 2)
                if kb >= R * c:
                    triangled.wait(pe, g, 2 * (R * c + kb - R * c) + 2)
                if kb == 0:
                    out_copied.wait_before(pe, g, 1 - c)
                for h in range(G):
                    last = pe.matmul(out_ps[2 * HD * h:2 * HD * (h + 1), off:CHUNK], v_ones[:, kb, h, :],
                                     probs[:, s % 2, h // 2, h % 2, off:CHUNK], start=(kb == 0), stop=(kb == R * (c + 1) - 1),
                                     tile_position=(0, 2 * HD * h))
                last.then_inc(weighted.sem, 1)

            def turn_out(g, c):
                out_copied.wait(pe, g, c + 1)
                out_ready.wait_before(pe, g, 1 - c)
                if c == 0:
                    split_steps.wait(pe, g)
                for r in range(R):
                    last = pe.transpose(misc_ps[:, r * P:(r + 1) * P], out_t[:, r * P:(r + 1) * P], core.ident[:])
                last.then_inc(out_turned.sem, 1)

            def prologue(g):
                stacks_loaded.wait(pe, 0)
                for s in range(NS):
                    row_scores(0, s)
                turn_max(0)

            def group(g, last):
                v_ones_ready.wait(pe, g)
                max_loaded.wait(pe, g)
                if not last:
                    stacks_loaded.wait(pe, g + 1)
                pending = None
                for s, (c, kb) in enumerate(E_STEPS):
                    key_scores(g, s)
                    if not last:
                        row_scores(g + 1, s)
                    if s > 0:
                        weigh(g, s - 1, None)
                    if pending is not None and kb == 1:
                        turn_out(g, pending)
                        pending = None
                    if kb == R * (c + 1) - 1:
                        pending = c
                weigh(g, NS - 1, None)
                turn_out(g, CHUNKS - 1)
                if not last:
                    turn_max(g + 1)

            passes(pe, prologue, group)

        @block.scalar
        def _(act):
            exped.credit(act), out_copied.credit(act)

            def copy_out(g, c):
                weighted.wait(act, g, sum(R * (x + 1) for x in range(c + 1)))
                out_turned.wait_before(act, g, 1 - c)
                act.activation(out_t[:], out_ps[:], ACT.Copy).then_inc(out_copied.sem, 1)

            def group(g):
                pending = None
                for s, (c, kb) in enumerate(E_STEPS):
                    off = max(0, kb - R * c) * P
                    for hp in range(2):
                        keyed_scored.wait(act, g, 2 * s + hp + 1)
                        if hp == 0:
                            weighted.wait_before(act, g, 2 - s)
                        act.activation(probs[:, s % 2, hp, :, off:CHUNK], keyed_ps[:, hp, :, off:CHUNK],
                                       ACT.Exp).then_inc(exped.sem, 1)
                    if pending is not None:
                        copy_out(g, pending)
                        pending = None
                    if kb == R * (c + 1) - 1:
                        pending = c
                copy_out(g, CHUNKS - 1)

            with act.Fori(0, GROUPS1) as g:
                group(g)

        @block.vector
        def _(dve):
            for s in (rows_reduced, max_ready, neg_max_ready, split_steps, max_split_ready, inv_ready, out_ready):
                s.credit(dve)
            dve.wait_ge(prepared, 5)

            def reduce_rows(g, s):
                c, r, kc = M_STEPS[s]
                for h in range(G):
                    rows_scored.wait(dve, g, G * s + h + 1)
                    if kc == c and r == 0:
                        stand_alone(dve, dve_passed)
                    ps, to = rows_ps[:, h % 2, :], maxima[:, h, R * c + r, :]
                    if kc < c:
                        last = dve.reduce_max(to[:, kc:kc + 1], ps, AX_X)
                    else:
                        if r > 0:
                            dve.reduce_max(to[:, kc:kc + 1], ps[:, 0:r * P], AX_X)
                        last = dve.tensor_tensor_reduce(masked[:, h % 2, :], ps[:, r * P:(r + 1) * P], causal[:], 1.0, NEG,
                                                        ALU.add, ALU.max, to[:, 4:5])
                    last.then_inc(rows_reduced.sem, 1)

            def finish_max(g):
                rows_reduced.wait(dve, g)
                dve.reduce_max(row_max[:], maxima[:].rearrange("p h b s -> p (h b) s"), AX_X).then_inc(max_ready.sem, 1)
                max_ready.wait(dve, g)
                dve.tensor_scalar(neg_max[:], row_max[:], -1.0, None, ALU.mult).then_inc(neg_max_ready.sem, 1)

            def split_max(g):
                max_turned.wait(dve, g)
                max_stored.wait_before(dve, g, 16 - 15)
                turned = misc_ps[0:G * QB, 0:P]
                dve.tensor_copy(max_split[:, 0, :], turned).then_inc(split_steps.sem, 1)
                split_steps.wait(dve, g, 1)
                dve.tensor_tensor(max_rest[:, 0, :], turned, max_split[:, 0, :], ALU.subtract).then_inc(split_steps.sem, 1)
                split_steps.wait(dve, g, 2)
                dve.tensor_copy(max_split[:, 1, :], max_rest[:, 0, :]).then_inc(split_steps.sem, 1)
                split_steps.wait(dve, g, 3)
                dve.tensor_tensor(max_rest[:, 1, :], max_rest[:, 0, :], max_split[:, 1, :], ALU.subtract).then_inc(split_steps.sem, 1)
                split_steps.wait(dve, g, 4)
                dve.tensor_copy(max_split[:, 2, :], max_rest[:, 1, :]).then_inc(max_split_ready.sem, 1)

            def divide(g, c):
                out_turned.wait(dve, g, c + 1)
                turned = misc_ps[:].rearrange("p (r h d) -> p r h d", r=R, h=G)
                dve.reciprocal(inv_sum[:], turned[:, :, :, HD]).then_inc(inv_ready.sem, 1)
                inv_ready.wait(dve, g, c + 1)
                for r in range(R):
                    out = att[:, R * c + r, cols(g, G * HD)].rearrange("p (h d) -> p h d", h=G)
                    last = dve.tensor_tensor(out, turned[:, r, :, 0:HD],
                                             inv_sum[:, r, :].unsqueeze(2).to_broadcast([P, G, HD]), ALU.mult)
                last.then_inc(out_ready.sem, 1)

            def prologue(g):
                for s in range(NS):
                    reduce_rows(0, s)
                finish_max(0)
                split_max(0)

            def group(g, last):
                pending = None
                for s, (c, kb) in enumerate(E_STEPS):
                    if not last:
                        reduce_rows(g + 1, s)
                    if pending is not None and kb == 3:
                        divide(g, pending)
                        pending = None
                    if kb == R * (c + 1) - 1:
                        pending = c
                if not last:
                    finish_max(g + 1)
                divide(g, CHUNKS - 1)
                if not last:
                    split_max(g + 1)

            passes(dve, prologue, group)


def phase_attention_out(nc, core, att, w_out, b_out):
    with ExitStack() as ctx:
        m = Mem(nc, ctx, "out")
        raw = m.sb("raw", [P, KD, D])
        w_hi, w_lo = m.sb("w_hi", [P, KD, D], F32R), m.sb("w_lo", [P, KD, D], F32R)
        bias = m.sb("bias", [P, D])
        att_hi, att_lo = m.sb("att_hi", [P, KD, CHUNK], F32R), m.sb("att_lo", [P, KD, CHUNK], F32R)
        y, y_normed = m.sb("y", [P, R, D]), m.sb("y_normed", [P, R, D])
        post, pre, turn = Stats(m, "post"), Stats(m, "pre"), Turn(m, core)
        att_ps, y_ps = m.ps("att_ps", [P, KD, CHUNK]), m.ps("y_ps", [P, R // 2, 2 * D])
        w_loaded, b_loaded = m.sem("w_loaded"), m.sem("b_loaded")
        att_chunk = m.sb("att_chunk", [P, R, D])
        att_staged, pool_passed = m.sem("att_staged"), m.sem("pool_passed")
        att_turned, att_hi_ready, att_lo_ready = m.sem("att_turned"), m.sem("att_hi_ready"), m.sem("att_lo_ready")
        projected, y_ready, y_read, x_updated = (m.sem(s) for s in ("projected", "y_ready", "y_read", "x_updated"))
        turning = TurnWeights(m, core, lambda u: att_ps[:, u % 2, :])
        units = [([raw[:, j, k * P:(k + 1) * P] for j in range(KD)], w_hi[:, k, :], w_lo[:, k, :], 0) for k in range(KD)]
        block = m.start()

        @block.sync
        def _(sp):
            sp.dma_start(raw[:], w_out.rearrange("(j p) n -> p j n", p=P)).then_inc(w_loaded, 16)
            sp.dma_start(bias[:], b_out.rearrange("(a n) -> a n", a=1).to_broadcast([P, D])).then_inc(b_loaded, 16)

        @block.tensor
        def _(pe):
            turning.pe(pe, units, lambda w: pe.wait_ge(w_loaded, 16))
            pe.wait_ge(turning.lo_ready, len(units))

            def chunk(c):
                reach(pe, att_lo_ready, KD * c)
                for k in range(KD):
                    for r in range(R):
                        last = pe.transpose(att_ps[:, k, r * P:(r + 1) * P], att_chunk[:, r, k * P:(k + 1) * P], core.ident[:])
                    last.then_inc(att_turned, 1)
                pe.wait_ge(att_lo_ready, KD * (c + 1))
                reach(pe, y_ready, c)
                for r in range(R):
                    at = slice(r * P, (r + 1) * P)
                    for k in range(KD):
                        for i, (a, w) in enumerate(((att_hi, w_hi), (att_hi, w_lo), (att_lo, w_hi))):
                            last = pe.matmul(y_ps[:, r // 2, (r % 2) * D:(r % 2 + 1) * D], a[:, k, at], w[:, k, :],
                                             start=(k == 0 and i == 0), stop=(k == KD - 1 and i == 2))
                last.then_inc(projected, 1)
                turn.pe_turn(pe, c)

            def staged(c):
                pe.wait_ge(att_staged, c + 1)
                chunk(c)

            first_then_loop(pe, CHUNKS, staged)

        @block.gpsimd
        def _(pool):
            def chunk(c):
                reach(pool, att_turned, KD * c)
                stand_alone(pool, pool_passed)
                pool.tensor_copy(att_chunk[:], att[:, cols(c, R), :]).then_inc(att_staged, 1)
            first_then_loop(pool, CHUNKS, chunk)

        @block.scalar
        def _(act):
            turning.act(act, units)

            def chunk(c):
                reach(act, projected, c)
                for k in range(KD):
                    act.wait_ge(att_turned, KD * c + k + 1)
                    act.activation(att_hi[:, k, :], att_ps[:, k, :], ACT.Copy).then_inc(att_hi_ready, 1)
                post.act_std(act, c)
                pre.act_std(act, c)
                turn.act_hi(act, c, c)
            first_then_loop(act, CHUNKS, chunk)

        @block.vector
        def _(dve):
            turning.dve(dve, units)
            dve.wait_ge(b_loaded, 16)

            def chunk(c):
                for k in range(KD):
                    dve.wait_ge(att_hi_ready, KD * c + k + 1)
                    dve.tensor_tensor(att_lo[:, k, :], att_ps[:, k, :], att_hi[:, k, :].bitcast(F32),
                                      ALU.subtract).then_inc(att_lo_ready, 1)
                dve.wait_ge(projected, c + 1)
                for r in range(R):
                    last = dve.tensor_tensor(y[:, r, :], y_ps[:, r // 2, (r % 2) * D:(r % 2 + 1) * D], bias[:], ALU.add)
                last.then_inc(y_ready, 1)
                dve.wait_ge(y_ready, c + 1)
                post.dve_variance(dve, lambda r: y[:, r, :], c)
                post.dve_rstd(dve, c)
                post.dve_normalise(dve, lambda r: y_normed[:, r, :], lambda r: y[:, r, :]).then_inc(y_read, 1)
                dve.wait_ge(y_read, c + 1)
                dve.tensor_tensor(core.x_chunk(c), core.x_chunk(c), y_normed[:].rearrange("p a d -> p (a d)"),
                                  ALU.add).then_inc(x_updated, 1)
                dve.wait_ge(x_updated, c + 1)
                pre.dve_variance(dve, core.x_tile(c), c)
                pre.dve_rstd(dve, c)
                pre.dve_normalise(dve, lambda r: turn.xn[:, r, :], core.x_tile(c)).then_inc(turn.xn_ready, 1)
                turn.dve_lo(dve, c, c)

            first_then_loop(dve, CHUNKS, chunk)



def build(nc, x, w_q, w_k, w_v, w_o, betas, w_gate0, w_up0, w_down0, w_qkv, b_qkv, w_out, b_out,
          w_gate1, gate_scale, w_up1, up_scale, w_down1, down_scale, out):
    q_parts = nc.dram_tensor("q_parts", [PARTS, D, T], BF16, kind="Internal").ap()
    k_parts = nc.dram_tensor("k_parts", [PARTS, D, T], BF16, kind="Internal").ap()
    max_parts = nc.dram_tensor("max_parts", [PARTS, G * QB, P], BF16, kind="Internal").ap()
    memory_att = nc.dram_tensor("memory_att", [T, D], F32, kind="Internal").ap()
    sigmoids = nc.dram_tensor("sigmoids", [HEADS, 2, DH], F32, kind="Internal").ap()
    with ExitStack() as ctx:
        core = Core(nc, ctx)
        phase_input(nc, core, x)
        phase_memory_attention(nc, core, memory_att, sigmoids, w_q, w_k, w_v, w_o, betas)
        core.hold_x(nc, ctx)
        phase_residual(nc, core, x, memory_att, "res0")
        phase_ffn(nc, core, "ffn0", w_gate0, w_up0, w_down0)
        mixed = ctx.enter_context(nc.sbuf_tensor("mixed", [P, TILES, D], F32))
        with nc.sbuf_tensor("values", [P, TILES, D], F32) as values:
            phase_qkv(nc, core, values, w_qkv, b_qkv, q_parts, k_parts)
            phase_attention(nc, core, mixed, values, q_parts, k_parts, max_parts)
        phase_attention_out(nc, core, mixed, w_out, b_out)
        phase_ffn(nc, core, "ffn1", w_gate1, w_up1, w_down1, scales=(gate_scale, up_scale, down_scale), out=out)


_INS = ["L0_attn_x", "L0_attn_Wq", "L0_attn_Wk", "L0_attn_Wv", "L0_attn_Wo", "L0_attn_betas",
        "L0_ffn_w_gate", "L0_ffn_w_up", "L0_ffn_w_down",
        "L1_attn_w_qkv", "L1_attn_b_qkv", "L1_attn_w_out", "L1_attn_b_out",
        "L1_ffn_gate_w", "L1_ffn_gate_scale", "L1_ffn_up_w", "L1_ffn_up_scale", "L1_ffn_down_w", "L1_ffn_down_scale"]


def kernel(**inputs):
    import numpy as np
    import concourse.bacc as bacc
    from concourse.bass_utils import run_bass_kernel_spmd

    nc = bacc.Bacc("TRN2", target_bir_lowering=False, num_devices=1)
    nc.disable_value_cache = True
    arrays, args = {}, []
    for name in _INS:
        a = np.ascontiguousarray(inputs[name])
        arrays[name] = a
        args.append(nc.dram_tensor(name, a.shape, mybir.dt.from_np(a.dtype), kind="ExternalInput").ap())
    out = nc.dram_tensor("out", (1, T, D), F32, kind="ExternalOutput").ap()
    build(nc, *args, out)
    r = run_bass_kernel_spmd(nc, [arrays], core_ids=[0])
    return r.results[0]["out"]
```

```python
from contextlib import ExitStack

import concourse.bass as bass
from concourse import mybir

F32 = mybir.dt.float32
F32R = mybir.dt.float32r
BF16 = mybir.dt.bfloat16
I32 = mybir.dt.int32
ALU = mybir.AluOpType
ACT = mybir.ActivationFunctionType
AX_X = mybir.AxisListType.X

P = 128
D = 256
KD = D // P
T = 2048
TILES = T // P
CHUNK = 512
R = CHUNK // P
CHUNKS = T // CHUNK
F = 1024
FB = F // P
EPS = 1e-5


def reach(eng, sem, value):
    if isinstance(value, int) and value <= 0:
        return
    eng.wait_ge(sem, value)


def stand_alone(eng, passed):
    eng.sem_inc(passed, 1)


def first_then_loop(eng, count, body):
    body(0)
    with eng.Fori(1, count) as n:
        body(n)


def cols(n, width):
    return bass.ds(n * width, width)


class Mem:
    last_phase = None

    def __init__(self, nc, ctx, phase):
        self.nc, self.ctx, self.phase, self.sems = nc, ctx, phase, []

    def start(self):
        if Mem.last_phase is not None and Mem.last_phase.nc is self.nc:
            self.nc.clear_and_free_semaphores(Mem.last_phase.sems)
        Mem.last_phase = self
        return self.ctx.enter_context(self.nc.Block(no_gpsimd_drain=True))

    def sb(self, name, shape, dt=F32):
        return self.ctx.enter_context(self.nc.sbuf_tensor(f"{self.phase}_{name}", shape, dt))

    def ps(self, name, shape, dt=F32):
        return self.ctx.enter_context(self.nc.psum_tensor(f"{self.phase}_{name}", shape, dt))

    def sem(self, name):
        self.sems.append(self.nc.alloc_semaphore(f"{self.phase}_{name}"))
        return self.sems[-1]


class Stats:

    def __init__(self, m, name):
        self.sums = m.sb(name + "_sums", [P, R, 6])
        self.mean_var = m.sb(name + "_mean_var", [P, R, 2])
        self.var_eps = m.sb(name + "_var_eps", [P, R])
        self.std = m.sb(name + "_std", [P, R])
        self.rstd = m.sb(name + "_rstd", [P, R])
        self.sums_ready = m.sem(name + "_sums_ready")
        self.sums_passed = m.sem(name + "_sums_passed")
        self.mean_ready = m.sem(name + "_mean_ready")
        self.var_ready = m.sem(name + "_var_ready")
        self.std_ready = m.sem(name + "_std_ready")
        self.rstd_ready = m.sem(name + "_rstd_ready")

    def dve_variance(self, dve, tile_of, n):
        for r in range(R):
            last = dve.bn_stats(self.sums[:, r, :], tile_of(r))
        last.then_inc(self.sums_ready, 1)
        dve.wait_ge(self.sums_ready, n + 1)
        stand_alone(dve, self.sums_passed)
        for r in range(R):
            last = dve.bn_aggr(self.mean_var[:, r, :], self.sums[:, r, :])
        last.then_inc(self.mean_ready, 1)
        dve.wait_ge(self.mean_ready, n + 1)
        reach(dve, self.std_ready, n)
        dve.tensor_scalar(self.var_eps[:], self.mean_var[:, :, 1], EPS, None, ALU.add).then_inc(self.var_ready, 1)

    def act_std(self, act, n):
        act.wait_ge(self.var_ready, n + 1)
        reach(act, self.rstd_ready, n)
        act.activation(self.std[:], self.var_eps[:], ACT.Sqrt).then_inc(self.std_ready, 1)

    def dve_rstd(self, dve, n):
        dve.wait_ge(self.std_ready, n + 1)
        dve.reciprocal(self.rstd[:], self.std[:]).then_inc(self.rstd_ready, 1)
        dve.wait_ge(self.rstd_ready, n + 1)

    def dve_normalise(self, dve, out_of, tile_of):
        for r in range(R):
            last = dve.tensor_scalar(out_of(r), tile_of(r), self.mean_var[:, r, 0:1], self.rstd[:, r:r + 1],
                                     ALU.subtract, ALU.mult)
        return last


class Turn:

    def __init__(self, m, core, name="turn"):
        self.core = core
        self.xn = m.sb(name + "_xn", [P, R, D])
        self.turned = m.ps(name + "_turned", [P, KD, CHUNK])
        self.xn_ready = m.sem(name + "_xn_ready")
        self.turned_ready = m.sem(name + "_turned_ready")
        self.hi_ready = m.sem(name + "_hi_ready")
        self.lo_ready = m.sem(name + "_lo_ready")

    def pe_turn(self, pe, n):
        pe.wait_ge(self.xn_ready, n + 1)
        reach(pe, self.lo_ready, KD * n)
        for k in range(KD):
            for r in range(R):
                last = pe.transpose(self.turned[:, k, r * P:(r + 1) * P], self.xn[:, r, k * P:(k + 1) * P],
                                    self.core.ident[:])
            last.then_inc(self.turned_ready, 1)

    def act_hi(self, act, n, c):
        for k in range(KD):
            act.wait_ge(self.turned_ready, KD * n + k + 1)
            act.activation(self.core.xt_hi[:, k, cols(c, CHUNK)], self.turned[:, k, :],
                           ACT.Copy).then_inc(self.hi_ready, 1)

    def dve_lo(self, dve, n, c):
        for k in range(KD):
            dve.wait_ge(self.hi_ready, KD * n + k + 1)
            dve.tensor_tensor(self.core.xt_lo[:, k, cols(c, CHUNK)], self.turned[:, k, :],
                              self.core.xt_hi[:, k, cols(c, CHUNK)].bitcast(F32),
                              ALU.subtract).then_inc(self.lo_ready, 1)


class Ahead:

    def __init__(self, nc, ctx, name, parts):
        m = Mem(nc, ctx, name)
        self.tiles = [m.sb(n, shape) for n, shape, source in parts]
        self.sources = [source for n, shape, source in parts]

    def signal_in(self, m):
        self.loaded = m.sem("ahead_loaded")

    def load(self, eng):
        for tile, source in zip(self.tiles, self.sources):
            eng.dma_start(tile[:], source).then_inc(self.loaded, 16)

    def finish(self, eng):
        eng.wait_ge(self.loaded, 16 * len(self.tiles))


class Core:

    def __init__(self, nc, ctx):
        m = Mem(nc, ctx, "core")
        self.xt_hi = m.sb("xt_hi", [P, KD, T], F32R)
        self.xt_lo = m.sb("xt_lo", [P, KD, T], F32R)
        self.ident = m.sb("ident", [P, P])

    def hold_x(self, nc, ctx):
        self.x = Mem(nc, ctx, "core").sb("x", [P, TILES, D])

    def x_tile(self, c):
        return lambda r: self.x[:, bass.ds(c * R + r, 1), :].rearrange("p a d -> p (a d)")

    def x_chunk(self, c):
        return self.x[:, cols(c, R), :].rearrange("p a d -> p (a d)")


def phase_input(nc, core, x_in, ahead):
    with ExitStack() as ctx:
        m = Mem(nc, ctx, "in")
        norm, turn = Stats(m, "norm"), Turn(m, core)
        x = m.sb("x", [P, TILES, D])
        zeroed, ident_ready = m.sem("zeroed"), m.sem("ident_ready")
        ahead.signal_in(m)
        x_loaded = [m.sem(f"x_loaded{c}") for c in range(CHUNKS)]
        block = m.start()

        @block.sync
        def _(sp):
            for c in range(CHUNKS):
                sp.dma_start(x[:, c * R:(c + 1) * R, :],
                             x_in[0, c * CHUNK:(c + 1) * CHUNK, :].rearrange("(a p) d -> p a d", p=P)).then_inc(x_loaded[c], 16)
            ahead.load(sp)
            ahead.finish(sp)

        @block.gpsimd
        def _(pool):
            pool.memset(core.ident[:], 0.0).then_inc(zeroed, 1)
            pool.wait_ge(zeroed, 1)
            pool.affine_select(out=core.ident[:], in_=core.ident[:], compare_op=ALU.not_equal, fill=1.0, base=0,
                               pattern=[[-1, P]], channel_multiplier=1).then_inc(ident_ready, 1)

        @block.vector
        def _(dve):
            def normalise(c):
                x_tile = lambda r: x[:, c * R + r, :]
                dve.wait_ge(x_loaded[c], 16)
                norm.dve_variance(dve, x_tile, c)
                norm.dve_rstd(dve, c)
                reach(dve, turn.turned_ready, KD * c)
                norm.dve_normalise(dve, lambda r: turn.xn[:, r, :], x_tile).then_inc(turn.xn_ready, 1)

            for c in range(CHUNKS):
                normalise(c)
                turn.dve_lo(dve, c, c)

        @block.scalar
        def _(act):
            for c in range(CHUNKS):
                norm.act_std(act, c)
                turn.act_hi(act, c, c)

        @block.tensor
        def _(pe):
            pe.wait_ge(ident_ready, 1)
            for c in range(CHUNKS):
                turn.pe_turn(pe, c)


class TurnWeights:

    def __init__(self, m, core, bank_of, units):
        self.core, self.bank_of, self.units = core, bank_of, units
        self.turned_ready = m.sem("weights_turned_ready")
        self.hi_ready = m.sem("weights_hi_ready")
        self.lo_ready = m.sem("weights_lo_ready")

    def pe(self, pe, source_ready, some=None):
        for u in some if some is not None else range(len(self.units)):
            sources, hi, lo, needs = self.units[u]
            source_ready(needs)
            reach(pe, self.lo_ready, u - 1)
            for s, source in enumerate(sources):
                last = pe.transpose(self.bank_of(u)[:, s * P:(s + 1) * P], source, self.core.ident[:])
            last.then_inc(self.turned_ready, 1)

    def act(self, act, some=None):
        for u in some if some is not None else range(len(self.units)):
            sources, hi, lo, needs = self.units[u]
            act.wait_ge(self.turned_ready, u + 1)
            act.activation(hi, self.bank_of(u)[:, 0:len(sources) * P], ACT.Copy).then_inc(self.hi_ready, 1)

    def dve(self, dve, some=None):
        for u in some if some is not None else range(len(self.units)):
            sources, hi, lo, needs = self.units[u]
            dve.wait_ge(self.hi_ready, u + 1)
            dve.tensor_tensor(lo, self.bank_of(u)[:, 0:len(sources) * P], hi.bitcast(F32),
                              ALU.subtract).then_inc(self.lo_ready, 1)


class FfnWeights:
    ZERO_POINT = 128.0
    PLACES = 2

    def __init__(self, nc, ctx, core, name, w_gate, w_up, w_down, scales=None):
        m = Mem(nc, ctx, name)
        self.core, self.sources, self.scales = core, (w_gate, w_up, w_down), scales
        self.gate_hi, self.gate_lo = m.sb("gate_hi", [P, KD, F], F32R), m.sb("gate_lo", [P, KD, F], F32R)
        self.up_hi, self.up_lo = m.sb("up_hi", [P, KD, F], F32R), m.sb("up_lo", [P, KD, F], F32R)
        self.down_hi, self.down_lo = m.sb("down_hi", [P, FB, D], F32R), m.sb("down_lo", [P, FB, D], F32R)

    def prepare_in(self, m, first_chunk):
        raw_dt = F32 if self.scales is None else I32
        self.raw = [m.sb("raw_gate", [P, FB, D], raw_dt), m.sb("raw_up", [P, FB, D], raw_dt), m.sb("raw_down", [P, KD, F], raw_dt)]
        bank = m.ps("weights_ps", [P, 2, CHUNK])
        self.raw_loaded = [m.sem(f"raw_loaded_{w}") for w in ("gate", "up", "down")]
        gate, up, down = self.raw
        if self.scales is not None:
            self.scaled, self.scales_loaded = m.sem("weights_scaled"), m.sem("scales_loaded")
            self.scale = m.sb("scale", [P, 2 * FB + KD])
            gate, up, down = (t[:].bitcast(F32) for t in self.raw)
        units = []
        for w, (src, hi, lo) in enumerate(((gate, self.gate_hi, self.gate_lo), (up, self.up_hi, self.up_lo))):
            for k in range(KD):
                for j0 in range(0, FB, 4):
                    units.append(([src[:, j, k * P:(k + 1) * P] for j in range(j0, j0 + 4)],
                                  hi[:, k, j0 * P:(j0 + 4) * P], lo[:, k, j0 * P:(j0 + 4) * P], w))
        for j0 in range(0, FB, 2):
            units.append(([down[:, k, j * P:(j + 1) * P] for j in (j0, j0 + 1) for k in range(KD)],
                          self.down_hi[:, j0:j0 + 2, :].rearrange("p j d -> p (j d)"),
                          self.down_lo[:, j0:j0 + 2, :].rearrange("p j d -> p (j d)"), 2))
        self.turning = TurnWeights(m, self.core, lambda u: bank[:, u % 2, :], units)
        self.first_chunk, self.slots = first_chunk, (CHUNKS - first_chunk) * self.PLACES

    def some(self, c, place):
        slot = (c - self.first_chunk) * self.PLACES + place
        n = len(self.turning.units)
        return range(max(0, n * slot // self.slots), max(0, n * (slot + 1) // self.slots))

    def load(self, sp, w):
        if self.scales is not None:
            at, n = ((0, FB), (FB, FB), (2 * FB, KD))[w]
            sp.dma_start(self.scale[:, at:at + n], self.scales[w].rearrange("(j p) -> p j", p=P), allow_slow_non_contiguous=True).then_inc(self.scales_loaded, 16)
        sp.dma_start(self.raw[w][:], self.sources[w].rearrange("(j p) n -> p j n", p=P)).then_inc(self.raw_loaded[w], 16)

    def pool_scale(self, pool):
        if self.scales is None:
            return
        pool.wait_ge(self.scales_loaded, 16 * 3)
        for w, (at, n) in enumerate(((0, FB), (FB, FB), (2 * FB, KD))):
            pool.wait_ge(self.raw_loaded[w], 16)
            for j in range(n):
                last = pool.tensor_scalar(self.raw[w][:, j, :].bitcast(F32), self.raw[w][:, j, :], self.ZERO_POINT,
                                          self.scale[:, at + j:at + j + 1], ALU.subtract, ALU.mult)
            last.then_inc(self.scaled, 1)

    def pe(self, pe, c, place):
        if self.scales is None:
            ready = lambda w: pe.wait_ge(self.raw_loaded[w], 16)
        else:
            ready = lambda w: pe.wait_ge(self.scaled, w + 1)
        self.turning.pe(pe, ready, self.some(c, place))

    def act(self, act, c, place):
        self.turning.act(act, self.some(c, place))

    def dve(self, dve, c, place):
        self.turning.dve(dve, self.some(c, place))


def phase_ffn(nc, core, name, weights, ahead=None, out=None):
    with ExitStack() as ctx:
        m = Mem(nc, ctx, name)
        gate_hi, gate_lo, up_hi, up_lo = weights.gate_hi, weights.gate_lo, weights.up_hi, weights.up_lo
        down_hi, down_lo = weights.down_hi, weights.down_lo
        silu = m.sb("silu", [P, 2, CHUNK])
        hidden = m.sb("hidden", [P, 2, CHUNK])
        hidden_hi, hidden_lo = m.sb("hidden_hi", [P, 2, CHUNK], F32R), m.sb("hidden_lo", [P, 2, CHUNK], F32R)
        y, y_normed = m.sb("y", [P, R, D]), m.sb("y_normed", [P, R, D])
        post, pre, turn = Stats(m, "post"), Stats(m, "pre"), Turn(m, core)

        gate_ps = m.ps("gate_ps", [P, 2, CHUNK])
        up_ps = m.ps("up_ps", [P, 2, CHUNK])
        y_ps = m.ps("y_ps", [P, R // 2, 2 * D])

        gate_up_ready = m.sem("gate_up_ready")
        silu_ready = m.sem("silu_ready")
        hidden_ready = m.sem("hidden_ready")
        hidden_hi_ready = m.sem("hidden_hi_ready")
        hidden_lo_ready = m.sem("hidden_lo_ready")
        down_done = m.sem("down_done")
        y_copied = m.sem("y_copied")
        y_read = m.sem("y_read")
        x_updated = m.sem("x_updated")
        stored = m.sem("stored")
        last_layer = out is not None
        if ahead is not None:
            ahead.signal_in(m)
        LAG = 2

        block = m.start()

        @block.sync
        def _(sp):
            if ahead is not None:
                ahead.load(sp)
                ahead.finish(sp)
            if last_layer:
                def store(n):
                    sp.wait_ge(x_updated, n + 1)
                    sp.dma_start(out[0, cols(n, CHUNK), :].rearrange("(a p) d -> p a d", p=P),
                                 core.x[:, cols(n, R), :]).then_inc(stored, 16)
                with sp.Fori(0, CHUNKS) as n:
                    store(n)
                sp.wait_ge(stored, 16 * CHUNKS)

        @block.tensor
        def _(pe):
            def gate_up(n, j):
                reach(pe, hidden_ready, FB * n + j - 1)
                for w_hi, w_lo, ps in ((gate_hi, gate_lo, gate_ps), (up_hi, up_lo, up_ps)):
                    for k in range(KD):
                        for i, (w, x) in enumerate(((w_hi, core.xt_hi), (w_hi, core.xt_lo), (w_lo, core.xt_hi))):
                            last = pe.matmul(ps[:, j % 2, :], w[:, k, j * P:(j + 1) * P], x[:, k, cols(n, CHUNK)],
                                             start=(k == 0 and i == 0), stop=(k == KD - 1 and i == 2))
                last.then_inc(gate_up_ready, 1)

            def down(n, j):
                if j == 0:
                    reach(pe, y_copied, 2 * n)
                pe.wait_ge(hidden_lo_ready, FB * n + j + 1)
                for r in range(R):
                    at = slice(r * P, (r + 1) * P)
                    for i, (h, w) in enumerate(((hidden_hi, down_hi), (hidden_hi, down_lo), (hidden_lo, down_hi))):
                        last = pe.matmul(y_ps[:, r // 2, (r % 2) * D:(r % 2 + 1) * D], h[:, j % 2, at], w[:, j, :],
                                         start=(j == 0 and r % 2 == 0 and i == 0), stop=(j == FB - 1 and i == 2),
                                         skip_group_check=True)
                last.then_inc(down_done, 1)

            def chunk(n):
                first = isinstance(n, int) and n == 0
                for j in range(FB):
                    gate_up(n, j)
                    if j >= LAG:
                        down(n, j - LAG)
                    elif not first:
                        down(n - 1, FB + j - LAG)
                    if j == FB - 2 and not last_layer and not first:
                        turn.pe_turn(pe, n - 1)

            first_then_loop(pe, CHUNKS, chunk)
            for j in range(FB - LAG, FB):
                down(CHUNKS - 1, j)
            if not last_layer:
                turn.pe_turn(pe, CHUNKS - 1)

        @block.scalar
        def _(act):
            def copy_y(n):
                act.wait_ge(down_done, FB * (n + 1))
                reach(act, y_read, n)
                for half in range(2):
                    act.activation(y[:, half * (R // 2):(half + 1) * (R // 2), :].rearrange("p a d -> p (a d)"), y_ps[:, half, :],
                                   ACT.Copy).then_inc(y_copied, 1)

            def chunk(n):
                first = isinstance(n, int) and n == 0
                for j in range(FB):
                    act.wait_ge(gate_up_ready, FB * n + j + 1)
                    reach(act, hidden_ready, FB * n + j - 1)
                    act.activation(silu[:, j % 2, :], gate_ps[:, j % 2, :], ACT.Silu).then_inc(silu_ready, 1)
                    act.wait_ge(hidden_ready, FB * n + j + 1)
                    reach(act, down_done, FB * n + j - 1)
                    act.activation(hidden_hi[:, j % 2, :], hidden[:, j % 2, :], ACT.Copy).then_inc(hidden_hi_ready, 1)
                    if not first:
                        if j == LAG - 1:
                            copy_y(n - 1)
                        if j == LAG:
                            post.act_std(act, n - 1)
                        if j == LAG + 1 and not last_layer:
                            pre.act_std(act, n - 1)
                        if j == FB - 2 and not last_layer:
                            turn.act_hi(act, n - 1, n - 1)

            first_then_loop(act, CHUNKS, chunk)
            copy_y(CHUNKS - 1)
            post.act_std(act, CHUNKS - 1)
            if not last_layer:
                pre.act_std(act, CHUNKS - 1)
                turn.act_hi(act, CHUNKS - 1, CHUNKS - 1)

        @block.gpsimd
        def _(pool):
            def chunk(n):
                for j in range(FB):
                    pool.wait_ge(hidden_hi_ready, FB * n + j + 1)
                    pool.tensor_tensor(hidden_lo[:, j % 2, :], hidden[:, j % 2, :], hidden_hi[:, j % 2, :].bitcast(F32),
                                       ALU.subtract).then_inc(hidden_lo_ready, 1)

            with pool.Fori(0, CHUNKS) as n:
                chunk(n)

        @block.vector
        def _(dve):
            y_tile = lambda r: y[:, r, :]

            def tail_y_stats(c):
                dve.wait_ge(y_copied, 2 * (c + 1))
                post.dve_variance(dve, y_tile, c)

            def tail_add(c):
                post.dve_rstd(dve, c)
                post.dve_normalise(dve, lambda r: y_normed[:, r, :], y_tile).then_inc(y_read, 1)
                dve.wait_ge(y_read, c + 1)
                dve.tensor_tensor(core.x_chunk(c), core.x_chunk(c), y_normed[:].rearrange("p a d -> p (a d)"),
                                  ALU.add).then_inc(x_updated, 1)
                dve.wait_ge(x_updated, c + 1)
                if not last_layer:
                    pre.dve_variance(dve, core.x_tile(c), c)

            def tail_xn(c):
                pre.dve_rstd(dve, c)
                pre.dve_normalise(dve, lambda r: turn.xn[:, r, :], core.x_tile(c)).then_inc(turn.xn_ready, 1)

            def chunk(n):
                first = isinstance(n, int) and n == 0
                for j in range(FB):
                    dve.wait_ge(silu_ready, FB * n + j + 1)
                    reach(dve, hidden_lo_ready, FB * n + j - 1)
                    dve.tensor_tensor(hidden[:, j % 2, :], silu[:, j % 2, :], up_ps[:, j % 2, :],
                                      ALU.mult).then_inc(hidden_ready, 1)
                    if not first:
                        if j == LAG - 1:
                            tail_y_stats(n - 1)
                        if j == LAG:
                            tail_add(n - 1)
                        if j == LAG + 1 and not last_layer:
                            tail_xn(n - 1)
                        if j == FB - 2 and not last_layer:
                            turn.dve_lo(dve, n - 1, n - 1)

            first_then_loop(dve, CHUNKS, chunk)
            tail_y_stats(CHUNKS - 1)
            tail_add(CHUNKS - 1)
            if not last_layer:
                tail_xn(CHUNKS - 1)
                turn.dve_lo(dve, CHUNKS - 1, CHUNKS - 1)

HEADS = 16
DH = 128
SEG = 64
G = 4
GROUPS = HEADS // G
HALF = 2 * P
HALVES = T // HALF
UNITS = 6
PAIRS = T // P
QUADS = PAIRS // 4
STRIPS = SEG // HEADS
CREDIT = 8
NEG = -1e30


class Beat:

    def __init__(self, m, name, per=1):
        self.sem, self.per = m.sem(name), per

    def credit(self, eng):
        eng.sem_inc(self.sem, CREDIT)

    def at(self, n, m=None):
        return n * self.per + (CREDIT + (self.per if m is None else m))

    def wait(self, eng, n, m=None):
        eng.wait_ge(self.sem, self.at(n, m))

    def wait_alone(self, eng, passed, n, m=None):
        self.wait(eng, n, m)
        stand_alone(eng, passed)

    def wait_before(self, eng, n, back=1):
        eng.wait_ge(self.sem, n * self.per + (CREDIT + 1 - back))


def phase_memory_attention(nc, core, y_out, sigmoids, first_weights, w_q, w_k, w_v, w_o, betas):
    with ExitStack() as ctx:
        m = Mem(nc, ctx, "mem")
        W = G * DH
        raw = first_weights.tiles
        hi = [m.sb(f"{n}_hi", [P, KD, W], F32R) for n in "kqv"]
        lo = [m.sb(f"{n}_lo", [P, KD, W], F32R) for n in "kqv"]
        o_hi, o_lo = m.sb("o_hi", [P, HEADS, D], F32R), m.sb("o_lo", [P, HEADS, D], F32R)
        beta_heads = m.sb("beta_heads", [HEADS, 2, DH])
        beta, beta_rest = m.sb("beta", [P, W]), m.sb("beta_rest", [P, W])
        mask = m.sb("mask", [P, P])
        keyed_hi = [m.sb(f"keyed_hi{b}", [P, KD, HALF], F32R) for b in range(2)]
        keyed_lo = [m.sb(f"keyed_lo{b}", [P, KD, HALF], F32R) for b in range(2)]
        q_t = [m.sb(f"q_t{b}", [P, G, 2, P]) for b in range(2)]
        k_t = [m.sb(f"k_t{b}", [P, G, 2, P]) for b in range(2)]
        sigma = [m.sb(f"sigma{b}", [P, G, 2, 4 * SEG]) for b in range(2)]
        sigma_kt = [m.sb(f"sigma_kt{b}", [P, G, 2, P]) for b in range(2)]
        v = [m.sb(f"v{b}", [P, 2, W]) for b in range(2)]
        v_rest = [m.sb(f"v_rest{b}", [P, 2, W]) for b in range(2)]
        z_step = [m.sb(f"z_step{b}", [P, G, 2, 2]) for b in range(2)]
        exp_min = m.sb("exp_min", [P, 2, W])
        memory = m.sb("memory", [P, G, DH + 1])
        probs = m.sb("probs", [P, G, P])
        row_max, neg_max = m.sb("row_max", [P, G]), m.sb("neg_max", [P, G])
        row_sum, inv_sum = m.sb("row_sum", [P, G]), m.sb("inv_sum", [P, G])
        probs_t = m.sb("probs_t", [P, G, P])
        sigma_k = m.sb("sigma_k", [P, G, DH])
        inv_den = m.sb("inv_den", [P, 2, 2])
        neg_delta = m.sb("neg_delta", [P, G, DH])
        from_memory, weighted_memory, att = (m.sb(n, [P, W]) for n in ("from_memory", "weighted_memory", "att"))
        att_hi, att_lo = m.sb("att_hi", [P, HEADS, P], F32R), m.sb("att_lo", [P, HEADS, P], F32R)
        y_stage = m.sb("y_stage", [P, D])

        proj_ps = m.ps("proj_ps", [P, 2, W])
        scores_ps = m.ps("scores_ps", [P, G, P])
        out_ps = m.ps("out_ps", [P, W])
        turn_ps = m.ps("turn_ps", [P, G, P])
        read_ps = m.ps("read_ps", [P, 2, 512])
        update_ps = m.ps("update_ps", [P, G, DH])

        w_loaded, betas_loaded = Beat(m, "w_loaded", 48), m.sem("betas_loaded")
        o_loaded, o_hi_ready, o_lo_ready = m.sem("o_loaded"), m.sem("o_hi_ready"), m.sem("o_lo_ready")
        w_hi, w_lo = Beat(m, "w_hi", 3), Beat(m, "w_lo", 3)
        beta_steps, betas_stored = m.sem("beta_steps"), m.sem("betas_stored")
        beta_loaded, beta_rest_loaded = Beat(m, "beta_loaded", 16), Beat(m, "beta_rest_loaded", 16)
        mask_steps = m.sem("mask_steps")
        pool_passed, dve_passed = m.sem("pool_passed"), m.sem("dve_passed")
        memory_reset = m.sem("memory_reset")
        keyed = Beat(m, "keyed")
        projected = Beat(m, "projected", UNITS)
        raw_copied = Beat(m, "raw_copied", 4)
        relued, exped = Beat(m, "relued", 4), Beat(m, "exped", 4)
        sigma_ready, z_ready = Beat(m, "sigma_ready", 4), Beat(m, "z_ready", 2)
        keys_copied = Beat(m, "keys_copied", 2)
        v_ready, v_rest_ready = Beat(m, "v_ready", 2), Beat(m, "v_rest_ready", 2)
        scored = Beat(m, "scored")
        max_ready, neg_ready = Beat(m, "max_ready"), Beat(m, "neg_ready")
        probs_ready, probs_turned, probs_t_ready = Beat(m, "probs_ready"), Beat(m, "probs_turned"), Beat(m, "probs_t_ready")
        sigma_turned, sigma_k_ready = Beat(m, "sigma_turned"), Beat(m, "sigma_k_ready")
        retrieved, den_ready = Beat(m, "retrieved", 2), Beat(m, "den_ready", 2)
        delta_ready, from_memory_ready = Beat(m, "delta_ready", 2), Beat(m, "from_memory_ready", 2)
        memory_weighted = Beat(m, "memory_weighted")
        updated, memory_ready = Beat(m, "updated", 2), Beat(m, "memory_ready", 2)
        attended, inv_sum_ready, att_ready = Beat(m, "attended"), Beat(m, "inv_sum_ready"), Beat(m, "att_ready")
        att_turned, att_hi_ready, att_lo_ready = (Beat(m, n) for n in ("att_turned", "att_hi_ready", "att_lo_ready"))
        y_ready, y_copied, y_stored = Beat(m, "y_ready"), Beat(m, "y_copied"), Beat(m, "y_stored", 16)

        raw_o = [sigma[b][:].rearrange("p h t c -> p (h t c)").rearrange("p (j n) -> p j n", n=D) for b in range(2)]

        KINDS = ("k", "q", "v", "k", "q", "v")
        EVEN, ODD = 0, 1
        Q_ROWS = {EVEN: slice(0, SEG), ODD: slice(SEG, P)}
        K_ROWS = {EVEN: slice(SEG, P), ODD: slice(0, SEG)}
        SIGMA_OF = {EVEN: slice(P, 2 * P), ODD: slice(0, P)}
        ROWS = 2 * G * STRIPS
        LAST_Q, LAST_N = GROUPS * QUADS - 1, GROUPS * PAIRS - 1

        class Pair:

            def __init__(self, g, i, b, p, kind):
                self.g, self.b, self.p, self.slot = g, b, p, 2 * b + p
                self.q = g * QUADS + i
                self.h, self.n = self.q * 2 + b, self.q * 4 + self.slot
                ends = kind in ("switch", "last")
                self.c = i * 2 + b
                self.c1 = 0 if ends and b == 1 else self.c + 1
                self.c2 = b if ends else self.c + 2
                self.first = kind == "first" and self.slot == 0
                self.switch = kind == "switch" and b == 1
                self.has_next_half = not (kind == "last" and b == 1)
                self.has_second_next = kind != "last"
                self.has_next_pair = not (kind == "last" and self.slot == 3)
                self.group_ends = ends and self.slot == 3
                self.next_h, self.next_b = (self.h, b) if p == 0 else (self.h + 1, 1 - b)
                self.quad_before = self.q - 1 if self.slot == 0 else self.q

        def pairs(eng, pair):
            def body(g, i, kind):
                for b in range(2):
                    for p in range(2):
                        pair(Pair(g, i, b, p, kind))
            def middle(g):
                with eng.Fori(1, QUADS - 1) as i:
                    body(g, i, "middle")
            body(0, 0, "first")
            with eng.Fori(0, GROUPS - 1) as g:
                middle(g)
                body(g, QUADS - 1, "switch")
                body(g + 1, 0, "middle")
            middle(GROUPS - 1)
            body(GROUPS - 1, QUADS - 1, "last")

        def turned_rows():
            return turn_ps[:].rearrange("p a b -> p (a b)").rearrange("p (r j) -> p j r", j=HEADS)

        block = m.start()

        @block.sync
        def _(sp):
            for s in (w_loaded, y_stored, beta_loaded, beta_rest_loaded):
                s.credit(sp)

            def load_weights(g):
                for src, dst in zip((w_k, w_q, w_v), raw):
                    sp.dma_start(dst[:], src[:, cols(g, W)].rearrange("(k p) n -> p k n", p=P)).then_inc(w_loaded.sem, 16)

            def load_beta(g, which, dst, loaded):
                sp.dma_start(dst[:], sigmoids[cols(g, G), which, :].rearrange("h (a d) -> a h d", a=1).to_broadcast([P, G, DH])
                             ).then_inc(loaded.sem, 16)

            def store_y(g, i):
                y_copied.wait(sp, g * QUADS + i)
                sp.dma_start(y_out.rearrange("(t r) d -> t r d", r=SEG)[:, bass.ds(g * (G * STRIPS), G * STRIPS), :][cols(i, 8), :, :],
                             y_stage[:]).then_inc(y_stored.sem, 16)

            sp.sem_inc(w_loaded.sem, w_loaded.per)
            sp.dma_start(beta_heads[:, 0, :], betas.rearrange("a h b d -> (a h) (b d)")).then_inc(betas_loaded, 16)
            for i in range(2):
                sp.dma_start(raw_o[i], w_o[i * (HEADS // 2) * P:(i + 1) * (HEADS // 2) * P, :].rearrange("(j p) n -> p j n", p=P)
                             ).then_inc(o_loaded, 16)
            sp.wait_ge(beta_steps, 4)
            sp.dma_start(sigmoids, beta_heads[:]).then_inc(betas_stored, 16)
            sp.wait_ge(betas_stored, 16)
            load_beta(0, 1, beta_rest, beta_rest_loaded)
            load_beta(0, 0, beta, beta_loaded)

            with sp.Fori(0, GROUPS - 1) as g:
                w_lo.wait(sp, g)
                load_weights(g + 1)
                with sp.Fori(0, QUADS - 1) as i:
                    store_y(g, i)
                v_rest_ready.wait(sp, g * HALVES + (HALVES - 1))
                load_beta(g + 1, 1, beta_rest, beta_rest_loaded)
                memory_weighted.wait(sp, g * PAIRS + (PAIRS - 1))
                load_beta(g + 1, 0, beta, beta_loaded)
                store_y(g, QUADS - 1)
            with sp.Fori(0, QUADS) as i:
                store_y(GROUPS - 1, i)
            y_stored.wait(sp, LAST_Q)

        @block.gpsimd
        def _(pool):
            for s in (keyed, v_rest_ready, memory_weighted):
                s.credit(pool)

            def key_order(h, c, b, part):
                src, dst = ((core.xt_hi, keyed_hi[b]), (core.xt_lo, keyed_lo[b]))[part]
                s = src[:, :, cols(c, HALF)].rearrange("p k (t s c) -> p k t s c", t=2, s=2)
                d = dst[:].rearrange("p k (t s c) -> p k t s c", t=2, s=2)
                for k in range(KD):
                    for seg in range(2):
                        last = pool.tensor_copy(d[:, k, :, 1 - seg, :], s[:, k, :, seg, :].bitcast(F32))
                if part == 1:
                    last.then_inc(keyed.sem, 1)

            def weigh_values(h, b, p):
                v_ready.wait(pool, h, p + 1)
                pool.tensor_tensor(v_rest[b][:, p, :], v[b][:, p, :], beta_rest[:], ALU.mult).then_inc(v_rest_ready.sem, 1)

            for h in range(2):
                for part in range(2):
                    key_order(h, h, h, part)
            pool.memset(mask[:], 0.0).then_inc(mask_steps, 1)
            pool.wait_ge(mask_steps, 1)
            pool.affine_select(out=mask[:, 0:SEG], in_=mask[:, 0:SEG], compare_op=ALU.is_ge, fill=NEG, base=-SEG,
                               pattern=[[-1, SEG]], channel_multiplier=1).then_inc(mask_steps, 1)
            pool.affine_select(out=mask[:, SEG:P], in_=mask[:, SEG:P], compare_op=ALU.is_ge, fill=NEG, base=0,
                               pattern=[[-1, SEG]], channel_multiplier=1).then_inc(mask_steps, 1)
            pool.wait_ge(mask_steps, 3)
            pool.affine_select(out=mask[:, SEG:P], in_=mask[:, SEG:P], compare_op=ALU.is_ge, fill=NEG, base=SEG - 1,
                               pattern=[[0, SEG]], channel_multiplier=-1).then_inc(mask_steps, 1)
            beta_rest_loaded.wait(pool, 0)
            for p in range(2):
                weigh_values(0, 0, p)

            def pair(x):
                if x.has_second_next:
                    if x.p == 0:
                        projected.wait_alone(pool, pool_passed, x.h)
                    key_order(x.h + 2, x.c2, x.b, x.p)
                from_memory_ready.wait(pool, x.n)
                att_ready.wait_before(pool, x.n)
                if (x.c == 0 if isinstance(x.c, int) else False) and x.slot == 0:
                    beta_loaded.wait(pool, x.g)
                pool.tensor_tensor(weighted_memory[:], from_memory[:], beta[:], ALU.mult).then_inc(memory_weighted.sem, 1)
                if x.has_next_half:
                    if x.switch and x.p == 0:
                        beta_rest_loaded.wait(pool, x.g + 1)
                    weigh_values(x.h + 1, 1 - x.b, x.p)

            pairs(pool, pair)

        @block.tensor
        def _(pe):
            for s in (projected, scored, retrieved, updated, sigma_turned, probs_turned, att_turned, attended, y_ready):
                s.credit(pe)

            def unit(h, c, b, u):
                bank = proj_ps[:, u % 2, :]
                if u == 0:
                    keyed.wait(pe, h)
                before = (u - 2) % UNITS
                turn = h if u >= 2 else h - 1
                if KINDS[before] == "v":
                    v_ready.wait(pe, turn, before // 3 + 1)
                else:
                    sigma_ready.wait(pe, turn, 2 * (before // 3) + before % 3 + 1)
                kind, half = KINDS[u], u // 3
                w_h, w_l = hi["kqv".index(kind)], lo["kqv".index(kind)]
                if kind == "v":
                    at = slice(half * P, (half + 1) * P)
                    for k in range(KD):
                        for i, (x, w) in enumerate(((keyed_hi, w_h), (keyed_hi, w_l), (keyed_lo, w_h))):
                            last = pe.matmul(bank, x[b][:, k, at], w[:, k, :], start=(k == 0 and i == 0),
                                             stop=(k == KD - 1 and i == 2))
                else:
                    if kind == "k":
                        x_h, x_l = (lambda k: keyed_hi[b][:, k, :]), (lambda k: keyed_lo[b][:, k, :])
                    else:
                        x_h = lambda k: core.xt_hi[:, k, cols(c, HALF)]
                        x_l = lambda k: core.xt_lo[:, k, cols(c, HALF)]
                    for a in range(2):
                        head = slice((2 * half + a) * DH, (2 * half + a + 1) * DH)
                        for k in range(KD):
                            for i, (w, x) in enumerate(((w_h, x_h), (w_h, x_l), (w_l, x_h))):
                                last = pe.matmul(bank[:, a * HALF:(a + 1) * HALF], w[:, k, head], x(k),
                                                 start=(k == 0 and i == 0), stop=(k == KD - 1 and i == 2))
                last.then_inc(projected.sem, 1)

            def score(n, h, b, p):
                if p == 0:
                    raw_copied.wait(pe, h)
                max_ready.wait_before(pe, n)
                for hh in range(G):
                    mm = pe.matmul(scores_ps[:, hh, :], q_t[b][:, hh, p, :], k_t[b][:, hh, p, :], start=True, stop=True)
                mm.then_inc(scored.sem, 1)

            def turn_sigma(n, h, b, p):
                if p == 0:
                    keys_copied.wait(pe, h)
                probs_t_ready.wait_before(pe, n)
                for hh in range(G):
                    mm = pe.transpose(turn_ps[:, hh, :], sigma_kt[b][:, hh, p, :], core.ident[:])
                mm.then_inc(sigma_turned.sem, 1)

            def retrieve(x, seg):
                if seg == EVEN:
                    memory_ready.wait_before(pe, x.n)
                    from_memory_ready.wait_before(pe, x.n)
                else:
                    memory_ready.wait(pe, x.n, 1)
                    from_memory_ready.wait(pe, x.n, 1)
                for h in range(G):
                    last = pe.matmul(read_ps[:, h // 2, (h % 2) * (DH + 1):(h % 2 + 1) * (DH + 1)],
                                     sigma[x.b][:, h, x.p, SIGMA_OF[seg]], memory[:, h, :], start=True, stop=True)
                last.then_inc(retrieved.sem, 1)

            def update(n, seg):
                if seg == EVEN:
                    sigma_k_ready.wait(pe, n)
                delta_ready.wait(pe, n, seg + 1)
                rows = K_ROWS[seg]
                for h in range(G):
                    last = pe.matmul(update_ps[:, h, :], sigma_k[rows, h, :], neg_delta[rows, h, :], start=True, stop=True)
                last.then_inc(updated.sem, 1)

            def turn_att(n):
                att_ready.wait(pe, n)
                for h in range(G):
                    out = turn_ps[:].rearrange("p a b -> p (a b)").rearrange("p (s h c) -> p h s c", s=2, h=G)[:, h, :, :]
                    last = pe.transpose(out, att[:, h * DH:(h + 1) * DH], core.ident[:])
                last.then_inc(att_turned.sem, 1)

            def project_out(q, js):
                if js.start == 0:
                    att_lo_ready.wait(pe, q * 4 + 3)
                for j in js:
                    for i, (a, w) in enumerate(((att_hi, o_hi), (att_hi, o_lo), (att_lo, o_hi))):
                        last = pe.matmul(out_ps[:, 0:D], a[:, j, :], w[:, j, :], start=(j == 0 and i == 0),
                                         stop=(j == HEADS - 1 and i == 2))
                if js.stop == HEADS:
                    last.then_inc(y_ready.sem, 1)

            w_lo.wait(pe, 0)
            for u in range(UNITS):
                unit(0, 0, 0, u)
            score(0, 0, 0, 0)
            turn_sigma(0, 0, 0, 0)
            pe.wait_ge(memory_reset, 1)

            def pair(x):
                def next_unit(u):
                    if x.has_next_half:
                        if x.switch and x.p == 0:
                            w_lo.wait(pe, x.g + 1, u + 1)
                        unit(x.h + 1, x.c1, 1 - x.b, 3 * x.p + u)

                project = x.slot == 0 and not x.first
                if x.p == 0:
                    sigma_ready.wait(pe, x.h)
                retrieve(x, EVEN)
                next_unit(0)
                if not x.first:
                    sigma_k_ready.wait(pe, x.n)
                    turn_att(x.n - 1)
                update(x.n, EVEN)
                next_unit(1)
                retrieve(x, ODD)
                if project:
                    project_out(x.q - 1, range(0, HEADS // 2))
                probs_ready.wait(pe, x.n)
                att_lo_ready.wait_before(pe, x.n)
                sigma_k_ready.wait(pe, x.n)
                for hh in range(G):
                    mm = pe.transpose(turn_ps[:, hh, :], probs[:, hh, :], core.ident[:])
                mm.then_inc(probs_turned.sem, 1)
                if project:
                    project_out(x.q - 1, range(HEADS // 2, HEADS))
                next_unit(2)
                if x.has_next_pair:
                    score(x.n + 1, x.next_h, x.next_b, 1 - x.p)
                update(x.n, ODD)
                if x.has_next_pair:
                    turn_sigma(x.n + 1, x.next_h, x.next_b, 1 - x.p)
                probs_t_ready.wait(pe, x.n)
                if x.p == 0:
                    v_rest_ready.wait(pe, x.h)
                if x.slot == 0:
                    y_copied.wait_before(pe, x.q)
                for hh in range(G):
                    head = slice(hh * DH, (hh + 1) * DH)
                    mm = pe.matmul(out_ps[:, head], probs_t[:, hh, :], v_rest[x.b][:, x.p, head], start=True, stop=True)
                mm.then_inc(attended.sem, 1)

            pairs(pe, pair)
            turn_att(LAST_N)
            project_out(LAST_Q, range(0, HEADS))

        @block.scalar
        def _(act):
            for s in (y_copied, w_hi, raw_copied, relued, exped, v_ready, probs_ready, probs_t_ready, sigma_k_ready,
                      att_hi_ready, from_memory_ready):
                s.credit(act)

            def split_weights(g, i):
                if i == 0:
                    w_loaded.wait(act, g)
                act.activation(hi[i][:], raw[i][:], ACT.Copy).then_inc(w_hi.sem, 1)

            def unit(h, b, u):
                projected.wait(act, h, u + 1)
                bank = proj_ps[:, u % 2, :]
                kind, half = KINDS[u], u // 3
                if kind == "v":
                    act.activation(v[b][:, half, :], bank, ACT.Copy).then_inc(v_ready.sem, 1)
                    return
                s = 2 * half + u % 3
                dst = (k_t if kind == "k" else q_t)[b]
                act.activation(dst[:, 2 * half:2 * half + 2, :, :].rearrange("p h t c -> p (h t c)"), bank,
                               ACT.Copy).then_inc(raw_copied.sem, 1)
                sigma_ready.wait(act, h if s >= 2 else h - 1, (s - 2) % 4 + 1)
                act.activation(exp_min[:, s % 2, :], bank, ACT.Relu, scale=-1.0).then_inc(relued.sem, 1)
                relued.wait(act, h, s + 1)
                act.activation(exp_min[:, s % 2, :], exp_min[:, s % 2, :], ACT.Exp, scale=-1.0).then_inc(exped.sem, 1)

            def retrieval(n, seg):
                den_ready.wait(act, n, seg + 1)
                if seg == EVEN:
                    memory_weighted.wait_before(act, n)
                rows = Q_ROWS[seg]
                for h in range(G):
                    at = (h % 2) * (DH + 1)
                    last = act.activation(from_memory[rows, h * DH:(h + 1) * DH], read_ps[rows, h // 2, at:at + DH], ACT.Copy,
                                          scale=inv_den[rows, h // 2, h % 2:h % 2 + 1])
                last.then_inc(from_memory_ready.sem, 1)

            def att_part(n, q, slot):
                if slot == 0:
                    y_ready.wait_before(act, q)
                att_turned.wait(act, n)
                act.activation(att_hi[:, :, slot * ROWS:(slot + 1) * ROWS], turned_rows(),
                               ACT.Copy).then_inc(att_hi_ready.sem, 1)

            def copy_y(q):
                y_ready.wait(act, q)
                y_stored.wait_before(act, q)
                act.activation(y_stage[:], out_ps[:, 0:D], ACT.Copy).then_inc(y_copied.sem, 1)

            for i in range(3):
                split_weights(0, i)
            act.wait_ge(betas_loaded, 16)
            act.activation(beta_heads[:, 0, :], beta_heads[:, 0, :], ACT.Exp, scale=-1.0).then_inc(beta_steps, 1)
            act.wait_ge(o_loaded, 32)
            for i in range(2):
                act.activation(o_hi[:, i * (HEADS // 2):(i + 1) * (HEADS // 2), :], raw_o[i], ACT.Copy).then_inc(o_hi_ready, 1)
            for u in range(UNITS):
                unit(0, 0, u)

            def pair(x):
                def next_unit(u):
                    if x.has_next_half:
                        unit(x.h + 1, 1 - x.b, 3 * x.p + u)

                if x.switch and x.p == 0:
                    projected.wait(act, x.h)
                    split_weights(x.g + 1, 0)
                sigma_turned.wait(act, x.n)
                act.activation(sigma_k[:], turn_ps[:], ACT.Copy).then_inc(sigma_k_ready.sem, 1)
                neg_ready.wait(act, x.n)
                for hh in range(G):
                    e = act.activation(probs[:, hh, :], probs[:, hh, :], ACT.Exp, bias=neg_max[:, hh:hh + 1],
                                       accum_out=row_sum[:, hh:hh + 1])
                e.then_inc(probs_ready.sem, 1)
                retrieval(x.n, EVEN)
                if x.switch and x.p == 0:
                    split_weights(x.g + 1, 1)
                next_unit(0)
                if not x.first:
                    att_part(x.n - 1, x.quad_before, (x.slot - 1) % 4)
                if x.switch and x.p == 0:
                    split_weights(x.g + 1, 2)
                next_unit(1)
                retrieval(x.n, ODD)
                probs_turned.wait(act, x.n)
                act.activation(probs_t[:], turn_ps[:], ACT.Copy).then_inc(probs_t_ready.sem, 1)
                if x.slot == 0 and not x.first:
                    copy_y(x.q - 1)
                next_unit(2)

            pairs(act, pair)
            att_part(LAST_N, LAST_Q, 3)
            copy_y(LAST_Q)

        @block.vector
        def _(dve):
            for s in (w_lo, sigma_ready, z_ready, keys_copied, max_ready, neg_ready, den_ready, delta_ready,
                      memory_ready, inv_sum_ready, att_ready, att_lo_ready):
                s.credit(dve)

            def split_weights(g, i):
                w_hi.wait(dve, g, i + 1)
                dve.tensor_tensor(lo[i][:], raw[i][:], hi[i][:].bitcast(F32), ALU.subtract).then_inc(w_lo.sem, 1)

            def unit(h, b, u):
                kind, half = KINDS[u], u // 3
                if kind == "v":
                    return
                s = 2 * half + u % 3
                exped.wait(dve, h, s + 1)
                heads = slice(2 * half, 2 * half + 2)
                x = proj_ps[:, u % 2, :].rearrange("p (ht s c) -> p ht s c", s=2, c=SEG)
                e = exp_min[:, s % 2, :].rearrange("p (ht s c) -> p ht s c", s=2, c=SEG)
                out = sigma[b][:, heads, :, :].rearrange("p h t (s c) -> p (h t) s c", c=SEG)
                for seg in (EVEN, ODD):
                    to = 3 * seg if kind == "k" else 2 - seg
                    last = dve.scalar_tensor_tensor(out=out[:, :, to, :], in0=x[:, :, seg, :], scalar=0.0,
                                                    in1=e[:, :, seg, :], op0=ALU.max, op1=ALU.add)
                last.then_inc(sigma_ready.sem, 1)
                if kind == "k":
                    keys = out[:, :, 0:4:3, :]
                    sigma_ready.wait(dve, h, s + 1)
                    dve.tensor_copy(sigma_kt[b][:, heads, :, :].rearrange("p h t (s c) -> p (h t) s c", c=SEG),
                                    keys).then_inc(keys_copied.sem, 1)
                    dve.reduce_sum(z_step[b][:, heads, :, :].rearrange("p h t s -> p (h t) s"), keys,
                                   AX_X).then_inc(z_ready.sem, 1)

            def retrieval(x, seg):
                retrieved.wait(dve, x.n, seg + 1)
                dve.reciprocal(inv_den[:], read_ps[:, :, DH:2 * (DH + 1):DH + 1]).then_inc(den_ready.sem, 1)
                den_ready.wait(dve, x.n, seg + 1)
                rows = K_ROWS[seg]
                for h in range(G):
                    at = (h % 2) * (DH + 1)
                    last = dve.scalar_tensor_tensor(out=neg_delta[rows, h, :], in0=read_ps[rows, h // 2, at:at + DH],
                                                    scalar=inv_den[rows, h // 2, h % 2:h % 2 + 1],
                                                    in1=v[x.b][rows, x.p, h * DH:(h + 1) * DH], op0=ALU.mult, op1=ALU.subtract)
                last.then_inc(delta_ready.sem, 1)

            def reset_memory():
                dve.memset(memory[:, :, 0:DH], 0.0)
                return dve.memset(memory[:, :, DH], 1.0 / DH)

            def update(x, seg):
                updated.wait(dve, x.n, seg + 1)
                if seg == ODD and x.group_ends:
                    reset_memory().then_inc(memory_ready.sem, 1)
                else:
                    dve.tensor_tensor(memory[:, :, 0:DH], memory[:, :, 0:DH], update_ps[:], ALU.subtract)
                    z = memory[:, :, DH]
                    dve.tensor_tensor(z, z, z_step[x.b][:, :, x.p, 1 - seg], ALU.add).then_inc(memory_ready.sem, 1)

            def score_max(n):
                scored.wait_alone(dve, dve_passed, n)
                for hh in range(G):
                    t = dve.tensor_tensor_reduce(probs[:, hh, :], scores_ps[:, hh, :], mask[:], DH ** -0.5, NEG,
                                                 ALU.add, ALU.max, row_max[:, hh:hh + 1])
                t.then_inc(max_ready.sem, 1)
                max_ready.wait(dve, n)
                dve.tensor_scalar(neg_max[:], row_max[:], -1.0, None, ALU.mult).then_inc(neg_ready.sem, 1)

            def mix(n):
                inv_sum_ready.wait(dve, n)
                attended.wait(dve, n)
                memory_weighted.wait(dve, n)
                for hh in range(G):
                    head = slice(hh * DH, (hh + 1) * DH)
                    t = dve.scalar_tensor_tensor(out=att[:, head], in0=out_ps[:, head], scalar=inv_sum[:, hh:hh + 1],
                                                 in1=weighted_memory[:, head], op0=ALU.mult, op1=ALU.add)
                t.then_inc(att_ready.sem, 1)

            def att_part(n, slot):
                att_hi_ready.wait(dve, n)
                columns = slice(slot * ROWS, (slot + 1) * ROWS)
                dve.tensor_tensor(att_lo[:, :, columns], turned_rows(), att_hi[:, :, columns].bitcast(F32),
                                  ALU.subtract).then_inc(att_lo_ready.sem, 1)

            reset_memory().then_inc(memory_reset, 1)
            for i in range(3):
                split_weights(0, i)
            dve.wait_ge(beta_steps, 1)
            dve.tensor_scalar(beta_heads[:, 0, :], beta_heads[:, 0, :], 1.0, None, ALU.add).then_inc(beta_steps, 1)
            dve.wait_ge(beta_steps, 2)
            dve.reciprocal(beta_heads[:, 0, :], beta_heads[:, 0, :]).then_inc(beta_steps, 1)
            dve.wait_ge(beta_steps, 3)
            dve.tensor_scalar(beta_heads[:, 1, :], beta_heads[:, 0, :], -1.0, 1.0, ALU.mult, ALU.add).then_inc(beta_steps, 1)
            for i in range(2):
                dve.wait_ge(o_hi_ready, i + 1)
                part = slice(i * (HEADS // 2), (i + 1) * (HEADS // 2))
                dve.tensor_tensor(o_lo[:, part, :], raw_o[i], o_hi[:, part, :].bitcast(F32), ALU.subtract).then_inc(o_lo_ready, 1)
            dve.wait_ge(o_lo_ready, 2)
            dve.wait_ge(mask_steps, 4)
            for u in range(UNITS):
                unit(0, 0, u)
            score_max(0)

            def pair(x):
                def next_unit(u):
                    if x.has_next_half:
                        unit(x.h + 1, 1 - x.b, 3 * x.p + u)

                def next_weights(i):
                    if x.switch and x.p == 0:
                        split_weights(x.g + 1, i)

                if not x.first:
                    mix(x.n - 1)
                next_weights(0)
                retrieval(x, EVEN)
                next_weights(1)
                update(x, EVEN)
                if not x.first:
                    att_part(x.n - 1, (x.slot - 1) % 4)
                next_unit(0)
                next_weights(2)
                retrieval(x, ODD)
                next_unit(1)
                probs_ready.wait(dve, x.n)
                dve.reciprocal(inv_sum[:], row_sum[:]).then_inc(inv_sum_ready.sem, 1)
                if x.has_next_pair:
                    score_max(x.n + 1)
                update(x, ODD)

            pairs(dve, pair)
            mix(LAST_N)
            att_part(LAST_N, 3)

def phase_residual(nc, core, x_in, y_in, ffn_weights, name):
    with ExitStack() as ctx:
        m = Mem(nc, ctx, name)
        post, pre, turn = Stats(m, "post"), Stats(m, "pre"), Turn(m, core)
        ffn_weights.prepare_in(m, first_chunk=0)
        y, y_normed = m.sb("y", [P, TILES, D]), m.sb("y_normed", [P, R, D])
        loaded = [m.sem(f"loaded{c}") for c in range(CHUNKS)]
        y_read, x_updated = m.sem("y_read"), m.sem("x_updated")
        block = m.start()

        @block.sync
        def _(sp):
            for c in range(CHUNKS):
                for src, dst in ((y_in, y), (x_in[0], core.x)):
                    sp.dma_start(dst[:, c * R:(c + 1) * R, :],
                                 src[c * CHUNK:(c + 1) * CHUNK, :].rearrange("(a p) d -> p a d", p=P)).then_inc(loaded[c], 16)
                if c < 3:
                    ffn_weights.load(sp, c)

        @block.vector
        def _(dve):
            def begin(c):
                if c < CHUNKS:
                    dve.wait_ge(loaded[c], 32)
                    post.dve_variance(dve, lambda r: y[:, c * R + r, :], c)

            begin(0)
            for c in range(CHUNKS):
                y_tile = lambda r: y[:, c * R + r, :]
                post.dve_rstd(dve, c)
                post.dve_normalise(dve, lambda r: y_normed[:, r, :], y_tile).then_inc(y_read, 1)
                dve.wait_ge(y_read, c + 1)
                dve.tensor_tensor(core.x_chunk(c), core.x_chunk(c), y_normed[:].rearrange("p a d -> p (a d)"),
                                  ALU.add).then_inc(x_updated, 1)
                dve.wait_ge(x_updated, c + 1)
                pre.dve_variance(dve, core.x_tile(c), c)
                if c > 0:
                    turn.dve_lo(dve, c - 1, c - 1)
                begin(c + 1)
                ffn_weights.dve(dve, c, 0)
                pre.dve_rstd(dve, c)
                reach(dve, turn.turned_ready, KD * c)
                pre.dve_normalise(dve, lambda r: turn.xn[:, r, :], core.x_tile(c)).then_inc(turn.xn_ready, 1)
                ffn_weights.dve(dve, c, 1)
            turn.dve_lo(dve, CHUNKS - 1, CHUNKS - 1)

        @block.scalar
        def _(act):
            post.act_std(act, 0)
            for c in range(CHUNKS):
                pre.act_std(act, c)
                if c + 1 < CHUNKS:
                    post.act_std(act, c + 1)
                ffn_weights.act(act, c, 0)
                ffn_weights.act(act, c, 1)
                turn.act_hi(act, c, c)

        @block.tensor
        def _(pe):
            for c in range(CHUNKS):
                for place in range(ffn_weights.PLACES):
                    ffn_weights.pe(pe, c, place)
                turn.pe_turn(pe, c)



H1 = 16
HD = 16
QB = (T // P)
TERMS = ((0, 0), (0, 1), (1, 0), (0, 2), (2, 0), (1, 1))
MAX_ROW = HD * len(TERMS)
STACK = MAX_ROW + 3
PARTS = 3


class Stacks:
    LOADS = 16 * 2 * len(TERMS)
    AHEAD = 2

    def __init__(self, nc, ctx, q_parts, k_parts):
        m = Mem(nc, ctx, "stacks")
        self.q = m.sb("q", [P, 2, CHUNKS, G, CHUNK], BF16)
        self.k = m.sb("k", [P, 2, G, T], BF16)
        self.q_parts, self.k_parts = q_parts, k_parts

    def load(self, eng, g, c, chunks, loaded):
        for t, (q_part, k_part) in enumerate(TERMS):
            at = slice(t * HD, (t + 1) * HD)
            eng.dma_start(self.q[at, g % 2, bass.ds(c, chunks), :, :].rearrange("d c h n -> d c (h n)"),
                          self.q_parts[q_part, :, bass.ds(c, chunks), g * G:(g + 1) * G, :].rearrange("d c h n -> d c (h n)")
                          ).then_inc(loaded, 16)
            eng.dma_start(self.k[at, g % 2, :, bass.ds(c * CHUNK, chunks * CHUNK)],
                          self.k_parts[k_part, g * G * HD:(g + 1) * G * HD, bass.ds(c * CHUNK, chunks * CHUNK)]
                          .rearrange("(h d) n -> d h n", d=HD)).then_inc(loaded, 16)


def phase_qkv(nc, core, values, weights, b_qkv, q_parts, k_parts, stacks):
    NB = 3 * D // P
    QK = 4
    with ExitStack() as ctx:
        m = Mem(nc, ctx, "qkv")
        raw, = weights.tiles
        w_hi, w_lo = m.sb("w_hi", [P, KD, NB * P], F32R), m.sb("w_lo", [P, KD, NB * P], F32R)
        bias = m.sb("bias", [P, NB])
        biased = m.sb("biased", [P, NB, CHUNK])
        rest = m.sb("rest", [P, QK, CHUNK])
        parts = m.sb("parts", [P, QK, PARTS, CHUNK], BF16)
        qkv_ps = m.ps("qkv_ps", [P, NB, CHUNK])
        v_ps = m.ps("v_ps", [P, 2, CHUNK])

        bias_loaded = m.sem("bias_loaded")
        projected, biased_ready = m.sem("projected"), m.sem("biased_ready")
        part0_ready, rest_ready, part1_ready, part2_ready = (m.sem(s) for s in ("part0_ready", "rest_ready", "part1_ready", "part2_ready"))
        stored = [m.sem(f"stored{j}") for j in range(QK)]
        stacked = m.sem("stacked")
        v_turned, v_copied = m.sem("v_turned"), m.sem("v_copied")
        STORES = (16 * PARTS, 16 * PARTS, 16, 16)
        units = [([raw[:, j, k * P:(k + 1) * P] for j in range(j0, j0 + 3)], w_hi[:, k, j0 * P:(j0 + 3) * P],
                  w_lo[:, k, j0 * P:(j0 + 3) * P], 0) for k in range(KD) for j0 in (0, 3)]
        turning = TurnWeights(m, core, lambda u: v_ps[:, u % 2, :], units)
        block = m.start()

        @block.sync
        def _(sp):
            with nc.allow_non_contiguous_dma(reason="one bias per partition"):
                sp.dma_start(bias[:], b_qkv.rearrange("(j p) -> p j", p=P)).then_inc(bias_loaded, 16)
            def chunk(n):
                for j in range(QK):
                    sp.wait_ge(part2_ready, QK * n + j + 1)
                    if j < 2:
                        heads = slice(j * (H1 // 2), (j + 1) * (H1 // 2))
                        for part in range(PARTS):
                            sp.dma_start(q_parts[part, :, bass.ds(n, 1), heads, :].rearrange("d c h n -> (c h) d n"),
                                         parts[:, j, part, :]).then_inc(stored[j], 16)
                    else:
                        rows = slice((j % 2) * P, (j % 2 + 1) * P)
                        sp.dma_start(k_parts[:, rows, cols(n, CHUNK)].rearrange("a p n -> p a n"), parts[:, j, :, :]).then_inc(stored[j], 16)

            with sp.Fori(0, Stacks.AHEAD) as n:
                chunk(n)
                for j in range(QK):
                    sp.wait_ge(stored[j], STORES[j] * (n + 1))
                stacks.load(sp, 0, n, 1, stacked)
            for n in range(Stacks.AHEAD, CHUNKS):
                chunk(n)
            for j in range(QK):
                sp.wait_ge(stored[j], STORES[j] * CHUNKS)
            sp.wait_ge(stacked, Stacks.LOADS * Stacks.AHEAD)

        @block.tensor
        def _(pe):
            turning.pe(pe, lambda w: None)
            pe.wait_ge(turning.lo_ready, len(units))

            def turn_values(n, j):
                pe.wait_ge(biased_ready, NB * n + j + 1)
                reach(pe, v_copied, 2 * n + (j - QK) - 1)
                for r in range(R):
                    last = pe.transpose(v_ps[:, j - QK, r * P:(r + 1) * P], biased[:, j, r * P:(r + 1) * P], core.ident[:])
                last.then_inc(v_turned, 1)

            def chunk(n):
                for j in range(NB):
                    reach(pe, biased_ready, NB * n + j + 1 - NB)
                    for k in range(KD):
                        for i, (w, x) in enumerate(((w_hi, core.xt_hi), (w_hi, core.xt_lo), (w_lo, core.xt_hi))):
                            last = pe.matmul(qkv_ps[:, j, :], w[:, k, j * P:(j + 1) * P], x[:, k, cols(n, CHUNK)],
                                             start=(k == 0 and i == 0), stop=(k == KD - 1 and i == 2))
                    last.then_inc(projected, 1)
                for j in range(QK, NB):
                    turn_values(n, j)

            first_then_loop(pe, CHUNKS, chunk)

        @block.vector
        def _(dve):
            turning.dve(dve)
            dve.wait_ge(bias_loaded, 16)

            def chunk(n):
                for s in range(NB + 2):
                    if s < NB:
                        dve.wait_ge(projected, NB * n + s + 1)
                        if s < QK:
                            reach(dve, rest_ready, QK * n + s + 1 - QK)
                        else:
                            reach(dve, v_turned, 2 * n + (s - QK) + 1 - 2)
                        dve.tensor_scalar(biased[:, s, :], qkv_ps[:, s, :], bias[:, s:s + 1],
                                          HD ** -0.5 if s < 2 else 1.0, ALU.add, ALU.mult).then_inc(biased_ready, 1)
                    if 0 <= s - 1 < QK:
                        j = s - 1
                        dve.wait_ge(part0_ready, QK * n + j + 1)
                        dve.tensor_tensor(rest[:, j, :], biased[:, j, :], parts[:, j, 0, :], ALU.subtract).then_inc(rest_ready, 1)
                    if 0 <= s - 2 < QK:
                        j = s - 2
                        dve.wait_ge(part1_ready, QK * n + j + 1)
                        dve.tensor_tensor(parts[:, j, 2, :], rest[:, j, :], parts[:, j, 1, :], ALU.subtract).then_inc(part2_ready, 1)

            first_then_loop(dve, CHUNKS, chunk)

        @block.scalar
        def _(act):
            turning.act(act)

            def chunk(n):
                for s in range(QK + 1):
                    if s < QK:
                        act.wait_ge(biased_ready, NB * n + s + 1)
                        reach(act, stored[s], STORES[s] * n)
                        act.activation(parts[:, s, 0, :], biased[:, s, :], ACT.Copy).then_inc(part0_ready, 1)
                    if s > 0:
                        j = s - 1
                        act.wait_ge(rest_ready, QK * n + j + 1)
                        act.activation(parts[:, j, 1, :], rest[:, j, :], ACT.Copy).then_inc(part1_ready, 1)
                for j in range(2):
                    act.wait_ge(v_turned, 2 * n + j + 1)
                    act.activation(values[:, cols(n, R), j * P:(j + 1) * P], v_ps[:, j, :].rearrange("p (a d) -> p a d", a=R),
                                   ACT.Copy).then_inc(v_copied, 1)

            first_then_loop(act, CHUNKS, chunk)


def phase_attention(nc, core, att, values, stacks, ahead):
    GROUPS1 = H1 // G
    with ExitStack() as ctx:
        m = Mem(nc, ctx, "att")
        q_stack, k_stack = stacks.q, stacks.k
        v_ones = m.sb("v_ones", [P, 2, QB, G, 2 * HD])
        probs = m.sb("probs", [P, 2, 2, 2, CHUNK])
        causal = m.sb("causal", [P, P])
        masked = m.sb("masked", [P, 2, P])
        maxima = m.sb("maxima", [P, CHUNKS, G * R, 5])
        neg_max, row_max = m.sb("neg_max", [P, G * R]), m.sb("row_max", [P, G * R])
        max_rows = m.sb("max_rows", [G * R, P])
        max_rest = m.sb("max_rest", [G * R, 2, P])
        max_split = m.sb("max_split", [G * R, PARTS, P], BF16)
        out_t = m.sb("out_t", [P, CHUNK])
        out_rows = m.sb("out_rows", [P, CHUNK])
        inv_sum = m.sb("inv_sum", [P, R, G])

        keyed_ps = m.ps("keyed_ps", [P, 2, 2, CHUNK])
        rows_ps = m.ps("rows_ps", [P, 2, CHUNK])
        out_ps = m.ps("out_ps", [P, CHUNK])
        misc_ps = m.ps("misc_ps", [P, CHUNK])

        E_STEPS = [(g, c, kb) for g in range(GROUPS1) for c in range(CHUNKS) for kb in range(R * (c + 1))]
        M_STEPS = [(g, c, r, kc) for g in range(GROUPS1) for c in range(CHUNKS) for r in range(R) for kc in range(c + 1)]
        STEPS = len(E_STEPS)
        assert len(M_STEPS) == STEPS
        OF_GROUP = STEPS // GROUPS1
        LEAD = OF_GROUP // 2
        TURNS = STEPS + LEAD + 4
        ends = [s for s in range(STEPS) if s + 1 == STEPS or E_STEPS[s][:2] != E_STEPS[s + 1][:2]]
        diagonals = [s for s, (g, c, kb) in enumerate(E_STEPS) if kb >= R * c]

        MAX_LAG, OUT_LAG = 1, 3 + LEAD
        misc_uses = [[(what, ends.index(s)) for what, s in (("max", t - MAX_LAG), ("out", t - OUT_LAG)) if s in ends]
                     for t in range(TURNS)]
        assert all(len(uses) <= 1 for uses in misc_uses)
        order = [use for uses in misc_uses for use in uses]
        use_of = {use: i for i, use in enumerate(order)}

        stacks_loaded = [m.sem(f"stacks_loaded{i}") for i in range(2)]
        ahead.signal_in(m)
        max_loaded = m.sem("max_loaded")
        v_ones_ready = m.sem("v_ones_ready")
        rows_scored, rows_reduced = m.sem("rows_scored"), m.sem("rows_reduced")
        max_ready, neg_max_ready, max_turned = m.sem("max_ready"), m.sem("neg_max_ready"), m.sem("max_turned")
        split_steps, max_split_ready = m.sem("split_steps"), m.sem("max_split_ready")
        keyed_scored, exped = m.sem("keyed_scored"), m.sem("exped")
        triangled = m.sem("triangled")
        weighted = m.sem("weighted")
        out_copied, out_turned, inv_ready, out_ready = (m.sem(s) for s in ("out_copied", "out_turned", "inv_ready", "out_ready"))
        misc_read = m.sem("misc_read")
        prepared, ones_rows = m.sem("prepared"), m.sem("ones_rows")
        block = m.start()

        def off_of(s):
            g, c, kb = E_STEPS[s]
            return max(0, kb - R * c) * P

        @block.sync
        def _(sp):
            stacks.load(sp, 0, Stacks.AHEAD, CHUNKS - Stacks.AHEAD, stacks_loaded[0])
            stacks.load(sp, 1, 0, CHUNKS, stacks_loaded[1])
            ahead.load(sp)
            for k, end in enumerate(ends):
                g, c, kb = E_STEPS[end]
                sp.wait_ge(max_split_ready, k + 1)
                for part in range(PARTS):
                    sp.dma_start(q_stack[MAX_ROW + part:MAX_ROW + part + 1, g % 2, c, :, :].rearrange("a h n -> a (h n)"),
                                 max_split[:, part, :]).then_inc(max_loaded, 16)
                if c == 1 and g >= 1 and g + 1 < GROUPS1:
                    sp.wait_ge(weighted, OF_GROUP * g)
                    stacks.load(sp, g + 1, 0, CHUNKS, stacks_loaded[(g + 1) % 2])
            sp.wait_ge(max_loaded, 16 * PARTS * len(ends))
            ahead.finish(sp)

        @block.gpsimd
        def _(pool):
            pool.memset(causal[:], 0.0).then_inc(prepared, 1)
            pool.memset(maxima[:], NEG).then_inc(prepared, 1)
            pool.wait_ge(prepared, 2)
            pool.affine_select(out=causal[:], in_=causal[:], compare_op=ALU.is_ge, fill=NEG, base=0,
                               pattern=[[-1, P]], channel_multiplier=1).then_inc(prepared, 1)
            pool.wait_ge(prepared, 3)
            pool.memset(k_stack[MAX_ROW:P, :, :, :], 1.0).then_inc(ones_rows, 1)
            pool.wait_ge(ones_rows, 1)
            pool.memset(v_ones[:], 0.0).then_inc(prepared, 1)
            pool.wait_ge(prepared, 4)
            pool.memset(v_ones[:, :, :, :, HD:HD + 1], 1.0).then_inc(prepared, 1)
            pool.wait_ge(prepared, 5)

            def gather_values(g):
                reach(pool, weighted, OF_GROUP * (g - 1))
                pool.tensor_copy(v_ones[:, g % 2, :, :, 0:HD],
                                 values[:, :, g * G * HD:(g + 1) * G * HD].rearrange("p b (h d) -> p b h d", d=HD)
                                 ).then_inc(v_ones_ready, 1)

            gather_values(0)
            gather_values(1)
            def mask_step(s):
                for hp in range(2):
                    pool.wait_ge(exped, 2 * s + hp + 1)
                    block_ = probs[:, s % 2, hp, :, off_of(s):off_of(s) + P]
                    pool.affine_select(out=block_, in_=block_, compare_op=ALU.is_ge, fill=0.0, base=0,
                                       pattern=[[0, 2], [1, P]], channel_multiplier=-1).then_inc(triangled, 1)

            def split_max(k):
                STEPS_OF = 4
                pool.wait_ge(misc_read, use_of["max", k] + 1)
                reach(pool, max_loaded, 16 * PARTS * k)
                pool.tensor_copy(max_split[:, 0, :], max_rows[:]).then_inc(split_steps, 1)
                pool.wait_ge(split_steps, STEPS_OF * k + 1)
                pool.tensor_tensor(max_rest[:, 0, :], max_rows[:], max_split[:, 0, :], ALU.subtract).then_inc(split_steps, 1)
                pool.wait_ge(split_steps, STEPS_OF * k + 2)
                pool.tensor_copy(max_split[:, 1, :], max_rest[:, 0, :]).then_inc(split_steps, 1)
                pool.wait_ge(split_steps, STEPS_OF * k + 3)
                pool.tensor_tensor(max_rest[:, 1, :], max_rest[:, 0, :], max_split[:, 1, :], ALU.subtract).then_inc(split_steps, 1)
                pool.wait_ge(split_steps, STEPS_OF * k + 4)
                pool.tensor_copy(max_split[:, 2, :], max_rest[:, 1, :]).then_inc(max_split_ready, 1)

            def divide(k):
                g, c, kb = E_STEPS[ends[k]]
                pool.wait_ge(inv_ready, k + 1)
                rows = out_rows[:].rearrange("p (r h d) -> p r h d", r=R, h=G)
                for r in range(R):
                    out = att[:, R * c + r, g * G * HD:(g + 1) * G * HD].rearrange("p (h d) -> p h d", h=G)
                    last = pool.tensor_tensor(out, rows[:, r, :, 0:HD], inv_sum[:, r, :].unsqueeze(2).to_broadcast([P, G, HD]),
                                              ALU.mult)
                last.then_inc(out_ready, 1)

            work = [(s + LEAD, 1, mask_step, s) for s in diagonals]
            work += [(ends[k] + MAX_LAG + 1, 0, split_max, k) for k in range(len(ends))]
            work += [(ends[k] + OUT_LAG + 2, 2, divide, k) for k in range(len(ends))]
            work += [(OF_GROUP * g + LEAD + 5, 3, gather_values, g + 1) for g in range(1, GROUPS1 - 1)]
            for turn, kind, step, which in sorted(work, key=lambda w: w[:2]):
                step(which)

        @block.tensor
        def _(pe):
            def row_scores(s, heads):
                if s >= STEPS:
                    return
                g, c, r, kc = M_STEPS[s]
                if heads.start == 0 and (s % OF_GROUP == 0 if g > 0 else (c, r, kc) == (Stacks.AHEAD, 0, 0)):
                    pe.wait_ge(stacks_loaded[g % 2], stacks.LOADS * (g // 2 + 1))
                width = CHUNK if kc < c else (r + 1) * P
                for h in heads:
                    reach(pe, rows_reduced, G * s + h - 1)
                    pe.matmul(rows_ps[:, h % 2, 0:width], q_stack[0:MAX_ROW, g % 2, c, h, r * P:(r + 1) * P],
                              k_stack[0:MAX_ROW, g % 2, h, kc * CHUNK:kc * CHUNK + width], start=True, stop=True).then_inc(rows_scored, 1)

            def key_scores(s, hp):
                if not 0 <= s < STEPS:
                    return
                g, c, kb = E_STEPS[s]
                if s == 0 and hp == 0:
                    pe.wait_ge(ones_rows, 1)
                if kb == 0 and hp == 0:
                    pe.wait_ge(max_loaded, 16 * PARTS * (CHUNKS * g + c + 1))
                reach(pe, exped, 2 * (s - 1) + hp + 1)
                for a in range(2):
                    h = 2 * hp + a
                    last = pe.matmul(keyed_ps[:, hp, a, off_of(s):CHUNK], k_stack[0:STACK, g % 2, h, kb * P:(kb + 1) * P],
                                     q_stack[0:STACK, g % 2, c, h, off_of(s):CHUNK], start=True, stop=True)
                last.then_inc(keyed_scored, 1)

            def weigh(s):
                if not 0 <= s < STEPS:
                    return
                g, c, kb = E_STEPS[s]
                pe.wait_ge(exped, 2 * s + 2)
                if s in diagonals:
                    pe.wait_ge(triangled, 2 * diagonals.index(s) + 2)
                if kb == 0:
                    reach(pe, out_copied, CHUNKS * g + c)
                    pe.wait_ge(v_ones_ready, g + 1)
                for h in range(G):
                    last = pe.matmul(out_ps[2 * HD * h:2 * HD * (h + 1), off_of(s):CHUNK], v_ones[:, g % 2, kb, h, :],
                                     probs[:, s % 2, h // 2, h % 2, off_of(s):CHUNK], start=(kb == 0), stop=(kb == R * (c + 1) - 1),
                                     tile_position=(0, 2 * HD * h))
                last.then_inc(weighted, 1)

            def turn_max(k):
                pe.wait_ge(neg_max_ready, k + 1)
                pe.transpose(misc_ps[0:G * R, 0:P], neg_max[:], core.ident[:]).then_inc(max_turned, 1)

            def turn_out(k):
                pe.wait_ge(out_copied, k + 1)
                for r in range(R):
                    last = pe.transpose(misc_ps[:, r * P:(r + 1) * P], out_t[:, r * P:(r + 1) * P], core.ident[:])
                last.then_inc(out_turned, 1)

            for t in range(TURNS):
                e = t - LEAD
                key_scores(e, 0)
                row_scores(t, range(0, 1))
                key_scores(e, 1)
                row_scores(t, range(1, 3))
                weigh(e - 1)
                row_scores(t, range(3, 4))
                for what, k in misc_uses[t]:
                    reach(pe, misc_read, use_of[what, k])
                    turn_max(k) if what == "max" else turn_out(k)

        @block.scalar
        def _(act):
            for s in range(STEPS + 5):
                if s < STEPS:
                    off = off_of(s)
                    for hp in range(2):
                        act.wait_ge(keyed_scored, 2 * s + hp + 1)
                        if hp == 0:
                            reach(act, weighted, s - 1)
                        act.activation(probs[:, s % 2, hp, :, off:CHUNK], keyed_ps[:, hp, :, off:CHUNK],
                                       ACT.Exp).then_inc(exped, 1)
                if s - 1 in ends:
                    k = ends.index(s - 1)
                    act.wait_ge(weighted, s)
                    reach(act, out_turned, k)
                    act.activation(out_t[:], out_ps[:], ACT.Copy).then_inc(out_copied, 1)
                if s - 4 in ends:
                    k = ends.index(s - 4)
                    act.wait_ge(out_turned, k + 1)
                    reach(act, out_ready, k)
                    act.activation(out_rows[:], misc_ps[:], ACT.Copy).then_inc(misc_read, 1)

        @block.vector
        def _(dve):
            dve.wait_ge(prepared, 3)

            def reduce_rows(s):
                g, c, r, kc = M_STEPS[s]
                for h in range(G):
                    dve.wait_ge(rows_scored, G * s + h + 1)
                    ps, to = rows_ps[:, h % 2, :], maxima[:, c, h * R + r, :]
                    if kc < c:
                        last = dve.reduce_max(to[:, kc + 1:kc + 2], ps, AX_X)
                    else:
                        if r > 0:
                            dve.reduce_max(to[:, kc + 1:kc + 2], ps[:, 0:r * P], AX_X)
                        last = dve.tensor_tensor_reduce(masked[:, h % 2, :], ps[:, r * P:(r + 1) * P], causal[:], 1.0, NEG,
                                                        ALU.add, ALU.max, to[:, 0:1])
                    last.then_inc(rows_reduced, 1)

            def finish_max(s):
                k, c = ends.index(s), M_STEPS[s][1]
                dve.wait_ge(rows_reduced, G * (s + 1))
                dve.reduce_max(row_max[:], maxima[:, c, :, 0:c + 2], AX_X).then_inc(max_ready, 1)
                dve.wait_ge(max_ready, k + 1)
                dve.tensor_scalar(neg_max[:], row_max[:], -1.0, None, ALU.mult).then_inc(neg_max_ready, 1)

            def copy_max(k):
                dve.wait_ge(max_turned, k + 1)
                reach(dve, max_split_ready, k)
                dve.tensor_copy(max_rows[:], misc_ps[0:G * R, 0:P]).then_inc(misc_read, 1)

            def invert_sums(k):
                dve.wait_ge(misc_read, use_of["out", k] + 1)
                dve.reciprocal(inv_sum[:], out_rows[:].rearrange("p (r h d) -> p r h d", r=R, h=G)[:, :, :, HD]).then_inc(inv_ready, 1)

            for t in range(TURNS + 2):
                if t < STEPS:
                    reduce_rows(t)
                    if t in ends:
                        finish_max(t)
                if t - 1 - MAX_LAG in ends:
                    copy_max(ends.index(t - 1 - MAX_LAG))
                if t - 2 - OUT_LAG in ends:
                    invert_sums(ends.index(t - 2 - OUT_LAG))


def phase_attention_out(nc, core, att, ahead, b_out, ffn_weights):
    with ExitStack() as ctx:
        m = Mem(nc, ctx, "out")
        raw, = ahead.tiles
        w_hi, w_lo = m.sb("w_hi", [P, KD, D], F32R), m.sb("w_lo", [P, KD, D], F32R)
        bias = m.sb("bias", [P, D])
        att_hi, att_lo = m.sb("att_hi", [P, KD, CHUNK], F32R), m.sb("att_lo", [P, KD, CHUNK], F32R)
        y, y_normed = m.sb("y", [P, R, D]), m.sb("y_normed", [P, R, D])
        post, pre, turn = Stats(m, "post"), Stats(m, "pre"), Turn(m, core)
        ffn_weights.prepare_in(m, first_chunk=1)
        att_ps, y_ps = m.ps("att_ps", [P, KD, CHUNK]), m.ps("y_ps", [P, R // 2, 2 * D])
        b_loaded = m.sem("b_loaded")
        w_turned, w_hi_ready, w_lo_ready = m.sem("w_turned"), m.sem("w_hi_ready"), m.sem("w_lo_ready")
        att_turned, att_hi_ready, att_lo_ready = m.sem("att_turned"), m.sem("att_hi_ready"), m.sem("att_lo_ready")
        projected, y_ready, y_read, x_updated = (m.sem(s) for s in ("projected", "y_ready", "y_read", "x_updated"))
        block = m.start()

        @block.sync
        def _(sp):
            sp.dma_start(bias[:], b_out.rearrange("(a n) -> a n", a=1).to_broadcast([P, D])).then_inc(b_loaded, 16)
            for w in range(3):
                ffn_weights.load(sp, w)

        @block.gpsimd
        def _(pool):
            ffn_weights.pool_scale(pool)

        @block.tensor
        def _(pe):
            def turn_att(c):
                if c >= CHUNKS:
                    return
                pe.wait_ge(att_lo_ready, KD * c) if c else pe.wait_ge(w_lo_ready, 1)
                for k in range(KD):
                    for r in range(R):
                        last = pe.transpose(att_ps[:, k, r * P:(r + 1) * P], att[:, c * R + r, k * P:(k + 1) * P], core.ident[:])
                    last.then_inc(att_turned, 1)

            def project(c):
                if c >= CHUNKS:
                    return
                pe.wait_ge(att_lo_ready, KD * (c + 1))
                reach(pe, y_ready, c)
                for r in range(R):
                    at = slice(r * P, (r + 1) * P)
                    for k in range(KD):
                        for i, (a, w) in enumerate(((att_hi, w_hi), (att_hi, w_lo), (att_lo, w_hi))):
                            last = pe.matmul(y_ps[:, r // 2, (r % 2) * D:(r % 2 + 1) * D], a[:, k, at], w[:, k, :],
                                             start=(k == 0 and i == 0), stop=(k == KD - 1 and i == 2))
                last.then_inc(projected, 1)

            for k in range(KD):
                for j in range(KD):
                    last = pe.transpose(att_ps[:, 0, k * D + j * P:k * D + (j + 1) * P], raw[:, j, k * P:(k + 1) * P], core.ident[:])
            last.then_inc(w_turned, 1)
            turn_att(0)
            project(0)
            for c in range(CHUNKS):
                turn_att(c + 1)
                project(c + 1)
                ffn_weights.pe(pe, c, 0)
                ffn_weights.pe(pe, c, 1)
                turn.pe_turn(pe, c)

        @block.scalar
        def _(act):
            def split_att(c):
                if c >= CHUNKS:
                    return
                reach(act, projected, c)
                for k in range(KD):
                    act.wait_ge(att_turned, KD * c + k + 1)
                    act.activation(att_hi[:, k, :], att_ps[:, k, :], ACT.Copy).then_inc(att_hi_ready, 1)

            act.wait_ge(w_turned, 1)
            act.activation(w_hi[:].rearrange("p k d -> p (k d)"), att_ps[:, 0, :], ACT.Copy).then_inc(w_hi_ready, 1)
            split_att(0)
            post.act_std(act, 0)
            for c in range(CHUNKS):
                split_att(c + 1)
                pre.act_std(act, c)
                if c + 1 < CHUNKS:
                    post.act_std(act, c + 1)
                ffn_weights.act(act, c, 0)
                ffn_weights.act(act, c, 1)
                turn.act_hi(act, c, c)

        @block.vector
        def _(dve):
            def split_att(c):
                if c >= CHUNKS:
                    return
                for k in range(KD):
                    dve.wait_ge(att_hi_ready, KD * c + k + 1)
                    dve.tensor_tensor(att_lo[:, k, :], att_ps[:, k, :], att_hi[:, k, :].bitcast(F32),
                                      ALU.subtract).then_inc(att_lo_ready, 1)

            dve.wait_ge(w_hi_ready, 1)
            dve.tensor_tensor(w_lo[:].rearrange("p k d -> p (k d)"), att_ps[:, 0, :],
                              w_hi[:].rearrange("p k d -> p (k d)").bitcast(F32), ALU.subtract).then_inc(w_lo_ready, 1)
            dve.wait_ge(b_loaded, 16)
            y_tile = lambda r: y[:, r, :]

            def begin(c):
                if c >= CHUNKS:
                    return
                dve.wait_ge(projected, c + 1)
                for r in range(R):
                    last = dve.tensor_tensor(y[:, r, :], y_ps[:, r // 2, (r % 2) * D:(r % 2 + 1) * D], bias[:], ALU.add)
                last.then_inc(y_ready, 1)
                dve.wait_ge(y_ready, c + 1)
                post.dve_variance(dve, y_tile, c)

            split_att(0)
            begin(0)
            for c in range(CHUNKS):
                split_att(c + 1)
                post.dve_rstd(dve, c)
                post.dve_normalise(dve, lambda r: y_normed[:, r, :], y_tile).then_inc(y_read, 1)
                dve.wait_ge(y_read, c + 1)
                dve.tensor_tensor(core.x_chunk(c), core.x_chunk(c), y_normed[:].rearrange("p a d -> p (a d)"),
                                  ALU.add).then_inc(x_updated, 1)
                dve.wait_ge(x_updated, c + 1)
                pre.dve_variance(dve, core.x_tile(c), c)
                if c > 0:
                    turn.dve_lo(dve, c - 1, c - 1)
                begin(c + 1)
                ffn_weights.dve(dve, c, 0)
                pre.dve_rstd(dve, c)
                reach(dve, turn.turned_ready, KD * c)
                pre.dve_normalise(dve, lambda r: turn.xn[:, r, :], core.x_tile(c)).then_inc(turn.xn_ready, 1)
                ffn_weights.dve(dve, c, 1)
            turn.dve_lo(dve, CHUNKS - 1, CHUNKS - 1)



def build(nc, x, w_q, w_k, w_v, w_o, betas, w_gate0, w_up0, w_down0, w_qkv, b_qkv, w_out, b_out,
          w_gate1, gate_scale, w_up1, up_scale, w_down1, down_scale, out):
    q_parts = nc.dram_tensor("q_parts", [PARTS, HD, CHUNKS, H1, CHUNK], BF16, kind="Internal").ap()
    k_parts = nc.dram_tensor("k_parts", [PARTS, D, T], BF16, kind="Internal").ap()
    memory_att = nc.dram_tensor("memory_att", [T, D], F32, kind="Internal").ap()
    sigmoids = nc.dram_tensor("sigmoids", [HEADS, 2, DH], F32, kind="Internal").ap()
    with ExitStack() as ctx:
        core = Core(nc, ctx)
        with ExitStack() as layer:
            first = [(n, [P, KD, G * DH], w[:, 0:G * DH].rearrange("(k p) n -> p k n", p=P)) for n, w in (("k", w_k), ("q", w_q), ("v", w_v))]
            weights = Ahead(nc, layer, "raw", first)
            phase_input(nc, core, x, weights)
            phase_memory_attention(nc, core, memory_att, sigmoids, weights, w_q, w_k, w_v, w_o, betas)
        core.hold_x(nc, ctx)
        qkv_weights = Ahead(nc, ctx, "qkv_raw", [("w", [P, 3 * KD, D], w_qkv.rearrange("(j p) n -> p j n", p=P))])
        with ExitStack() as layer:
            weights = FfnWeights(nc, layer, core, "ffn0_weights", w_gate0, w_up0, w_down0)
            phase_residual(nc, core, x, memory_att, weights, "res0")
            phase_ffn(nc, core, "ffn0", weights, ahead=qkv_weights)
        with ExitStack() as layer:
            mixed = layer.enter_context(nc.sbuf_tensor("mixed", [P, TILES, D], F32))
            out_weights = Ahead(nc, layer, "out_raw", [("w", [P, KD, D], w_out.rearrange("(j p) n -> p j n", p=P))])
            with ExitStack() as attention:
                values = attention.enter_context(nc.sbuf_tensor("values", [P, TILES, D], F32))
                stacks = Stacks(nc, attention, q_parts, k_parts)
                phase_qkv(nc, core, values, qkv_weights, b_qkv, q_parts, k_parts, stacks)
                phase_attention(nc, core, mixed, values, stacks, out_weights)
            weights = FfnWeights(nc, layer, core, "ffn1_weights", w_gate1, w_up1, w_down1, (gate_scale, up_scale, down_scale))
            phase_attention_out(nc, core, mixed, out_weights, b_out, weights)
            phase_ffn(nc, core, "ffn1", weights, out=out)


_INS = ["L0_attn_x", "L0_attn_Wq", "L0_attn_Wk", "L0_attn_Wv", "L0_attn_Wo", "L0_attn_betas",
        "L0_ffn_w_gate", "L0_ffn_w_up", "L0_ffn_w_down",
        "L1_attn_w_qkv", "L1_attn_b_qkv", "L1_attn_w_out", "L1_attn_b_out",
        "L1_ffn_gate_w", "L1_ffn_gate_scale", "L1_ffn_up_w", "L1_ffn_up_scale", "L1_ffn_down_w", "L1_ffn_down_scale"]


def kernel(**inputs):
    import numpy as np
    import concourse.bacc as bacc
    from concourse.bass_utils import run_bass_kernel_spmd

    nc = bacc.Bacc("TRN2", target_bir_lowering=False, num_devices=1)
    nc.disable_value_cache = True
    arrays, args = {}, []
    for name in _INS:
        a = np.ascontiguousarray(inputs[name])
        arrays[name] = a
        args.append(nc.dram_tensor(name, a.shape, mybir.dt.from_np(a.dtype), kind="ExternalInput").ap())
    out = nc.dram_tensor("out", (1, T, D), F32, kind="ExternalOutput").ap()
    build(nc, *args, out)
    r = run_bass_kernel_spmd(nc, [arrays], core_ids=[0])
    return r.results[0]["out"]
```
